# Optimizing a Trainium2 kernel written in Bass

```python
import numpy as np
import jax
import jax.numpy as jnp

def _softmax(x, axis=-1):
    return jax.nn.softmax(x, axis=axis)

def _gelu(x):
    return jax.nn.gelu(x, approximate=True)

def _silu(x):
    return jax.nn.silu(x)

def _sigmoid(x):
    return jax.nn.sigmoid(x)

def _layernorm(x, axis=-1, eps=1e-05):
    m = jnp.mean(x, axis=axis, keepdims=True)
    v = jnp.var(x, axis=axis, keepdims=True)
    return (x - m) / jnp.sqrt(v + eps)

def _scatter_add(tgt, idx, src, axis=0):
    return tgt.at[idx].add(src)

def _segment_sum(src, seg, n):
    return jax.ops.segment_sum(src, seg, n)
kernel_name = 'mk_gnn_preln_d4_gnn_r16_606a63'

def setup_inputs(seed: int=0):
    np.random.seed(seed)
    _w = jnp.asarray

    def _rec_inputs():
        import jax
        import jax.numpy as jnp
        _gk = jax.random.key(seed)
        x = -0.0002928 + 1 * jax.random.normal(jax.random.fold_in(_gk, 1), (3125, 64), jnp.float32)
        src = jax.random.randint(jax.random.fold_in(_gk, 2), (100000,), 0, 3125, jnp.int32)
        dst = jax.random.randint(jax.random.fold_in(_gk, 3), (100000,), 0, 3125, jnp.int32)
        _o = jnp.argsort(dst, stable=True)
        src = src[_o]
        dst = dst[_o]
        edge_type_8 = jax.random.randint(jax.random.fold_in(_gk, 13), (100000,), 0, 8, jnp.int32)
        edge_weight = jax.random.uniform(jax.random.fold_in(_gk, 14), (100000,), jnp.float32, 0.0, 0.999999)
        edge_weight_n2 = jax.random.uniform(jax.random.fold_in(_gk, 15), (100000,), jnp.float32, 0.0, 0.999999)
        return (x, src, dst, edge_type_8, edge_weight, edge_weight_n2)
    x, src, dst, edge_type_8, edge_weight, edge_weight_n2 = _rec_inputs()

    def _L0_gnn_setup():
        import jax, jax.numpy as jnp
        import numpy as np
        N, E, D_IN, D_OUT = (4096, 65536, 64, 64)
        EPS = 1e-08
        key = jax.random.key(seed)
        ks = jax.random.split(key, 8)
        h = jax.random.normal(ks[0], (N, D_IN), dtype=jnp.float32)
        edge_index = jax.random.randint(ks[1], (2, E), 0, N, dtype=jnp.int64 if jax.config.jax_enable_x64 else jnp.int32)
        adj_v = jax.random.uniform(ks[2], (E,), dtype=jnp.float32)
        deg_v = jax.random.uniform(ks[3], (E,), dtype=jnp.float32)
        W = jax.random.normal(ks[4], (D_IN, D_OUT), dtype=jnp.float32) / np.sqrt(D_IN)
        b = jax.random.normal(ks[5], (D_OUT,), dtype=jnp.float32) * 0.01
        deg_coeff = jnp.array([0.5, 0.0], dtype=jnp.float32)
        coeff_param = jnp.zeros((3,), dtype=jnp.float32)
        scale_param = 2.0 * jnp.ones((1,), dtype=jnp.float32)
        return {'h': h, 'edge_index': edge_index, 'adj_v': adj_v, 'deg_v': deg_v, 'W': W, 'b': b, 'deg_coeff': deg_coeff, 'coeff_param': coeff_param, 'scale_param': scale_param}
    _L0_gnn_all = _L0_gnn_setup()
    _L0_gnn_in = {k: v for k, v in _L0_gnn_all.items() if k in ('W', 'b', 'deg_coeff', 'coeff_param', 'scale_param')}
    del _L0_gnn_all

    def _L1_gnn_setup():
        import jax, jax.numpy as jnp
        import numpy as np
        NEG_SLOPE = 0.2

        def _gat_relation(x, src, dst, mask, N, Wr, a_src, a_dst, br):
            h = x @ Wr
            s = h @ a_src
            d = h @ a_dst
            e = jax.nn.leaky_relu(s[src] + d[dst], negative_slope=NEG_SLOPE)
            e = jnp.where(mask, e, -jnp.inf)
            m = jax.ops.segment_max(e, dst, num_segments=N)
            w = jnp.where(mask, jnp.exp(e - m[dst]), 0.0)
            denom = jax.ops.segment_sum(w, dst, num_segments=N)
            alpha = w / denom[dst]
            msg = alpha[:, None] * h[src]
            return jax.ops.segment_sum(msg, dst, num_segments=N) + br
        key = jax.random.key(seed)
        ks = jax.random.split(key, 9)
        N, E, D, F, R = (6250, 100000, 64, 64, 8)
        x = jax.random.normal(ks[0], (N, D), dtype=jnp.float32)
        edge_index = jax.random.randint(ks[1], (2, E), 0, N, dtype=jnp.int32)
        edge_type = jax.random.randint(ks[2], (E,), 0, R, dtype=jnp.int32)
        W_self = jax.random.normal(ks[3], (D, F), dtype=jnp.float32) * 0.1
        b_self = jax.random.normal(ks[4], (F,), dtype=jnp.float32) * 0.1
        W = jax.random.normal(ks[5], (R, D, F), dtype=jnp.float32) * 0.1
        att_src = jax.random.normal(ks[6], (R, F), dtype=jnp.float32) * 0.1
        att_dst = jax.random.normal(ks[7], (R, F), dtype=jnp.float32) * 0.1
        bias = jax.random.normal(ks[8], (R, F), dtype=jnp.float32) * 0.1
        return {'x': x, 'edge_index': edge_index, 'edge_type': edge_type, 'W_self': W_self, 'b_self': b_self, 'W': W, 'att_src': att_src, 'att_dst': att_dst, 'bias': bias}
    _L1_gnn_all = _L1_gnn_setup()
    _L1_gnn_in = {k: v for k, v in _L1_gnn_all.items() if k in ('W_self', 'b_self', 'W', 'att_src', 'att_dst', 'bias')}
    del _L1_gnn_all

    def _L2_gnn_setup():
        import jax, jax.numpy as jnp
        import numpy as np
        N_NODES = 6250
        N_EDGES = 62500
        D = 64
        H = 128
        key = jax.random.key(seed)
        ks = jax.random.split(key, 12)
        x = jax.random.normal(ks[0], (N_NODES, D), dtype=jnp.float32)
        start = jax.random.randint(ks[1], (N_EDGES,), 0, N_NODES)
        end = jax.random.randint(ks[2], (N_EDGES,), 0, N_NODES)

        def w(k, fan_in, shape):
            return jax.random.normal(k, shape, dtype=jnp.float32) / jnp.sqrt(jnp.float32(fan_in))
        We1 = w(ks[3], 2 * D, (2 * D, H))
        be1 = jnp.zeros((H,), jnp.float32)
        We2 = w(ks[4], H, (H, 1))
        be2 = jnp.zeros((1,), jnp.float32)
        Wn1 = w(ks[5], 3 * D, (3 * D, H))
        bn1 = jnp.zeros((H,), jnp.float32)
        Wn2 = w(ks[6], H, (H, D))
        bn2 = jnp.zeros((D,), jnp.float32)
        return {'x': x, 'start': start, 'end': end, 'We1': We1, 'be1': be1, 'We2': We2, 'be2': be2, 'Wn1': Wn1, 'bn1': bn1, 'Wn2': Wn2, 'bn2': bn2}
    _L2_gnn_all = _L2_gnn_setup()
    _L2_gnn_in = {k: v for k, v in _L2_gnn_all.items() if k in ('We1', 'be1', 'We2', 'be2', 'Wn1', 'bn1', 'Wn2', 'bn2')}
    del _L2_gnn_all

    def _L3_gnn_setup():
        import jax, jax.numpy as jnp
        import numpy as np
        N_NODES = 1250
        N_EDGES = 20000
        HIDDEN = 64
        HEADS = 4
        D_INNER = 256
        NEG_SLOPE = 0.2
        BN_EPS = 1e-05

        def _batch_norm(x, gamma, beta):
            mu = x.mean(0)
            var = jnp.mean((x - mu) ** 2, axis=0)
            return (x - mu) * jax.lax.rsqrt(var + BN_EPS) * gamma + beta

        def _gatv2(x, edge_index, W_l, b_l, W_r, b_r, att, bias_gat):
            N = x.shape[0]
            H, C = att.shape
            src, dst = (edge_index[0], edge_index[1])
            xl = (x @ W_l + b_l).reshape(N, H, C)
            xr = (x @ W_r + b_r).reshape(N, H, C)
            e = jax.nn.leaky_relu(xl[src] + xr[dst], NEG_SLOPE)
            score = jnp.einsum('ehc,hc->eh', e, att)
            m = jax.ops.segment_max(score, dst, num_segments=N)
            ex = jnp.exp(score - m[dst])
            denom = jax.ops.segment_sum(ex, dst, num_segments=N)
            alpha = ex / jnp.maximum(denom[dst], 1e-16)
            out = jax.ops.segment_sum(alpha[:, :, None] * xl[src], dst, num_segments=N)
            return out.mean(axis=1) + bias_gat
        key = jax.random.key(seed)
        ks = jax.random.split(key, 8)
        s = 1.0 / np.sqrt(HIDDEN)
        return {'x': jax.random.normal(ks[0], (N_NODES, HIDDEN), jnp.float32), 'edge_index': jax.random.randint(ks[1], (2, N_EDGES), 0, N_NODES, jnp.int64), 'W_l': jax.random.normal(ks[2], (HIDDEN, HEADS * HIDDEN), jnp.float32) * s, 'b_l': jnp.zeros((HEADS * HIDDEN,), jnp.float32), 'W_r': jax.random.normal(ks[3], (HIDDEN, HEADS * HIDDEN), jnp.float32) * s, 'b_r': jnp.zeros((HEADS * HIDDEN,), jnp.float32), 'att': jax.random.normal(ks[4], (HEADS, HIDDEN), jnp.float32) * s, 'bias_gat': jnp.zeros((HIDDEN,), jnp.float32), 'gamma1': jnp.ones((HIDDEN,), jnp.float32), 'beta1': jnp.zeros((HIDDEN,), jnp.float32), 'W1': jax.random.normal(ks[5], (HIDDEN, D_INNER), jnp.float32) * s, 'b1': jnp.zeros((D_INNER,), jnp.float32), 'W2': jax.random.normal(ks[6], (D_INNER, HIDDEN), jnp.float32) / np.sqrt(D_INNER), 'b2': jnp.zeros((HIDDEN,), jnp.float32), 'gamma2': jnp.ones((HIDDEN,), jnp.float32), 'beta2': jnp.zeros((HIDDEN,), jnp.float32)}
    _L3_gnn_all = _L3_gnn_setup()
    _L3_gnn_in = {k: v for k, v in _L3_gnn_all.items() if k in ('W_l', 'b_l', 'W_r', 'b_r', 'att', 'bias_gat', 'gamma1', 'beta1', 'W1', 'b1', 'W2', 'b2', 'gamma2', 'beta2')}
    del _L3_gnn_all
    return {'x': x, 'src': src, 'dst': dst, 'edge_type_8': edge_type_8, 'edge_weight': edge_weight, 'edge_weight_n2': edge_weight_n2, 'L0_gnn_W': _L0_gnn_in['W'], 'L0_gnn_b': _L0_gnn_in['b'], 'L0_gnn_deg_coeff': _L0_gnn_in['deg_coeff'], 'L0_gnn_coeff_param': _L0_gnn_in['coeff_param'], 'L0_gnn_scale_param': _L0_gnn_in['scale_param'], 'L1_gnn_W_self': _L1_gnn_in['W_self'], 'L1_gnn_b_self': _L1_gnn_in['b_self'], 'L1_gnn_W': _L1_gnn_in['W'], 'L1_gnn_att_src': _L1_gnn_in['att_src'], 'L1_gnn_att_dst': _L1_gnn_in['att_dst'], 'L1_gnn_bias': _L1_gnn_in['bias'], 'L2_gnn_We1': _L2_gnn_in['We1'], 'L2_gnn_be1': _L2_gnn_in['be1'], 'L2_gnn_We2': _L2_gnn_in['We2'], 'L2_gnn_be2': _L2_gnn_in['be2'], 'L2_gnn_Wn1': _L2_gnn_in['Wn1'], 'L2_gnn_bn1': _L2_gnn_in['bn1'], 'L2_gnn_Wn2': _L2_gnn_in['Wn2'], 'L2_gnn_bn2': _L2_gnn_in['bn2'], 'L3_gnn_W_l': _L3_gnn_in['W_l'], 'L3_gnn_b_l': _L3_gnn_in['b_l'], 'L3_gnn_W_r': _L3_gnn_in['W_r'], 'L3_gnn_b_r': _L3_gnn_in['b_r'], 'L3_gnn_att': _L3_gnn_in['att'], 'L3_gnn_bias_gat': _L3_gnn_in['bias_gat'], 'L3_gnn_gamma1': _L3_gnn_in['gamma1'], 'L3_gnn_beta1': _L3_gnn_in['beta1'], 'L3_gnn_W1': _L3_gnn_in['W1'], 'L3_gnn_b1': _L3_gnn_in['b1'], 'L3_gnn_W2': _L3_gnn_in['W2'], 'L3_gnn_b2': _L3_gnn_in['b2'], 'L3_gnn_gamma2': _L3_gnn_in['gamma2'], 'L3_gnn_beta2': _L3_gnn_in['beta2']}

def reference(x, src, dst, edge_type_8, edge_weight, edge_weight_n2, L0_gnn_W, L0_gnn_b, L0_gnn_deg_coeff, L0_gnn_coeff_param, L0_gnn_scale_param, L1_gnn_W_self, L1_gnn_b_self, L1_gnn_W, L1_gnn_att_src, L1_gnn_att_dst, L1_gnn_bias, L2_gnn_We1, L2_gnn_be1, L2_gnn_We2, L2_gnn_be2, L2_gnn_Wn1, L2_gnn_bn1, L2_gnn_Wn2, L2_gnn_bn2, L3_gnn_W_l, L3_gnn_b_l, L3_gnn_W_r, L3_gnn_b_r, L3_gnn_att, L3_gnn_bias_gat, L3_gnn_gamma1, L3_gnn_beta1, L3_gnn_W1, L3_gnn_b1, L3_gnn_W2, L3_gnn_b2, L3_gnn_gamma2, L3_gnn_beta2):
    import jax
    import jax.numpy as jnp

    def _L0_gnn_ref(h, edge_index, adj_v, deg_v, W, b, deg_coeff, coeff_param, scale_param):
        import jax, jax.numpy as jnp
        import numpy as np
        N, E, D_IN, D_OUT = (4096, 65536, 64, 64)
        EPS = 1e-08
        n_nodes = h.shape[0]
        Wh = h @ W + b
        row, col = (edge_index[0], edge_index[1])
        sc = jax.nn.softplus(deg_coeff[0] * deg_v + deg_coeff[1])
        Wr = Wh[row]
        Wc = Wh[col]
        dot = jnp.sum(Wr * Wc, axis=-1)
        nr = jnp.sqrt(jnp.sum(Wr * Wr, axis=-1))
        nc = jnp.sqrt(jnp.sum(Wc * Wc, axis=-1))
        sim = dot / jnp.maximum(nr * nc, EPS)
        sim_pos = jax.nn.relu(sim)
        sim_neg = -jax.nn.relu(-sim)
        no_diag = (row != col).astype(Wh.dtype)
        base = adj_v * sc * no_diag
        prop_pos = jax.ops.segment_sum((base * sim_pos)[:, None] * Wc, row, num_segments=n_nodes)
        prop_neg = jax.ops.segment_sum((base * sim_neg)[:, None] * Wc, row, num_segments=n_nodes)
        coeff = jax.nn.softmax(coeff_param)
        scale = jax.nn.softplus(scale_param)
        return scale * (coeff[0] * prop_pos + coeff[1] * prop_neg + coeff[2] * Wh)

    def _L1_gnn_ref(x, edge_index, edge_type, W_self, b_self, W, att_src, att_dst, bias):
        import jax, jax.numpy as jnp
        import numpy as np
        NEG_SLOPE = 0.2

        def _gat_relation(x, src, dst, mask, N, Wr, a_src, a_dst, br):
            h = x @ Wr
            s = h @ a_src
            d = h @ a_dst
            e = jax.nn.leaky_relu(s[src] + d[dst], negative_slope=NEG_SLOPE)
            e = jnp.where(mask, e, -jnp.inf)
            m = jax.ops.segment_max(e, dst, num_segments=N)
            w = jnp.where(mask, jnp.exp(e - m[dst]), 0.0)
            denom = jax.ops.segment_sum(w, dst, num_segments=N)
            alpha = w / denom[dst]
            msg = alpha[:, None] * h[src]
            return jax.ops.segment_sum(msg, dst, num_segments=N) + br
        N = x.shape[0]
        R = W.shape[0]
        loops = jnp.arange(N, dtype=edge_index.dtype)
        src = jnp.concatenate([edge_index[0], loops])
        dst = jnp.concatenate([edge_index[1], loops])
        ones_loops = jnp.ones((N,), dtype=bool)
        out = x @ W_self + b_self
        for r in range(R):
            mask = jnp.concatenate([edge_type == r, ones_loops])
            out = out + _gat_relation(x, src, dst, mask, N, W[r], att_src[r], att_dst[r], bias[r])
        return out

    def _L2_gnn_ref(x, start, end, We1, be1, We2, be2, Wn1, bn1, Wn2, bn2):
        import jax, jax.numpy as jnp
        import numpy as np
        N_NODES = 6250
        N_EDGES = 62500
        D = 64
        H = 128
        n = x.shape[0]
        xs = x[start]
        edge_inputs = jnp.concatenate([xs, x[end]], axis=1)
        h = jax.nn.relu(edge_inputs @ We1 + be1)
        e = jax.nn.sigmoid(h @ We2 + be2)
        m = e * xs
        m_sum = jax.ops.segment_sum(m, end, num_segments=n)
        m_max = jax.ops.segment_max(m, end, num_segments=n)
        m_max = jnp.where(jnp.isneginf(m_max), jnp.float32(0.0), m_max)
        messages = jnp.concatenate([m_max, m_sum], axis=-1)
        node_inputs = jnp.concatenate([messages, x], axis=1)
        h2 = jax.nn.relu(node_inputs @ Wn1 + bn1)
        x_out = h2 @ Wn2 + bn2 + x
        return x_out

    def _L3_gnn_ref(x, edge_index, W_l, b_l, W_r, b_r, att, bias_gat, gamma1, beta1, W1, b1, W2, b2, gamma2, beta2):
        import jax, jax.numpy as jnp
        import numpy as np
        N_NODES = 1250
        N_EDGES = 20000
        HIDDEN = 64
        HEADS = 4
        D_INNER = 256
        NEG_SLOPE = 0.2
        BN_EPS = 1e-05

        def _batch_norm(x, gamma, beta):
            mu = x.mean(0)
            var = jnp.mean((x - mu) ** 2, axis=0)
            return (x - mu) * jax.lax.rsqrt(var + BN_EPS) * gamma + beta

        def _gatv2(x, edge_index, W_l, b_l, W_r, b_r, att, bias_gat):
            N = x.shape[0]
            H, C = att.shape
            src, dst = (edge_index[0], edge_index[1])
            xl = (x @ W_l + b_l).reshape(N, H, C)
            xr = (x @ W_r + b_r).reshape(N, H, C)
            e = jax.nn.leaky_relu(xl[src] + xr[dst], NEG_SLOPE)
            score = jnp.einsum('ehc,hc->eh', e, att)
            m = jax.ops.segment_max(score, dst, num_segments=N)
            ex = jnp.exp(score - m[dst])
            denom = jax.ops.segment_sum(ex, dst, num_segments=N)
            alpha = ex / jnp.maximum(denom[dst], 1e-16)
            out = jax.ops.segment_sum(alpha[:, :, None] * xl[src], dst, num_segments=N)
            return out.mean(axis=1) + bias_gat
        x2 = _gatv2(x, edge_index, W_l, b_l, W_r, b_r, att, bias_gat)
        x = x + x2
        x = _batch_norm(x, gamma1, beta1)
        ff = jax.nn.relu(x @ W1 + b1) @ W2 + b2
        x = x + ff
        x = _batch_norm(x, gamma2, beta2)
        return x
    edge_index = jnp.stack([src, dst])
    h = jnp.maximum(_layernorm(x, axis=-1), 0.0)
    x = x + _L0_gnn_ref(h, edge_index, edge_weight, edge_weight_n2, L0_gnn_W, L0_gnn_b, L0_gnn_deg_coeff, L0_gnn_coeff_param, L0_gnn_scale_param)
    h = jnp.maximum(_layernorm(x, axis=-1), 0.0)
    x = x + _L1_gnn_ref(h, edge_index, edge_type_8, L1_gnn_W_self, L1_gnn_b_self, L1_gnn_W, L1_gnn_att_src, L1_gnn_att_dst, L1_gnn_bias)
    h = jnp.maximum(_layernorm(x, axis=-1), 0.0)
    x = x + _L2_gnn_ref(h, src, dst, L2_gnn_We1, L2_gnn_be1, L2_gnn_We2, L2_gnn_be2, L2_gnn_Wn1, L2_gnn_bn1, L2_gnn_Wn2, L2_gnn_bn2)
    h = jnp.maximum(_layernorm(x, axis=-1), 0.0)
    x = x + _L3_gnn_ref(h, edge_index, L3_gnn_W_l, L3_gnn_b_l, L3_gnn_W_r, L3_gnn_b_r, L3_gnn_att, L3_gnn_bias_gat, L3_gnn_gamma1, L3_gnn_beta1, L3_gnn_W1, L3_gnn_b1, L3_gnn_W2, L3_gnn_b2, L3_gnn_gamma2, L3_gnn_beta2)
    return x

_drawn_inputs = setup_inputs


def setup_inputs(seed=0):
    import zlib

    import numpy as np

    out = dict(_drawn_inputs(seed))
    spreads = {'L0_gnn_coeff_param': (0.0, 0.1),
     'L2_gnn_be1': (0.0, 0.1),
     'L2_gnn_bn1': (0.0, 0.502),
     'L2_gnn_bn2': (0.0, 0.335),
     'L3_gnn_b_l': (0.0, 2.0),
     'L3_gnn_b_r': (0.0, 2.0),
     'L3_gnn_bias_gat': (0.0, 2.0),
     'L3_gnn_gamma1': (1.0, 0.553),
     'L3_gnn_beta1': (0.0, 0.8),
     'L3_gnn_b1': (0.0, 0.8),
     'L3_gnn_b2': (0.0, 2.0),
     'L3_gnn_gamma2': (1.0, 0.2),
     'L3_gnn_beta2': (0.0, 0.441)}
    factors = {'edge_weight_n2': 3.376,
     'L1_gnn_att_dst': 25.772,
     'L3_gnn_W_r': 6.918,
     'L3_gnn_att': 2.785}
    for name, (base, spread) in spreads.items():
        noise = np.random.default_rng([zlib.crc32(name.encode()), seed]).standard_normal(out[name].shape)
        drawn = base * np.exp(spread * noise) if base else spread * noise
        out[name] = jnp.asarray(drawn.astype(out[name].dtype))
    for name, factor in factors.items():
        out[name] = (out[name] * factor).astype(out[name].dtype)
    return out
```

```python
from contextlib import ExitStack

import concourse.bass as bass
from concourse import mybir

ALU = mybir.AluOpType
ACT = mybir.ActivationFunctionType
AX = mybir.AxisListType
F32 = mybir.dt.float32
I32 = mybir.dt.int32
BF16 = mybir.dt.bfloat16

P = 128
N = 3125
NT = 25
NP = P * NT
NV = N // NT
E = 100000
K = 8
T = 784
EP = P * T
EL = E - (P - 1) * T
NG = T // K
LOOPS = NG // 2
D = 64
R = 8
H = 4
HD = H * D
HID = 128
FF = 256
NB = 5
NBATCH = NT // NB
BC = NB * P
BIG = 1.0e30
ROUND = 12582912.0
EPS = 1e-5
W0 = D + 1
W1 = D + 1
W2 = HID + D
W3 = HD + H
SLOPE = 0.2

M_SRC, M_NS, M_NEG, M_REL, M_SRCF, M_W = 0, K, 2 * K, 3 * K, 4 * K, 5 * K


class Tally:

    def __init__(self, engine):
        self.engine, self.count = engine, {}

    def done(self, instruction, semaphore):
        self.count[semaphore.name] = self.count.get(semaphore.name, 0) + 1
        instruction.then_inc(semaphore, 1)
        self.engine.wait_ge(semaphore, self.count[semaphore.name])


class Beats:

    def __init__(self, engine, semaphore, each):
        self.engine, self.semaphore, self.each, self.g, self.k = engine, semaphore, each, 0, each

    def group(self, g):
        assert self.k == self.each, (self.semaphore.name, self.k)
        self.g, self.k = g, 0

    def add(self, instruction):
        instruction.then_inc(self.semaphore, 1)
        self.k += 1

    def wait(self, back=0):
        value = self.g * self.each + (self.k - back)
        if not isinstance(value, int) or value > 0:
            self.engine.wait_ge(self.semaphore, value)

    def done(self, instruction):
        self.add(instruction)
        self.wait()


def passes(engine, body):
    for h in range(2):
        body(0, h, True)
    with engine.Fori(1, LOOPS) as i:
        for h in range(2):
            body(i, h, False)


def gnn_program(nc, x, src, dst, etype, adj_v, deg_v, w0, b0, deg_coeff, coeff_param, scale_param,
                w_self, b_self, w_rel, a_src, a_dst, bias_rel, we1, be1, we2, be2, wn1, bn1, wn2, bn2,
                w_l, b_l, w_r, b_r, att, bias_gat, gamma1, beta1, w_f1, b_f1, w_f2, b_f2, gamma2, beta2,
                out):
    with ExitStack() as ctx:
        def sb(name, shape, dt=F32):
            return ctx.enter_context(nc.sbuf_tensor(name, shape, dt))

        def sem(name):
            return ctx.enter_context(nc.semaphore(name))

        def dram(name, shape):
            return nc.dram_tensor(name, shape, F32).ap()

        tab0, tab1 = dram("tab0", [NP, W0]), dram("tab1", [NP * R, W1])
        tab2, tab3 = dram("tab2", [NP, W2]), dram("tab3", [NP, W3])
        put0, put1 = dram("put0", [EP + NP, W0]), dram("put1", [EP + NP, 2 * R])
        put2, put3 = dram("put2", [EP + NP, HID]), dram("put3", [EP + NP, W3])
        rows1, rows2, rows3 = dram("rows1", [NP, 2 * R]), dram("rows2", [NP, HID]), dram("rows3", [NP, W3])
        acc = [dram(f"acc{k}", [NP + P, D]) for k in range(K)]
        spill1, spill3 = dram("spill1", [EP, W1]), dram("spill3", [EP, W3])
        state1, state2, state3 = dram("state1", [EP + 1, D]), dram("state2", [EP + 1, 2 * D]), dram("state3", [EP + 1, D])
        betas = dram("betas", [EP + 1, R])
        carry1, carry2, carry3 = dram("carry1", [P + 1, D]), dram("carry2", [P + 1, 2 * D]), dram("carry3", [P + 1, D])

        meta = sb("meta", [P, NG, M_W], I32)
        metaf = meta[:, :, :].bitcast(F32)
        ring = sb("ring", [P, 2, M_W], I32)
        ringf = ring[:, :, :].bitcast(F32)
        base = sb("base", [P, T])
        etypef = sb("etypef", [P, T])
        ns = sb("ns", [P, T])
        neg = sb("neg", [P, T])
        nl = sb("nl", [P, T])
        last = sb("last", [P, T])
        first_last = sb("first_last", [P, T])
        score = sb("score", [P, H, T])
        dst0 = sb("dst0", [P, 1], I32)
        zidx, eidx, cidx = sb("zidx", [P, NT], I32), sb("eidx", [P, NT], I32), sb("cidx", [P, NT], I32)
        nodev = sb("nodev", [P, 8, NT])
        xn, hn, agg = (sb(n, [P, NT, D]) for n in ("xn", "hn", "agg"))
        lnv = sb("lnv", [P, 4, NT])
        hst = sb("hst", [P, NB, D])
        hT = sb("hT", [D, NB, P])
        ident, lower, upper, ones, valid = (sb(n, [P, P]) for n in ("ident", "lower", "upper", "ones", "valid"))
        zero = sb("zero", [P, 1024])
        iota_row = sb("iota_row", [P, P])
        trash = sb("trash", [P, 1])
        node_trash = sb("node_trash", [P, NT])
        nhs_row, hneg_row, nhl_row = sb("nhs_row", [P, P]), sb("hneg_row", [P, P]), sb("nhl_row", [P, P])
        flags = sb("flags", [P, 2])
        tails, heads, cin = sb("tails", [P, R]), sb("heads", [P, R]), sb("cin", [P, P])
        cT = sb("cT", [P, P + 2])
        par = sb("par", [P, 16])
        sc = sb("sc", [P, 16])
        w0_sb, wself_sb, wrel_sb = sb("w0_sb", [D, D]), sb("wself_sb", [D, D]), sb("wrel_sb", [D, R, D])
        we1_sb = sb("we1_sb", [D, 2, HID])
        wn1m_sb, wn1h_sb, wn2_sb = sb("wn1m_sb", [2 * D, HID]), sb("wn1h_sb", [D, HID]), sb("wn2_sb", [HID, D])
        wlr_sb = sb("wlr_sb", [D, 2, HD])
        wf1_sb, wf2_sb = sb("wf1_sb", [D, FF]), sb("wf2_sb", [P, 2, D])
        rowb = sb("rowb", [P, 3520])
        colb = sb("colb", [P, 4])
        wa = sb("wa", [D, 2, R])
        lowest = sb("lowest", [P, D])
        arena = sb("arena", [P, 25200])
        psum = ctx.enter_context(nc.psum_tensor("psum", [P, 8, 512], F32))

        def area(at, *shape):
            n = 1
            for s in shape:
                n *= s
            assert at + n <= 25200
            v = arena[:, at:at + n]
            if len(shape) == 2:
                v = v.rearrange("p (a b) -> p a b", b=shape[1])
            if len(shape) == 3:
                v = v.rearrange("p (a b c) -> p a b c", b=shape[1], c=shape[2])
            return v

        def bank(b, n=1):
            return psum[:, b:b + n, :].rearrange("p a b -> p (a b)")

        names = [("b0", D, b0), ("b_self", D, b_self), ("bias_rel", R * D, bias_rel), ("be1", HID, be1),
                 ("we2", HID, we2), ("bn2", D, bn2), ("b_l", HD, b_l), ("b_r", HD, b_r), ("att", HD, att),
                 ("bias_gat", D, bias_gat), ("gamma1", D, gamma1), ("beta1", D, beta1), ("gamma2", D, gamma2),
                 ("beta2", D, beta2), ("b_f2", D, b_f2), ("a_src", R * D, a_src), ("a_dst", R * D, a_dst)]
        row, row_loads, at = {}, [], 0
        for name, width, source in names:
            row[name] = rowb[:, at:at + width]
            row_loads.append((row[name], source.flatten() if len(source.shape) > 1 else source))
            at += width
        assert at <= 3520

        def over(ap, *shape):
            return ap.to_broadcast(list(shape))

        dext = area(0, T + 2)
        ints = arena[:, 800:800 + T + 2].bitcast(I32)
        srci = arena[:, 1600:1600 + T].bitcast(I32)
        typei = arena[:, 2400:2400 + T].bitcast(I32)
        adj_sb, deg_sb = area(3200, T), area(4000, T)
        tmpa, tmpb, srcf = area(4800, T), area(5600, T + 1), area(6400, T)
        pn, im = area(7200, T), area(8000, T)
        hot_p = arena[:, 8800:8800 + 2 * K * P // 2].bitcast(BF16).rearrange("p (a c) -> p a c", c=P)
        hot_i = arena[:, 9900:9900 + 2 * K * NT // 2].bitcast(BF16).rearrange("p (a c) -> p a c", c=NT)
        tb0 = area(23500, NT, W0)
        g0, z0, hold0 = area(0, 2, K, W0), area(1100, 2, K, W0), area(2200, W0)
        prod0, eq0, eql0 = area(2300, K, D), area(2900, 2 * K, P).rearrange("p (h k) c -> p h k c", k=K), area(5000, K, P)
        msg0, merged0 = area(6100, 2, K, D), area(7200, 2, K, D)
        cnt0, sidx0 = area(8300, 8, K), arena[:, 8400:8400 + 2 * K].bitcast(I32).rearrange("p (a b) -> p a b", b=K)
        acc_sb = area(0, K, NT * D)
        g1, ds = area(0, 2, K, W1), area(12600, T, 2 * R)
        v1, f1 = area(0, R, T), area(6300, R, T)
        betae = area(0, T, R)
        tb1 = area(0, NB, R * W1).rearrange("p j (r c) -> p j r c", c=W1)
        dn1 = area(3000, NT, 2 * R)
        dinit1 = area(3500, 2 * R)
        gc1, y1, st1 = area(0, 2, K, W1), area(1100, K, D), area(1700, 2, K, D)
        cg = area(0, NT, D)
        beta_n = area(1700, NT, R)
        prod1 = area(2000, NB * R, D).rearrange("p (j r) c -> p j r c", r=R)
        red1 = area(4700, NB, D)
        tb2 = area(0, NB, W2)
        bn_rows = area(1000, NT, HID)
        g2, z2, hold2 = area(0, 2, K, W2), area(3100, 2, K, HID), area(5200, HID)
        zs2, pr2, e2 = area(5400, K, HID), area(6500, K, HID), area(7600, 4, K)
        m2, st2 = area(7700, 2, K, D), area(8800, 2, K, 2 * D)
        agg2, cg2 = area(0, NT, 2 * D), area(3300, NT, 2 * D)
        mst2, mT2, hidT2 = area(6600, NB, 2 * D), area(7300, BC), area(8000, BC)
        tb3 = area(0, NB, W3)
        xr_rows = area(1400, NT, W3)
        g3, z3, hold3 = area(0, 2, K, W3), area(4200, 2, K, W3), area(8400, W3)
        zs3, pr3, rs3 = area(8700, K, W3), area(10800, K, HD), area(12900, K, H)
        f3 = area(0, H, T)
        gc3, y3, ys3, st3 = area(0, 2, K, W3), area(4200, K, HD), area(6300, K, D), area(6900, 2, K, D)
        hid3 = area(1700, 2, BC)
        red3 = area(3100, NB, D)
        bnv = area(3500, 6, D)

        x_in, edges_in, params_in = sem("x_in"), sem("edges_in"), sem("params_in")
        zero0_out, zero_out = sem("zero0_out"), sem("zero_out")
        tab_out = [sem(f"tab_out{n}") for n in range(4)]
        rows_out = [sem(f"rows_out{n}") for n in range(4)]
        put_out = [sem(f"put_out{n}") for n in range(4)]
        hold_in = [sem(f"hold_in{n}") for n in range(4)]
        passes_of = ("0", "1a", "1c", "2", "3a", "3c")
        ring_in = {n: [sem(f"ring_in{n}{h}") for h in range(2)] for n in passes_of}
        rows_in = {n: [sem(f"rows_in{n}{h}") for h in range(2)] for n in passes_of}
        got = {n: [sem(f"got{n}{h}") for h in range(2)] for n in ("0", "1a", "2", "3a")}
        kept = {n: [sem(f"kept{n}{h}") for h in range(2)] for n in ("1a", "1c", "2", "3a", "3c")}
        added = [sem(f"added{h}") for h in range(2)]
        acc_in, ds_in, beta_out = sem("acc_in"), sem("ds_in"), sem("beta_out")
        carry_out = [sem(f"carry_out{n}") for n in range(4)]
        agg_in = [sem(f"agg_in{n}") for n in range(4)]
        result_out = sem("result_out")
        padded, zeroed, consts, iotas = sem("padded"), sem("zeroed"), sem("consts"), sem("iotas")
        vec, pool_turn, pe_turn, sp_turn = sem("vec"), sem("pool_turn"), sem("pe_turn"), sem("sp_turn")
        plus_in, plus_exp, plus_ln, mix_in, mix_exp = (sem(n) for n in ("plus_in", "plus_exp", "plus_ln", "mix_in", "mix_exp"))
        hot, counted, tallied, row_totals, prefix, indices = (sem(n) for n in ("hot", "counted", "tallied", "row_totals", "prefix", "indices"))
        flags_set, flags_spread = sem("flags_set"), sem("flags_spread")
        ln_var, ln_std = sem("ln_var"), sem("ln_std")
        staged, turned, lifted, mixed, taken = (sem(n) for n in ("staged", "turned", "lifted", "mixed", "taken"))
        hidden, hidden_up, lifted_m, turned_m = sem("hidden"), sem("hidden_up"), sem("lifted_m"), sem("turned_m")
        flags_read = sem("flags_read")
        BACKWARD = (1, 3, 7, 9)
        node_vec = [sem(f"node_vec{n}") for n in range(7)]
        norm_in, norm_out = sem("norm_in"), sem("norm_out")
        filled, dots, wa_set = sem("filled"), sem("dots"), sem("wa_set")
        src_rows, equal, messages, merged, lifted0, sidx_set, slot_free = (
            sem(n) for n in ("src_rows", "equal", "messages", "merged", "lifted0", "sidx_set", "slot_free"))
        scattered = sem("scattered")
        dn_set, rows_set = sem("dn_set"), sem("rows_set")
        taken1, work1c, filled2, work2, gate2, scan2, filled3, work3, work3c = (
            sem(n) for n in ("taken1", "work1c", "filled2", "work2", "gate2", "scan2", "filled3", "work3", "work3c"))
        end1, end2, end3 = sem("end1"), sem("end2"), sem("end3")
        soft_in, soft_exp = sem("soft_in"), sem("soft_exp")
        beta_set = sem("beta_set")
        c_tail, c_turn, c_scan, c_back, c_in = (sem(n) for n in ("c_tail", "c_turn", "c_scan", "c_back", "c_in"))
        bn_in, bn_sum, bn_var, bn_std = (sem(n) for n in ("bn_in", "bn_sum", "bn_var", "bn_std"))
        result_set = sem("result_set")

        def need(engine, semaphore, value):
            if not isinstance(value, int) or value > 0:
                engine.wait_ge(semaphore, value)

        def batches(engine, body):
            body(0)
            with engine.Fori(1, NBATCH) as b:
                body(b)

        by_node = "(p i) c -> p i c"
        by_edge = "(p t) c -> p t c"

        def group_rows(table, g):
            return table[0:EP, :].rearrange(by_edge, t=T)[:, bass.ds(g * K, K), :]

        def clear(engine, table, count, width, semaphore):
            engine.dma_start(table.rearrange("(p t) c -> p (t c)", p=P).rearrange("p (n w) -> p n w", w=width),
                             over(zero[:, 0:width].unsqueeze(1), P, count, width)).then_inc(semaphore, 16)

        block = ctx.enter_context(nc.Block())

        @block.sync
        def _(sp):
            sp.wait_ge(padded, 7)
            sp.dma_start(ints[0:P - 1, 1:T + 1], dst[0:EP - T].rearrange("(p t) -> p t", t=T)).then_inc(edges_in, 16)
            sp.dma_start(ints[P - 1:P, 1:EL + 1], dst[EP - T:E].unsqueeze(0)).then_inc(edges_in, 16)
            with nc.allow_non_contiguous_dma(reason="one neighbour of each partition's edges"):
                sp.dma_start(ints[1:P, 0:1], dst[T - 1::T].unsqueeze(1)).then_inc(edges_in, 16)
                sp.dma_start(ints[0:P - 1, T + 1:T + 2], dst[T::T].unsqueeze(1)).then_inc(edges_in, 16)
            for tile, array in ((srci, src), (typei, etype), (adj_sb, adj_v), (deg_sb, deg_v)):
                sp.dma_start(tile[0:P - 1, :], array[0:EP - T].rearrange("(p t) -> p t", t=T)).then_inc(edges_in, 16)
                sp.dma_start(tile[P - 1:P, 0:EL], array[EP - T:E].unsqueeze(0)).then_inc(edges_in, 16)
            sp.dma_start(xn[0:NV, :, :], x.rearrange(by_node, i=NT)).then_inc(x_in, 16)
            for tile, array in ((w0_sb[:, :], w0), (wself_sb[:, :], w_self), (wn1m_sb[0:D, :], wn1[D:2 * D, :]), (wn1m_sb[D:2 * D, :], wn1[0:D, :]), (wn1h_sb[:, :], wn1[2 * D:, :]),
                                (wn2_sb[:, :], wn2), (wf1_sb[:, :], w_f1)):
                sp.dma_start(tile, array).then_inc(params_in, 16)
            sp.dma_start(wrel_sb[:, :, :], w_rel.rearrange("r d f -> d r f")).then_inc(params_in, 16)
            sp.dma_start(we1_sb[:, :, :], we1.rearrange("(a d) f -> d a f", a=2)).then_inc(params_in, 16)
            sp.dma_start(wf2_sb[:, :, :], w_f2.rearrange("(a d) f -> d a f", a=2)).then_inc(params_in, 16)
            sp.dma_start(wlr_sb[:, 0, :], w_l).then_inc(params_in, 16)
            sp.dma_start(wlr_sb[:, 1, :], w_r).then_inc(params_in, 16)
            for tile, array in row_loads:
                sp.dma_start(tile, array.partition_broadcast(P)).then_inc(params_in, 16)
            for at, array in ((0, deg_coeff), (2, coeff_param), (5, scale_param), (6, be2)):
                sp.dma_start(par[:, at:at + array.shape[0]], array.partition_broadcast(P)).then_inc(params_in, 16)
            with nc.allow_non_contiguous_dma(reason="bias columns"):
                sp.dma_start(colb[:, 0:1], bn1.unsqueeze(1)).then_inc(params_in, 16)
                sp.dma_start(colb[:, 1:3], b_f1.rearrange("(a p) -> p a", a=2)).then_inc(params_in, 16)

            sp.wait_ge(zeroed, 2)
            clear(sp, put0[0:EP, :], T * W0 // 980, 980, zero0_out)
            for k in range(K):
                clear(sp, acc[k][:, :], 2, (NP + P) * D // P // 2, zero0_out)

            def ring_load(n, g, h, first, i, used):
                for semaphore, value in used:
                    need(sp, semaphore, value)
                sp.dma_start(ring[:, h, :], meta[:, bass.ds(g, 1), :].rearrange("p a w -> p (a w)")).then_inc(ring_in[n][h], 16)

            sp.wait_ge(norm_out, 1)
            sp.dma_start(tab0.rearrange(by_node, i=NT), tb0).then_inc(tab_out[0], 16)
            sp.wait_ge(put_out[0], 16 * NT)

            def load0(i, h, first):
                g = i * 2 + h
                ring_load("0", g, h, first, i, () if first else ((got["0"][h], i * 16 * K), (messages, g - 1), (sidx_set, g - 1), (src_rows, g - 1)))
                sp.dma_start(z0[:, h, :, :], group_rows(put0, g)).then_inc(rows_in["0"][h], 16)
            passes(sp, load0)
            sp.wait_ge(scattered, 1)
            for k in range(K):
                sp.dma_start(acc_sb[:, k, :], acc[k][0:NP, :].rearrange("(p i) c -> p (i c)", i=NT)).then_inc(acc_in, 16)

            def table1(b):
                sp.wait_ge(taken, 5 + b + 1)
                sp.sem_inc(sp_turn, 1)
                sp.dma_start(tab1.rearrange("(p i r) c -> p i r c", i=NT, r=R)[:, bass.ds(b * NB, NB), :, :], tb1).then_inc(tab_out[1], 16)
            batches(sp, table1)
            sp.wait_ge(dn_set, 1)
            sp.dma_start(rows1.rearrange(by_node, i=NT), dn1).then_inc(rows_out[1], 16)
            sp.wait_ge(put_out[1], 16 * NT)
            sp.dma_start(ds, put1[0:EP, :].rearrange(by_edge, t=T)).then_inc(ds_in, 16)

            def load1a(i, h, first):
                g = i * 2 + h
                ring_load("1a", g, h, first, i, () if first else ((got["1a"][h], i * 16 * K),))
            passes(sp, load1a)
            sp.wait_ge(beta_set, 1)
            sp.dma_start(betas[0:EP, :].rearrange(by_edge, t=T), betae).then_inc(beta_out, 16)
            sp.wait_ge(beta_out, 16)

            def load1c(i, h, first):
                g = i * 2 + h
                ring_load("1c", g, h, first, i, () if first else ((work1c, (g - 1) * 9),))
                sp.dma_start(gc1[:, h, :, :], group_rows(spill1, g)).then_inc(rows_in["1c"][h], 16)
            passes(sp, load1c)

            def carry_store(n, uses, table, width):
                sp.wait_ge(c_in, uses)
                sp.dma_start(table[0:P, :], cin[:, 0:width]).then_inc(carry_out[n], 16)
            carry_store(1, 5, carry1, D)

            def table2(b):
                sp.wait_ge(taken, 15 + b + 1)
                sp.sem_inc(sp_turn, 1)
                sp.dma_start(tab2.rearrange(by_node, i=NT)[:, bass.ds(b * NB, NB), :], tb2).then_inc(tab_out[2], 16)
            batches(sp, table2)
            sp.dma_start(rows2.rearrange(by_node, i=NT), bn_rows).then_inc(rows_out[2], 16)
            sp.wait_ge(put_out[2], 16 * NT)
            sp.wait_ge(rows_out[2], 16)

            def load2(i, h, first):
                g = i * 2 + h
                ring_load("2", g, h, first, i, () if first else ((got["2"][h], i * 16 * K), (scan2, (g - 1) * 2 * K)))
                if not first:
                    sp.wait_ge(work2, (g - 1) * 4)
                sp.dma_start(z2[:, h, :, :], group_rows(put2, g)).then_inc(rows_in["2"][h], 16)
            passes(sp, load2)
            carry_store(2, 6, carry2, 2 * D)

            def table3(b):
                sp.wait_ge(taken, 25 + b + 1)
                sp.sem_inc(sp_turn, 1)
                sp.dma_start(tab3.rearrange(by_node, i=NT)[:, bass.ds(b * NB, NB), :], tb3).then_inc(tab_out[3], 16)
            batches(sp, table3)
            sp.dma_start(rows3.rearrange(by_node, i=NT), xr_rows).then_inc(rows_out[3], 16)
            sp.wait_ge(put_out[3], 16 * NT)
            sp.wait_ge(rows_out[3], 16)

            def load3a(i, h, first):
                g = i * 2 + h
                ring_load("3a", g, h, first, i, () if first else ((work3, (g - 1) * 4), (got["3a"][h], i * 16 * K)))
                sp.dma_start(z3[:, h, :, :], group_rows(put3, g)).then_inc(rows_in["3a"][h], 16)
            passes(sp, load3a)

            def load3c(i, h, first):
                g = i * 2 + h
                ring_load("3c", g, h, first, i, () if first else ((work3c, (g - 1) * 10),))
                sp.dma_start(gc3[:, h, :, :], group_rows(spill3, g)).then_inc(rows_in["3c"][h], 16)
            sp.wait_ge(end3, 1)
            passes(sp, load3c)
            carry_store(3, 11, carry3, D)
            sp.wait_ge(result_set, 1)
            sp.dma_start(out.rearrange(by_node, i=NT), xn[0:NV, :, :]).then_inc(result_out, 16)
            sp.wait_ge(result_out, 16)

        @block.gpsimd
        def _(pool):
            tally = Tally(pool)
            tally.done(pool.memset(ones[:, :], 1.0), consts)
            tally.done(pool.memset(ident[:, :], 0.0), consts)
            tally.done(pool.affine_select(out=ident[:, :], in_=ident[:, :], compare_op=ALU.not_equal, fill=1.0, base=0,
                                          pattern=[[-1, P]], channel_multiplier=1), consts)
            tally.done(pool.affine_select(out=lower[:, :], in_=ones[:, :], compare_op=ALU.is_gt, fill=0.0, base=0,
                                          pattern=[[-1, P]], channel_multiplier=1), consts)
            tally.done(pool.affine_select(out=upper[:, :], in_=ones[:, :], compare_op=ALU.is_gt, fill=0.0, base=0,
                                          pattern=[[1, P]], channel_multiplier=-1), consts)
            tally.done(pool.affine_select(out=valid[:, :], in_=ones[:, :], compare_op=ALU.is_ge, fill=0.0, base=NV - 1,
                                          pattern=[[0, P]], channel_multiplier=-1), consts)
            tally.done(pool.iota(iota_row[:, :], pattern=[[1, P]], base=0, channel_multiplier=0,
                                 allow_small_or_imprecise_dtypes=True), consts)
            tally.done(pool.iota(trash[:, :], pattern=[[1, 1]], base=NP, channel_multiplier=1,
                                 allow_small_or_imprecise_dtypes=True), consts)
            tally.done(pool.iota(node_trash[:, :], pattern=[[1, NT]], base=EP, channel_multiplier=NT,
                                 allow_small_or_imprecise_dtypes=True), consts)

            def ready(*waits):
                for semaphore, value in waits:
                    need(pool, semaphore, value)
                pool.sem_inc(pool_turn, 1)

            def put(n, table, rows):
                for i in range(NT):
                    pool.indirect_dma_start(out=table[:, :], out_offset=bass.IndirectOffsetOnAxis(ap=zidx[:, i:i + 1], axis=0),
                                            in_=rows[:, i, :], in_offset=None).then_inc(put_out[n], 16)

            def hold(n, table, rows):
                pool.indirect_dma_start(out=rows, out_offset=None, in_=table[:, :],
                                        in_offset=bass.IndirectOffsetOnAxis(ap=dst0[:, :], axis=0)).then_inc(hold_in[n], 16)

            def gather(n, table, rows, word, h):
                for k in range(K):
                    pool.indirect_dma_start(out=rows[:, h, k, :], out_offset=None, in_=table[:, :],
                                            in_offset=bass.IndirectOffsetOnAxis(ap=ring[:, h, word + k:word + k + 1], axis=0)
                                            ).then_inc(got[n][h], 16)

            def collect(n, table, index, rows):
                for i in range(NT):
                    pool.indirect_dma_start(out=rows[:, i, :], out_offset=None, in_=table[:, :],
                                            in_offset=bass.IndirectOffsetOnAxis(ap=index[:, i:i + 1], axis=0)).then_inc(agg_in[n], 16)

            ready((indices, 1), (norm_out, 1), (zero0_out, 16 * (1 + K)))
            put(0, put0, tb0)
            ready((tab_out[0], 16))
            hold(0, tab0, hold0)

            def gather0(i, h, first):
                g = i * 2 + h
                ready((ring_in["0"][h], i * 16 + 16), *(() if first else ((dots, (g - 1) * 14),)))
                gather("0", tab0, g0, M_SRC, h)

            def add0(i, h, first, last_add):
                g = i * 2 + h
                ready((lifted0, g + 1), (sidx_set, g + 1), *(() if last_add is None else ((added[1 - h], last_add),)))
                if last_add is not None:
                    pool.sem_inc(slot_free, 1)
                for k in range(K):
                    pool.indirect_dma_start(out=acc[k][:, :], out_offset=bass.IndirectOffsetOnAxis(ap=sidx0[:, h, k:k + 1], axis=0),
                                            in_=merged0[:, h, k, :], in_offset=None, compute_op=ALU.add).then_inc(added[h], 16)

            gather0(0, 0, True)
            gather0(0, 1, True)
            add0(0, 0, True, None)
            gather0(1, 0, False)
            add0(0, 1, True, 16 * K)
            with pool.Fori(1, LOOPS - 1) as i:
                gather0(i, 1, False)
                add0(i, 0, False, i * 16 * K)
                gather0(i + 1, 0, False)
                add0(i, 1, False, i * 16 * K + 16 * K)
            gather0(LOOPS - 1, 1, False)
            add0(LOOPS - 1, 0, False, (LOOPS - 1) * 16 * K)
            add0(LOOPS - 1, 1, False, LOOPS * 16 * K)
            pool.wait_ge(added[1], LOOPS * 16 * K)
            pool.sem_inc(scattered, 1)

            ready((dn_set, 1), (zero_out, 16 * 11))
            put(1, put1, dn1)
            ready((rows_out[1], 16))
            hold(1, rows1, dinit1)
            ready((tab_out[1], 16 * NBATCH))

            def gather1(i, h, first):
                g = i * 2 + h
                ready((ring_in["1a"][h], i * 16 + 16), *(() if first else ((taken1, g - 1), (kept["1a"][h], i * 16))))
                gather("1a", tab1, g1, M_REL, h)
            passes(pool, gather1)
            ready((end1, 1), (kept["1c"][0], 16 * LOOPS), (kept["1c"][1], 16 * LOOPS), (carry_out[1], 16))
            collect(1, state1, eidx, agg)
            collect(1, carry1, cidx, cg)
            collect(1, betas, eidx, beta_n)

            ready((taken, 20))
            put(2, put2, bn_rows)
            ready((rows_out[2], 16), (tab_out[2], 16 * NBATCH), (put_out[2], 16 * NT))
            hold(2, rows2, hold2)

            def gather2(i, h, first):
                g = i * 2 + h
                ready((ring_in["2"][h], i * 16 + 16), *(() if first else ((work2, (g - 1) * 4),)))
                gather("2", tab2, g2, M_SRC, h)
            passes(pool, gather2)
            ready((end2, 1), (kept["2"][0], 16 * LOOPS), (kept["2"][1], 16 * LOOPS), (carry_out[2], 16))
            collect(2, state2, eidx, agg2)
            collect(2, carry2, cidx, cg2)

            ready((taken, 30))
            put(3, put3, xr_rows)
            ready((rows_out[3], 16), (tab_out[3], 16 * NBATCH), (put_out[3], 16 * NT))
            hold(3, rows3, hold3)

            def gather3(i, h, first):
                g = i * 2 + h
                ready((ring_in["3a"][h], i * 16 + 16), *(() if first else ((work3, (g - 1) * 4), (kept["3a"][h], i * 16))))
                gather("3a", tab3, g3, M_SRC, h)
            passes(pool, gather3)
            ready((end3, 2), (kept["3c"][0], 16 * LOOPS), (kept["3c"][1], 16 * LOOPS), (carry_out[3], 16))
            collect(3, state3, eidx, agg)
            collect(3, carry3, cidx, cg)

        PARAMS = 16 * (7 + 5 + len(row_loads) + 4 + 2)

        @block.scalar
        def _(act):
            act.wait_ge(zeroed, 2)
            clear(act, put1[0:EP, :], 2 * R, T, zero_out)
            clear(act, put2[0:EP, :], T * HID // 1024, 1024, zero_out)
            clear(act, put3[0:EP, :], T * W3 // 980, 980, zero_out)
            for table, at, line in ((state1, EP, zero[0:1, 0:D]), (state2, EP, zero[0:1, 0:2 * D]), (state3, EP, zero[0:1, 0:D]),
                                    (carry1, P, zero[0:1, 0:D]), (carry3, P, zero[0:1, 0:D])):
                act.dma_start(table[at:at + 1, :], line).then_inc(zero_out, 16)
            act.dma_start(carry2[P:P + 1, 0:D], zero[0:1, 0:D]).then_inc(zero_out, 16)
            act.dma_start(carry2[P:P + 1, D:2 * D], lowest[0:1, :]).then_inc(zero_out, 16)
            act.wait_ge(consts, 1)
            act.dma_start(betas[EP:EP + 1, :], ones[0:1, 0:R]).then_inc(zero_out, 16)

            for n, ax in ((0, tmpb[:, 0:T]), (1, sc[:, 1:2])):
                act.wait_ge(plus_in, n + 1)
                act.activation(ax, ax, ACT.Exp, scale=-1.0).then_inc(plus_exp, 1)
                act.wait_ge(plus_exp, n + 1)
                act.activation(ax, ax, ACT.Ln, bias=1.0).then_inc(plus_ln, 1)
            act.wait_ge(mix_in, 1)
            act.activation(sc[:, 4:7], sc[:, 4:7], ACT.Exp).then_inc(mix_exp, 1)

            def deviation(n):
                act.wait_ge(ln_var, n + 1)
                act.activation(lnv[:, 2, :], lnv[:, 1, :], ACT.Sqrt).then_inc(ln_std, 1)

            def lift(s, b):
                act.wait_ge(turned, 5 * s + b + 1)
                need(act, mixed, 5 * s + b)
                act.activation(hT[:, :, :], bank(6, 2)[0:D, 0:BC].rearrange("d (j n) -> d j n", n=P), ACT.Copy).then_inc(lifted, 1)

            def lift_only(s):
                batches(act, lambda b: lift(s, b))

            deviation(0)
            lift_only(0)
            act.wait_ge(norm_in, 1)
            act.activation(tb0[:, :, D:W0], lnv[:, 0, :].unsqueeze(2), ACT.Sqrt).then_inc(norm_out, 1)

            def lift0(i, h, first):
                g = i * 2 + h
                act.wait_ge(merged, g + 1)
                if not first:
                    act.wait_ge(slot_free, g - 1)
                act.activation(merged0[:, h, :, :], bank(4 + h).rearrange("p (k c) -> p k c", c=D), ACT.Copy).then_inc(lifted0, 1)
            passes(act, lift0)

            deviation(1)
            lift_only(1)

            def keep1a(i, h, first):
                act.wait_ge(got["1a"][h], i * 16 * K + 16 * K)
                act.dma_start(group_rows(spill1, i * 2 + h), g1[:, h, :, :]).then_inc(kept["1a"][h], 16)
            passes(act, keep1a)
            for h in range(2):
                act.wait_ge(kept["1a"][h], 16 * LOOPS)
            act.wait_ge(soft_in, 1)
            act.activation(v1, v1, ACT.Exp).then_inc(soft_exp, 1)
            act.activation(ds[:, :, R:2 * R], ds[:, :, R:2 * R], ACT.Exp).then_inc(soft_exp, 1)

            def keep1c(i, h, first):
                g = i * 2 + h
                act.wait_ge(work1c, g * 9 + 9)
                act.dma_start(group_rows(state1, g), st1[:, h, :, :]).then_inc(kept["1c"][h], 16)
            passes(act, keep1c)
            lift_only(2)

            deviation(2)
            lift_only(3)

            def gate(i, h, first):
                g = i * 2 + h
                act.wait_ge(work2, g * 4 + 3)
                act.activation(e2[:, 2 + h, :], e2[:, h, :], ACT.Sigmoid, bias=par[:, 6:7]).then_inc(gate2, 1)
                act.wait_ge(scan2, g * 2 * K + 2 * K)
                act.dma_start(group_rows(state2, g), st2[:, h, :, :]).then_inc(kept["2"][h], 16)
            passes(act, gate)

            def lift2(b):
                lift(4, b)
                act.wait_ge(turned_m, b + 1)
                act.activation(mT2, bank(4, 2)[:, 0:BC], ACT.Copy).then_inc(lifted_m, 1)
                act.wait_ge(hidden, b + 1)
                act.activation(hidT2, bank(0, 2)[:, 0:BC], ACT.Relu, bias=colb[:, 0:1]).then_inc(hidden_up, 1)
            batches(act, lift2)

            deviation(3)
            lift_only(5)

            def keep3a(i, h, first):
                act.wait_ge(got["3a"][h], i * 16 * K + 16 * K)
                act.dma_start(group_rows(spill3, i * 2 + h), g3[:, h, :, :]).then_inc(kept["3a"][h], 16)
            passes(act, keep3a)
            for h in range(2):
                act.wait_ge(kept["3a"][h], 16 * LOOPS)
            act.wait_ge(soft_in, 2)
            act.activation(score[:, :, :], score[:, :, :], ACT.Exp).then_inc(soft_exp, 1)

            def keep3c(i, h, first):
                g = i * 2 + h
                act.wait_ge(work3c, g * 10 + 10)
                act.dma_start(group_rows(state3, g), st3[:, h, :, :]).then_inc(kept["3c"][h], 16)
            passes(act, keep3c)
            act.wait_ge(bn_var, 1)
            act.activation(bnv[:, 3, :], bnv[:, 2, :], ACT.Sqrt).then_inc(bn_std, 1)

            def lift3(b):
                lift(6, b)
                for c in range(2):
                    act.wait_ge(hidden, NBATCH + 2 * b + c + 1)
                    act.activation(hid3[:, c, :], bank(2 * c, 2)[:, 0:BC], ACT.Relu, bias=colb[:, 1 + c:2 + c]).then_inc(hidden_up, 1)
            batches(act, lift3)
            act.wait_ge(bn_var, 2)
            act.activation(bnv[:, 3, :], bnv[:, 2, :], ACT.Sqrt).then_inc(bn_std, 1)

        @block.tensor
        def _(pe):
            pe.wait_ge(consts, 9)
            pe.wait_ge(params_in, PARAMS)

            def turn(s, b):
                pe.wait_ge(staged, 5 * s + b + 1)
                need(pe, lifted, 5 * s + b)
                pe.sem_inc(pe_turn, 1)
                for j in range(NB):
                    mm = pe.transpose(bank(6, 2)[0:D, j * P:(j + 1) * P], hst[:, j, :], ident[:, :])
                return mm

            def mix(s, b, products):
                turn(s, b).then_inc(turned, 1)
                pe.wait_ge(lifted, 5 * s + b + 1)
                need(pe, taken, 5 * s + b)
                for j in range(NB):
                    for at, rhs in products:
                        width = rhs.shape[1]
                        mm = pe.matmul(bank(0, 6)[:, at + j * width:at + (j + 1) * width], lhsT=hT[:, j, :], rhs=rhs,
                                       start=True, stop=True)
                mm.then_inc(mixed, 1)

            def spread(column, b, at):
                return pe.matmul(bank(b)[:, at:at + P], lhsT=over(column, P, P), rhs=ident[:, :], start=True, stop=True)

            def carry(use, tail, width):
                pe.wait_ge(c_tail, use + 1)
                pe.transpose(bank(0)[0:width, 0:P], tail, ident[:, :]).then_inc(c_turn, 1)
                pe.wait_ge(c_scan, use + 1)
                pe.transpose(bank(1)[:, 0:width], cT[0:width, 1:P + 1] if use in BACKWARD else cT[0:width, 0:P],
                             ident[0:width, 0:width]).then_inc(c_back, 1)

            batches(pe, lambda b: mix(0, b, [(0, w0_sb[:, :])]))

            pe.wait_ge(taken, NBATCH)

            def count(i, h, first):
                g = i * 2 + h
                pe.wait_ge(hot, i * 4 + 2 * h + 2)
                if not first:
                    pe.wait_ge(tallied, g)
                for k in range(K):
                    mm = pe.matmul(bank(h)[:, 0:NT], lhsT=hot_p[:, h * K + k, :], rhs=hot_i[:, h * K + k, :], start=(k == 0),
                                   stop=(k == K - 1))
                mm.then_inc(counted, 1)
            passes(pe, count)
            pe.wait_ge(row_totals, 1)
            pe.matmul(bank(1)[:, 0:1], lhsT=upper[:, :], rhs=nodev[:, 1, NT - 1:NT], start=True, stop=True).then_inc(prefix, 1)
            pe.wait_ge(flags_set, 2)
            spread(flags[:, 0:1], 2, 0).then_inc(flags_spread, 1)
            spread(flags[:, 1:2], 2, P).then_inc(flags_spread, 1)

            pe.wait_ge(flags_read, 3)

            def merge0(i, h, first):
                g = i * 2 + h
                pe.wait_ge(ring_in["0"][h], i * 16 + 16)
                if not first:
                    pe.wait_ge(equal, g - 1)
                for k in range(K):
                    mm = spread(ringf[:, h, M_SRCF + k:M_SRCF + k + 1], 2 * h + k // 4, k % 4 * P)
                mm.then_inc(src_rows, 1)
                pe.wait_ge(equal, g + 1)
                pe.wait_ge(messages, g + 1)
                if not first:
                    pe.wait_ge(lifted0, g - 1)
                for k in range(K):
                    mm = pe.matmul(bank(4 + h)[:, k * D:(k + 1) * D], lhsT=eq0[:, h, k, :], rhs=msg0[:, h, k, :], start=True, stop=True)
                mm.then_inc(merged, 1)
            passes(pe, merge0)

            pe.wait_ge(lifted0, NG)
            pe.wait_ge(equal, NG)
            pe.wait_ge(wa_set, 2)
            wrel_all = wrel_sb[:, :, :].rearrange("d r f -> d (r f)")
            batches(pe, lambda b: mix(1, b, [(0, wrel_all), (5 * 512, wa[:, :, :].rearrange("d a r -> d (a r)"))]))
            pe.wait_ge(taken, 2 * NBATCH)
            carry(0, tails[:, :], R)
            carry(1, heads[:, :], R)
            carry(2, tails[:, :], R)
            carry(3, heads[:, :], R)
            carry(4, st1[:, 1, K - 1, :], D)
            pe.wait_ge(c_in, 5)
            batches(pe, lambda b: mix(2, b, [(0, wrel_all), (5 * 512, wself_sb[:, :])]))

            batches(pe, lambda b: mix(3, b, [(0, we1_sb[:, :, :].rearrange("d a f -> d (a f)"))]))
            pe.wait_ge(taken, 4 * NBATCH)
            carry(5, st2[:, 1, K - 1, :], 2 * D)
            pe.wait_ge(c_in, 6)

            def mlp2(b):
                turn(4, b).then_inc(turned, 1)
                need(pe, lifted_m, b)
                for j in range(NB):
                    mm = pe.transpose(bank(4, 2)[:, j * P:(j + 1) * P], mst2[:, j, :], ident[:, :])
                mm.then_inc(turned_m, 1)
                pe.wait_ge(lifted, 20 + b + 1)
                pe.wait_ge(lifted_m, b + 1)
                need(pe, hidden_up, b)
                for lo, hi in ((0, 512), (512, BC)):
                    pe.matmul(bank(0, 2)[:, lo:hi], lhsT=wn1m_sb[:, :], rhs=mT2[:, lo:hi], start=True, stop=False)
                    mm = pe.matmul(bank(0, 2)[:, lo:hi], lhsT=wn1h_sb[:, :], rhs=hT[:, :, :].rearrange("d j n -> d (j n)")[:, lo:hi],
                                   start=False, stop=True)
                mm.then_inc(hidden, 1)
                pe.wait_ge(hidden_up, b + 1)
                need(pe, taken, 20 + b)
                for j in range(NB):
                    mm = pe.matmul(bank(2)[:, j * D:(j + 1) * D], lhsT=hidT2[:, j * P:(j + 1) * P], rhs=wn2_sb[:, :], start=True, stop=True)
                mm.then_inc(mixed, 1)
            batches(pe, mlp2)

            pe.wait_ge(taken, 5 * NBATCH)
            batches(pe, lambda b: mix(5, b, [(0, wlr_sb[:, :, :].rearrange("d a f -> d (a f)"))]))
            pe.wait_ge(taken, 6 * NBATCH)
            carry(6, tails[:, 0:H], H)
            carry(7, heads[:, 0:H], H)
            carry(8, tails[:, 0:H], H)
            carry(9, heads[:, 0:H], H)
            carry(10, st3[:, 1, K - 1, :], D)
            pe.wait_ge(c_in, 11)

            def node_sum(n):
                pe.wait_ge(bn_in, n + 1)
                pe.matmul(bank(0)[:, 0:D], lhsT=valid[:, :], rhs=bnv[:, 0, :], start=True, stop=True).then_inc(bn_sum, 1)
            node_sum(0)
            node_sum(1)

            def mlp3(b):
                turn(6, b).then_inc(turned, 1)
                pe.wait_ge(lifted, 30 + b + 1)
                need(pe, hidden_up, NBATCH + 2 * b)
                for c in range(2):
                    for lo, hi in ((0, 512), (512, BC)):
                        mm = pe.matmul(bank(2 * c, 2)[:, lo:hi], lhsT=wf1_sb[:, c * P:(c + 1) * P],
                                       rhs=hT[:, :, :].rearrange("d j n -> d (j n)")[:, lo:hi], start=True, stop=True)
                    mm.then_inc(hidden, 1)
                pe.wait_ge(hidden_up, NBATCH + 2 * b + 2)
                need(pe, taken, 30 + b)
                for j in range(NB):
                    for c in range(2):
                        mm = pe.matmul(bank(4)[:, j * D:(j + 1) * D], lhsT=hid3[:, c, j * P:(j + 1) * P], rhs=wf2_sb[:, c, :],
                                       start=(c == 0), stop=(c == 1))
                mm.then_inc(mixed, 1)
            batches(pe, mlp3)
            pe.wait_ge(taken, 7 * NBATCH)
            node_sum(2)
            node_sum(3)

        @block.vector
        def _(dve):
            tally = Tally(dve)

            def step(instruction):
                tally.done(instruction, vec)

            def spread(ap, *shape):
                return ap.to_broadcast(list(shape))

            for tile, value in ((ints[:, 0:T + 1], N), (ints[:, T + 1:T + 2], -1), (srci, N), (typei, 0)):
                dve.memset(tile, value).then_inc(padded, 1)
            for tile in (adj_sb, deg_sb, xn[:, :, :]):
                dve.memset(tile, 0.0).then_inc(padded, 1)
            dve.memset(zero[:, :], 0.0).then_inc(zeroed, 1)
            dve.memset(lowest[:, :], -BIG).then_inc(zeroed, 1)
            dve.wait_ge(zeroed, 2)

            dve.wait_ge(edges_in, 16 * 12)
            dve.wait_ge(padded, 7)
            step(dve.tensor_copy(dext, ints))
            mid = dext[:, 1:T + 1]
            step(dve.tensor_tensor(ns[:, :], mid, dext[:, 0:T], ALU.is_equal))
            step(dve.tensor_tensor(nl[:, :], mid, dext[:, 2:T + 2], ALU.is_equal))
            step(dve.tensor_scalar(neg[:, :], ns[:, :], -1.0, BIG, ALU.add, ALU.mult))
            step(dve.tensor_scalar(last[:, :], nl[:, :], -1.0, 1.0, ALU.mult, ALU.add))
            tally.done(dve.tensor_reduce(flags[:, 0:1], ns[:, :], AX.X, ALU.min), flags_set)
            tally.done(dve.tensor_reduce(flags[:, 1:2], nl[:, :], AX.X, ALU.min), flags_set)
            step(dve.memset(tmpb[:, 0:1], 1.0))
            step(dve.tensor_tensor_scan(tmpb[:, 1:T + 1], nl[:, :], zero[:, 0:T], 1.0, ALU.mult, ALU.add))
            step(dve.tensor_tensor(first_last[:, :], tmpb[:, 0:T], tmpb[:, 1:T + 1], ALU.subtract))
            step(dve.tensor_copy(srcf, srci))
            step(dve.tensor_copy(etypef[:, :], typei))
            step(dve.tensor_copy(dst0[:, :], dext[:, 1:2]))

            def by_group(ap):
                return ap.rearrange("p (g k) -> p g k", k=K)
            step(dve.tensor_copy(meta[:, :, M_SRC:M_SRC + K], by_group(srci)))
            step(dve.tensor_copy(metaf[:, :, M_NS:M_NS + K], by_group(ns[:, :])))
            step(dve.tensor_copy(metaf[:, :, M_NEG:M_NEG + K], by_group(neg[:, :])))
            step(dve.tensor_copy(metaf[:, :, M_SRCF:M_SRCF + K], by_group(srcf)))
            step(dve.scalar_tensor_tensor(out=tmpa, in0=srcf, scalar=float(R), in1=etypef[:, :], op0=ALU.mult, op1=ALU.add))
            step(dve.tensor_copy(meta[:, :, M_REL:M_REL + K], by_group(tmpa)))

            dve.wait_ge(params_in, PARAMS)

            def softplus(x, ax, result, uses):
                step(dve.scalar_tensor_tensor(out=ax, in0=x, scalar=-1.0, in1=x, op0=ALU.mult, op1=ALU.max))
                dve.sem_inc(plus_in, 1)
                dve.wait_ge(plus_ln, uses)
                step(dve.scalar_tensor_tensor(out=result, in0=x, scalar=0.0, in1=ax, op0=ALU.max, op1=ALU.add))
            step(dve.tensor_scalar(tmpa, deg_sb, par[:, 0:1], par[:, 1:2], ALU.mult, ALU.add))
            softplus(tmpa, tmpb[:, 0:T], base[:, :], 1)
            step(dve.tensor_tensor(base[:, :], base[:, :], adj_sb, ALU.mult))
            step(dve.tensor_tensor(tmpa, srcf, mid, ALU.not_equal))
            step(dve.tensor_tensor(base[:, :], base[:, :], tmpa, ALU.mult))
            softplus(par[:, 5:6], sc[:, 1:2], sc[:, 2:3], 2)
            step(dve.tensor_reduce(sc[:, 3:4], par[:, 2:5], AX.X, ALU.max))
            step(dve.tensor_scalar(sc[:, 4:7], par[:, 2:5], sc[:, 3:4], None, ALU.subtract))
            dve.sem_inc(mix_in, 1)
            dve.wait_ge(mix_exp, 1)
            step(dve.tensor_reduce(sc[:, 7:8], sc[:, 4:7], AX.X, ALU.add))
            step(dve.reciprocal(sc[:, 8:9], sc[:, 7:8]))
            step(dve.tensor_scalar(sc[:, 4:7], sc[:, 4:7], sc[:, 8:9], None, ALU.mult))
            step(dve.tensor_scalar(pn, mid, 1.0 / NT, -(NT - 1) / 2 / NT, ALU.mult, ALU.add))
            step(dve.tensor_scalar(pn, pn, ROUND, -ROUND, ALU.add, ALU.add))
            step(dve.scalar_tensor_tensor(out=im, in0=pn, scalar=-float(NT), in1=mid, op0=ALU.mult, op1=ALU.add))

            def norm_relu(n):
                col = [lnv[:, k, :] for k in range(4)]
                step(dve.tensor_reduce(col[0], xn[:, :, :], AX.X, ALU.add))
                step(dve.tensor_scalar(col[0], col[0], 1.0 / D, None, ALU.mult))
                step(dve.tensor_tensor(hn[:, :, :], xn[:, :, :], spread(col[0].unsqueeze(2), P, NT, D), ALU.subtract))
                step(dve.tensor_tensor(agg[:, :, :], hn[:, :, :], hn[:, :, :], ALU.mult))
                step(dve.tensor_reduce(col[0], agg[:, :, :], AX.X, ALU.add))
                step(dve.tensor_scalar(col[1], col[0], 1.0 / D, EPS, ALU.mult, ALU.add))
                dve.sem_inc(ln_var, 1)
                dve.wait_ge(ln_std, n + 1)
                step(dve.reciprocal(col[3], col[2]))
                step(dve.tensor_tensor(hn[:, :, :], hn[:, :, :], spread(col[3].unsqueeze(2), P, NT, D), ALU.mult))
                step(dve.tensor_scalar(hn[:, :, :], hn[:, :, :], 0.0, None, ALU.max))

            def stage(s, b, rows):
                need(dve, turned, 5 * s + b)
                return dve.tensor_scalar(hst[:, :, :], rows[:, bass.ds(b * NB, NB), :], 1.0, None, ALU.mult)

            def product(first, n, width):
                return bank(0, 6)[:, first:first + n].rearrange("p (j c) -> p j c", c=width)

            dve.wait_ge(x_in, 16)
            norm_relu(0)

            def nodes0(b):
                stage(0, b, hn).then_inc(staged, 1)
                dve.wait_ge(mixed, b + 1)
                dve.tensor_tensor(tb0[:, bass.ds(b * NB, NB), 0:D], product(0, NB * D, D), spread(row["b0"].unsqueeze(1), P, NB, D),
                                  ALU.add).then_inc(taken, 1)
            batches(dve, nodes0)
            dve.wait_ge(taken, NBATCH)
            step(dve.tensor_tensor(agg[:, :, :], tb0[:, :, 0:D], tb0[:, :, 0:D], ALU.mult))
            tally.done(dve.tensor_reduce(lnv[:, 0, :], agg[:, :, :], AX.X, ALU.add), norm_in)

            dve.wait_ge(consts, 9)

            deg, cum, end, first_edge, has, at, from_before = (nodev[:, k, :] for k in range(7))
            dve.memset(deg, 0.0).then_inc(tallied, 1)

            def tally_counts(done, h):
                dve.wait_ge(counted, done)
                dve.wait_ge(tallied, done)
                dve.tensor_tensor(deg, bank(h)[:, 0:NT], deg, ALU.add).then_inc(tallied, 1)

            def one_hot(i, h, first):
                g = i * 2 + h
                if not first:
                    tally_counts(g - 1, h)
                for hots, place, width in ((hot_p, pn, P), (hot_i, im, NT)):
                    dve.tensor_tensor(hots[:, h * K:h * K + K, :], spread(iota_row[:, 0:width].unsqueeze(1), P, K, width),
                                      spread(place[:, bass.ds(g * K, K)].unsqueeze(2), P, K, width), ALU.is_equal).then_inc(hot, 1)
            passes(dve, one_hot)
            for h in range(2):
                tally_counts(NG - 1 + h, h)
            dve.wait_ge(tallied, 1 + NG)
            tally.done(dve.tensor_tensor_scan(cum, ones[:, 0:NT], deg, 0.0, ALU.mult, ALU.add), row_totals)
            dve.wait_ge(prefix, 1)
            step(dve.tensor_scalar(end, cum, bank(1)[:, 0:1], None, ALU.add))
            step(dve.tensor_tensor(first_edge, end, deg, ALU.subtract))
            step(dve.tensor_scalar(has, deg, 0.0, None, ALU.is_gt))
            step(dve.tensor_tensor(at, first_edge, node_trash[:, :], ALU.subtract))
            step(dve.tensor_tensor(at, at, has, ALU.mult))
            step(dve.tensor_tensor(zidx[:, :], at, node_trash[:, :], ALU.add))
            step(dve.scalar_tensor_tensor(out=at, in0=end, scalar=-1.0 - EP, in1=has, op0=ALU.add, op1=ALU.mult))
            step(dve.tensor_scalar(eidx[:, :], at, float(EP), None, ALU.add))
            step(dve.tensor_scalar(at, end, 1.0 / T, -(1 + (T - 1) / 2) / T, ALU.mult, ALU.add))
            step(dve.tensor_scalar(at, at, ROUND, -ROUND, ALU.add, ALU.add))
            step(dve.scalar_tensor_tensor(out=from_before, in0=at, scalar=float(T), in1=first_edge, op0=ALU.mult, op1=ALU.is_gt))
            step(dve.tensor_tensor(from_before, from_before, has, ALU.mult))
            step(dve.scalar_tensor_tensor(out=at, in0=at, scalar=-float(P), in1=from_before, op0=ALU.add, op1=ALU.mult))
            tally.done(dve.tensor_scalar(cidx[:, :], at, float(P), None, ALU.add), indices)
            dve.wait_ge(flags_spread, 2)
            tally.done(dve.tensor_copy(nhs_row[:, :], bank(2)[:, 0:P]), flags_read)
            tally.done(dve.tensor_copy(nhl_row[:, :], bank(2)[:, P:2 * P]), flags_read)
            tally.done(dve.tensor_scalar(hneg_row[:, :], nhs_row[:, :], -1.0, BIG, ALU.add, ALU.mult), flags_read)

            def fill(beats, rows, hold, h):
                for k in range(K):
                    before = hold if k == 0 else rows[:, h, k - 1, :]
                    beats.wait()
                    beats.add(dve.scalar_tensor_tensor(out=rows[:, h, k, :], in0=before, scalar=ringf[:, h, M_NS + k:M_NS + k + 1],
                                                       in1=rows[:, h, k, :], op0=ALU.mult, op1=ALU.add))
                beats.wait()
                beats.done(dve.tensor_scalar(hold, rows[:, h, K - 1, :], 1.0, None, ALU.mult))

            def segment_sum(beats, states, values, h, before):
                for k in range(K):
                    prior = states[:, h, k - 1, :] if k else before
                    beats.wait()
                    beats.add(dve.scalar_tensor_tensor(out=states[:, h, k, :], in0=prior, scalar=ringf[:, h, M_NS + k:M_NS + k + 1],
                                                       in1=values[:, k, :], op0=ALU.mult, op1=ALU.add))

            dve.wait_ge(hold_in[0], 16)
            dve.wait_ge(flags_read, 3)
            fills0, dots0 = Beats(dve, filled, K + 1), Beats(dve, dots, 14)

            def edges0(i, h, first):
                g = i * 2 + h
                fills0.group(g)
                dots0.group(g)
                dve.wait_ge(ring_in["0"][h], i * 16 + 16)
                srcs = ringf[:, h, M_SRCF:M_SRCF + K]
                dve.wait_ge(src_rows, g + 1)
                if not first:
                    dve.wait_ge(merged, g - 1)
                dve.tensor_tensor(eq0[:, h, :, :], bank(2 * h, 2).rearrange("p (k c) -> p k c", c=P),
                                  spread(srcs.unsqueeze(2), P, K, P), ALU.is_equal).then_inc(equal, 1)
                dve.wait_ge(equal, g + 1)
                dots0.done(dve.tensor_tensor(eql0, eq0[:, h, :, :], spread(lower[:, :].unsqueeze(1), P, K, P), ALU.mult))
                dots0.done(dve.tensor_reduce(cnt0[:, 0, :], eql0, AX.X, ALU.add))
                dots0.done(dve.tensor_scalar(cnt0[:, 1, :], cnt0[:, 0, :], 0.5, None, ALU.is_lt))
                dots0.done(dve.scalar_tensor_tensor(out=cnt0[:, 2, :], in0=srcs, scalar=trash[:, 0:1], in1=cnt0[:, 1, :],
                                                    op0=ALU.subtract, op1=ALU.mult))
                if not first:
                    dve.wait_ge(slot_free, g - 1)
                dve.tensor_scalar(sidx0[:, h, :], cnt0[:, 2, :], trash[:, 0:1], None, ALU.add).then_inc(sidx_set, 1)
                dve.wait_ge(rows_in["0"][h], i * 16 + 16)
                fill(fills0, z0, hold0, h)
                dve.wait_ge(got["0"][h], i * 16 * K + 16 * K)
                norms, dot, sim, pos, negs = (cnt0[:, k, :] for k in range(3, 8))
                dots0.add(dve.tensor_tensor(prod0, g0[:, h, :, 0:D], z0[:, h, :, 0:D], ALU.mult))
                dots0.done(dve.tensor_tensor(norms, g0[:, h, :, D], z0[:, h, :, D], ALU.mult))
                dots0.done(dve.tensor_scalar(norms, norms, 1e-8, None, ALU.max))
                dots0.add(dve.reciprocal(norms, norms))
                dots0.done(dve.tensor_reduce(dot, prod0, AX.X, ALU.add))
                dots0.done(dve.tensor_tensor(sim, dot, norms, ALU.mult))
                dots0.add(dve.tensor_scalar(pos, sim, 0.0, sc[:, 4:5], ALU.max, ALU.mult))
                dots0.done(dve.tensor_scalar(negs, sim, 0.0, sc[:, 5:6], ALU.min, ALU.mult))
                dots0.done(dve.tensor_tensor(pos, pos, negs, ALU.add))
                dots0.done(dve.tensor_tensor(pos, pos, base[:, bass.ds(g * K, K)], ALU.mult))
                dve.tensor_tensor(msg0[:, h, :, :], z0[:, h, :, 0:D], spread(pos.unsqueeze(2), P, K, D), ALU.mult).then_inc(messages, 1)
            passes(dve, edges0)
            dve.wait_ge(messages, NG)
            dve.wait_ge(acc_in, 16 * K)
            for k in range(1, K):
                step(dve.tensor_tensor(acc_sb[:, 0, :], acc_sb[:, 0, :], acc_sb[:, k, :], ALU.add))
            total = acc_sb[:, 0, :].rearrange("p (i c) -> p i c", c=D)
            step(dve.scalar_tensor_tensor(out=total, in0=tb0[:, :, 0:D], scalar=sc[:, 6:7], in1=total, op0=ALU.mult, op1=ALU.add))
            step(dve.scalar_tensor_tensor(out=xn[:, :, :], in0=total, scalar=sc[:, 2:3], in1=xn[:, :, :], op0=ALU.mult, op1=ALU.add))

            for side, name in ((0, "a_src"), (1, "a_dst")):
                prod = area(5300, R, D)[0:D, :, :]
                step(dve.tensor_tensor(prod, wrel_sb[:, :, :], row[name][0:D, :].rearrange("p (r f) -> p r f", f=D), ALU.mult))
                tally.done(dve.tensor_reduce(wa[:, side, :], prod, AX.X, ALU.add), wa_set)
            norm_relu(1)
            beats1 = Beats(dve, node_vec[1], 3)

            def nodes1(b):
                beats1.group(b)
                stage(1, b, hn).then_inc(staged, 1)
                dve.wait_ge(mixed, 5 + b + 1)
                need(dve, tab_out[1], b * 16)
                scores = product(5 * 512, NB * 2 * R, 2 * R)
                beats1.add(dve.tensor_copy(tb1.rearrange("p j r c -> p (j r) c")[:, :, 0:D], product(0, NB * R * D, D)))
                beats1.add(dve.tensor_copy(tb1[:, :, :, D], scores[:, :, 0:R]))
                beats1.done(dve.tensor_scalar(dn1[:, bass.ds(b * NB, NB), 0:R], scores[:, :, R:2 * R], 1.0, None, ALU.mult))
                dve.tensor_tensor(dn1[:, bass.ds(b * NB, NB), R:2 * R], dn1[:, bass.ds(b * NB, NB), 0:R], scores[:, :, 0:R],
                                  ALU.add).then_inc(taken, 1)
            batches(dve, nodes1)
            dve.wait_ge(taken, 2 * NBATCH)
            loops = dn1[:, :, R:2 * R]
            tally.done(dve.scalar_tensor_tensor(out=loops, in0=loops, scalar=SLOPE, in1=loops, op0=ALU.mult, op1=ALU.max), dn_set)

            dve.wait_ge(ds_in, 16)
            dve.wait_ge(hold_in[1], 16)
            for c in range(2 * R):
                step(dve.tensor_tensor_scan(ds[:, :, c], ns[:, :], ds[:, :, c], dinit1[:, c:c + 1], ALU.mult, ALU.add))
            s_src, ev, dsel, tmp = (score[:, k, :] for k in range(4))
            step(dve.scalar_tensor_tensor(out=dsel, in0=etypef[:, :], scalar=0.0, in1=ds[:, :, 0], op0=ALU.is_equal, op1=ALU.mult))
            for r in range(1, R):
                step(dve.scalar_tensor_tensor(out=tmp, in0=etypef[:, :], scalar=float(r), in1=ds[:, :, r], op0=ALU.is_equal, op1=ALU.mult))
                step(dve.tensor_tensor(dsel, dsel, tmp, ALU.add))

            def take1(i, h, first):
                dve.wait_ge(got["1a"][h], i * 16 * K + 16 * K)
                dve.tensor_scalar(s_src[:, bass.ds((i * 2 + h) * K, K)], g1[:, h, :, D], 1.0, None, ALU.mult).then_inc(taken1, 1)
            passes(dve, take1)
            dve.wait_ge(taken1, NG)
            for h in range(2):
                dve.wait_ge(kept["1a"][h], 16 * LOOPS)

            def over_partitions(use, source, width, op):
                flag = {"sum": nhs_row, "max": hneg_row, "back": nhl_row}[op]
                neutral = -BIG if op == "max" else 0.0
                ops = (ALU.add, ALU.max) if op == "max" else (ALU.mult, ALU.add)
                back = op == "back"
                assert back == (use in BACKWARD)
                dve.sem_inc(c_tail, 1)
                step(dve.memset(cT[:, P:P + 1] if back else cT[:, 0:1], neutral))
                dve.wait_ge(c_turn, use + 1)
                rows, flag = bank(0)[0:width, 0:P], flag[0:width, :]
                if back:
                    step(dve.tensor_tensor_scan(cT[0:width, 0:P][:, ::-1], flag[:, ::-1], rows[:, ::-1], neutral, *ops))
                else:
                    step(dve.tensor_tensor_scan(cT[0:width, 1:P + 1], flag, rows, neutral, *ops))
                dve.sem_inc(c_scan, 1)
                dve.wait_ge(c_back, use + 1)
                step(dve.tensor_copy(cin[:, 0:width], bank(1)[:, 0:width]))
                dve.sem_inc(c_in, 1)

            def segment_totals(use, values, totals, n, op):
                marks, neutral = (neg, -BIG) if op == "max" else (ns, 0.0)
                ops = (ALU.add, ALU.max) if op == "max" else (ALU.mult, ALU.add)
                for r in range(n):
                    step(dve.tensor_tensor_scan(totals[:, r, :], marks[:, :], values[:, r, :], neutral, *ops))
                step(dve.tensor_copy(tails[:, 0:n], totals[:, :, T - 1]))
                over_partitions(use, tails, n, op)
                for r in range(n):
                    step(dve.tensor_tensor_scan(totals[:, r, :], marks[:, :], values[:, r, :], cin[:, r:r + 1], *ops))
                step(dve.tensor_tensor(totals, totals, spread(last[:, :].unsqueeze(1), P, n, T), ALU.mult))
                for r in range(n):
                    step(dve.tensor_tensor(back_tmp, totals[:, r, :], first_last[:, :], ALU.mult))
                    step(dve.tensor_reduce(heads[:, r:r + 1], back_tmp, AX.X, ALU.add))
                over_partitions(use + 1, heads, n, "back")
                for r in range(n):
                    step(dve.tensor_tensor_scan(totals[:, r, ::-1], nl[:, ::-1], totals[:, r, ::-1], cin[:, r:r + 1], ALU.mult, ALU.add))

            back_tmp = tmp
            step(dve.tensor_tensor(ev, s_src, dsel, ALU.add))
            step(dve.scalar_tensor_tensor(out=ev, in0=ev, scalar=SLOPE, in1=ev, op0=ALU.mult, op1=ALU.max))
            for r in range(R):
                step(dve.scalar_tensor_tensor(out=v1[:, r, :], in0=etypef[:, :], scalar=float(r), in1=ev, op0=ALU.is_equal, op1=ALU.mult))
                step(dve.tensor_scalar(tmp, etypef[:, :], float(r), -BIG, ALU.not_equal, ALU.mult))
                step(dve.tensor_tensor(v1[:, r, :], v1[:, r, :], tmp, ALU.add))
            segment_totals(0, v1, f1, R, "max")
            loop_of_edge = ds[:, :, R:2 * R].rearrange("p t r -> p r t")
            step(dve.tensor_tensor(f1, f1, loop_of_edge, ALU.max))
            step(dve.tensor_tensor(v1, v1, f1, ALU.subtract))
            step(dve.tensor_tensor(loop_of_edge, loop_of_edge, f1, ALU.subtract))
            dve.sem_inc(soft_in, 1)
            dve.wait_ge(soft_exp, 2)
            segment_totals(2, v1, f1, R, "sum")
            step(dve.tensor_tensor(f1, f1, loop_of_edge, ALU.add))
            step(dve.reciprocal(f1, f1))
            step(dve.tensor_tensor(v1, v1, f1, ALU.mult))
            alpha1 = s_src
            step(dve.tensor_reduce(alpha1, v1.rearrange("p r t -> p t r"), AX.X, ALU.add))
            tally.done(dve.tensor_tensor(betae, ds[:, :, R:2 * R], f1.rearrange("p r t -> p t r"), ALU.mult), beta_set)

            dve.wait_ge(beta_out, 16)
            beats1c = Beats(dve, work1c, 1 + K)

            def edges1(i, h, first):
                g = i * 2 + h
                beats1c.group(g)
                dve.wait_ge(rows_in["1c"][h], i * 16 + 16)
                dve.wait_ge(ring_in["1c"][h], i * 16 + 16)
                beats1c.wait()
                beats1c.add(dve.tensor_tensor(y1, gc1[:, h, :, 0:D], spread(alpha1[:, bass.ds(g * K, K)].unsqueeze(2), P, K, D), ALU.mult))
                if not first:
                    dve.wait_ge(kept["1c"][h], i * 16)
                segment_sum(beats1c, st1, y1, h, zero[:, 0:D] if first and h == 0 else st1[:, 1 - h, K - 1, :])
            passes(dve, edges1)
            dve.wait_ge(work1c, NG * (1 + K))
            over_partitions(4, st1, D, "sum")
            dve.sem_inc(end1, 1)
            for r in range(R):
                step(dve.tensor_tensor(row["b_self"], row["b_self"], row["bias_rel"][:, r * D:(r + 1) * D], ALU.add))
            dve.wait_ge(agg_in[1], 16 * 3 * NT)
            beats1n = Beats(dve, node_vec[2], 4)

            def nodes1b(b):
                beats1n.group(b)
                stage(2, b, hn).then_inc(staged, 1)
                dve.wait_ge(mixed, 10 + b + 1)
                beats1n.done(dve.tensor_tensor(prod1, bank(0, 5).rearrange("p (j r c) -> p j r c", r=R, c=D),
                                               spread(beta_n[:, bass.ds(b * NB, NB), :].unsqueeze(3), P, NB, R, D), ALU.mult))
                beats1n.done(dve.tensor_reduce(red1, prod1.rearrange("p j r c -> p j c r"), AX.X, ALU.add))
                beats1n.done(dve.tensor_tensor(red1, red1, product(5 * 512, NB * D, D), ALU.add))
                beats1n.done(dve.tensor_tensor(red1, red1, spread(row["b_self"].unsqueeze(1), P, NB, D), ALU.add))
                dve.tensor_tensor(xn[:, bass.ds(b * NB, NB), :], xn[:, bass.ds(b * NB, NB), :], red1, ALU.add).then_inc(taken, 1)
            batches(dve, nodes1b)
            dve.wait_ge(taken, 3 * NBATCH)
            step(dve.tensor_tensor(agg[:, :, :], agg[:, :, :], cg, ALU.add))
            step(dve.tensor_tensor(xn[:, :, :], xn[:, :, :], agg[:, :, :], ALU.add))

            norm_relu(2)
            beats2t = Beats(dve, node_vec[3], 2)

            def nodes2(b):
                beats2t.group(b)
                stage(3, b, hn).then_inc(staged, 1)
                dve.wait_ge(mixed, 15 + b + 1)
                need(dve, tab_out[2], b * 16)
                halves = product(0, NB * 2 * HID, 2 * HID)
                beats2t.add(dve.tensor_copy(tb2[:, :, 0:HID], halves[:, :, 0:HID]))
                beats2t.add(dve.tensor_scalar(tb2[:, :, HID:W2], hn[:, bass.ds(b * NB, NB), :], 1.0, None, ALU.mult))
                beats2t.wait()
                dve.tensor_tensor(bn_rows[:, bass.ds(b * NB, NB), :], halves[:, :, HID:2 * HID], spread(row["be1"].unsqueeze(1), P, NB, HID),
                                  ALU.add).then_inc(taken, 1)
            batches(dve, nodes2)
            dve.wait_ge(taken, 4 * NBATCH)

            dve.wait_ge(hold_in[2], 16)
            fills2, beats2, scans2 = Beats(dve, filled2, K + 1), Beats(dve, work2, 4), Beats(dve, scan2, 2 * K)

            def edges2(i, h, first):
                g = i * 2 + h
                fills2.group(g)
                beats2.group(g)
                scans2.group(g)
                dve.wait_ge(ring_in["2"][h], i * 16 + 16)
                dve.wait_ge(rows_in["2"][h], i * 16 + 16)
                fill(fills2, z2, hold2, h)
                dve.wait_ge(got["2"][h], i * 16 * K + 16 * K)
                beats2.done(dve.tensor_tensor(zs2, g2[:, h, :, 0:HID], z2[:, h, :, :], ALU.add))
                beats2.done(dve.scalar_tensor_tensor(out=pr2, in0=zs2, scalar=0.0, in1=spread(row["we2"].unsqueeze(1), P, K, HID),
                                                     op0=ALU.max, op1=ALU.mult))
                beats2.done(dve.tensor_reduce(e2[:, h, :], pr2, AX.X, ALU.add))
                dve.wait_ge(gate2, g + 1)
                beats2.done(dve.tensor_tensor(m2[:, h, :, :], g2[:, h, :, HID:W2], spread(e2[:, 2 + h, :].unsqueeze(2), P, K, D), ALU.mult))
                if not first:
                    dve.wait_ge(kept["2"][h], i * 16)
                for k in range(K):
                    start = first and h == 0 and k == 0
                    prior = st2[:, h, k - 1, :] if k else st2[:, 1 - h, K - 1, :]
                    scans2.wait(1 if k else 0)
                    scans2.add(dve.scalar_tensor_tensor(out=st2[:, h, k, 0:D], in0=zero[:, 0:D] if start else prior[:, 0:D],
                                                        scalar=ringf[:, h, M_NS + k:M_NS + k + 1], in1=m2[:, h, k, :],
                                                        op0=ALU.mult, op1=ALU.add))
                    scans2.wait(1)
                    scans2.add(dve.scalar_tensor_tensor(out=st2[:, h, k, D:2 * D], in0=lowest[:, :] if start else prior[:, D:2 * D],
                                                        scalar=ringf[:, h, M_NEG + k:M_NEG + k + 1], in1=m2[:, h, k, :],
                                                        op0=ALU.add, op1=ALU.max))
            passes(dve, edges2)
            dve.wait_ge(scan2, NG * 2 * K)
            dve.sem_inc(c_tail, 1)
            step(dve.memset(cT[0:D, 0:1], 0.0))
            step(dve.memset(cT[D:2 * D, 0:1], -BIG))
            dve.wait_ge(c_turn, 6)
            step(dve.tensor_tensor_scan(cT[0:D, 1:P + 1], nhs_row[0:D, :], bank(0)[0:D, 0:P], 0.0, ALU.mult, ALU.add))
            step(dve.tensor_tensor_scan(cT[D:2 * D, 1:P + 1], hneg_row[D:2 * D, :], bank(0)[D:2 * D, 0:P], -BIG, ALU.add, ALU.max))
            dve.sem_inc(c_scan, 1)
            dve.wait_ge(c_back, 6)
            step(dve.tensor_copy(cin[:, :], bank(1)[:, 0:2 * D]))
            dve.sem_inc(c_in, 1)
            dve.sem_inc(end2, 1)
            dve.wait_ge(agg_in[2], 16 * 2 * NT)
            step(dve.tensor_tensor(agg2[:, :, 0:D], agg2[:, :, 0:D], cg2[:, :, 0:D], ALU.add))
            step(dve.tensor_tensor(agg2[:, :, D:2 * D], agg2[:, :, D:2 * D], cg2[:, :, D:2 * D], ALU.max))
            step(dve.tensor_tensor(xn[:, :, :], xn[:, :, :], hn[:, :, :], ALU.add))
            beats2n = Beats(dve, node_vec[4], 2)

            def nodes2b(b):
                beats2n.group(b)
                beats2n.done(stage(4, b, hn))
                need(dve, turned_m, b)
                dve.tensor_scalar(mst2, agg2[:, bass.ds(b * NB, NB), :], 1.0, None, ALU.mult).then_inc(staged, 1)
                dve.wait_ge(mixed, 20 + b + 1)
                red = area(9000, NB, D)
                beats2n.done(dve.tensor_tensor(red, bank(2)[:, 0:NB * D].rearrange("p (j c) -> p j c", c=D),
                                               spread(row["bn2"].unsqueeze(1), P, NB, D), ALU.add))
                dve.tensor_tensor(xn[:, bass.ds(b * NB, NB), :], xn[:, bass.ds(b * NB, NB), :], red, ALU.add).then_inc(taken, 1)
            batches(dve, nodes2b)
            dve.wait_ge(taken, 5 * NBATCH)

            norm_relu(3)
            step(dve.tensor_scalar(rowb[:, 0:HD], row["att"], 1.0 - SLOPE, None, ALU.mult))
            att_relu = rowb[:, 0:HD]
            step(dve.tensor_scalar(row["att"], row["att"], SLOPE, None, ALU.mult))
            lin, xs = area(8000, NB, HD), area(9300, NB, W3)
            beats3t = Beats(dve, node_vec[5], 6)

            def nodes3(b):
                beats3t.group(b)
                stage(5, b, hn).then_inc(staged, 1)
                dve.wait_ge(mixed, 25 + b + 1)
                need(dve, tab_out[3], b * 16)
                sides = product(0, NB * 2 * HD, 2 * HD)
                beats3t.wait()
                need(dve, taken, 25 + b)
                for side, rows, name in ((0, tb3, "b_l"), (1, xs, "b_r")):
                    beats3t.done(dve.tensor_tensor(rows[:, :, 0:HD], sides[:, :, side * HD:(side + 1) * HD],
                                                   spread(row[name].unsqueeze(1), P, NB, HD), ALU.add))
                    beats3t.done(dve.tensor_tensor(lin, rows[:, :, 0:HD], spread(row["att"].unsqueeze(1), P, NB, HD), ALU.mult))
                    beats3t.done(dve.tensor_reduce(rows[:, :, HD:W3], lin.rearrange("p j (h c) -> p j h c", c=D), AX.X, ALU.add))
                dve.tensor_scalar(xr_rows[:, bass.ds(b * NB, NB), :], xs, 1.0, None, ALU.mult).then_inc(taken, 1)
            batches(dve, nodes3)
            dve.wait_ge(taken, 6 * NBATCH)

            dve.wait_ge(hold_in[3], 16)
            fills3, beats3 = Beats(dve, filled3, K + 1), Beats(dve, work3, 4)

            def edges3(i, h, first):
                g = i * 2 + h
                fills3.group(g)
                beats3.group(g)
                dve.wait_ge(ring_in["3a"][h], i * 16 + 16)
                dve.wait_ge(rows_in["3a"][h], i * 16 + 16)
                fill(fills3, z3, hold3, h)
                dve.wait_ge(got["3a"][h], i * 16 * K + 16 * K)
                beats3.done(dve.tensor_tensor(zs3, g3[:, h, :, :], z3[:, h, :, :], ALU.add))
                beats3.done(dve.scalar_tensor_tensor(out=pr3, in0=zs3[:, :, 0:HD], scalar=0.0, in1=spread(att_relu.unsqueeze(1), P, K, HD),
                                                     op0=ALU.max, op1=ALU.mult))
                beats3.done(dve.tensor_reduce(rs3, pr3.rearrange("p k (h c) -> p k h c", c=D), AX.X, ALU.add))
                beats3.done(dve.tensor_tensor(score[:, :, bass.ds(g * K, K)].rearrange("p h k -> p k h"), rs3, zs3[:, :, HD:W3], ALU.add))
            passes(dve, edges3)
            for h in range(2):
                dve.wait_ge(kept["3a"][h], 16 * LOOPS)

            back_tmp = area(3200, T)
            segment_totals(6, score[:, :, :], f3, H, "max")
            step(dve.tensor_tensor(score[:, :, :], score[:, :, :], f3, ALU.subtract))
            dve.sem_inc(soft_in, 1)
            dve.wait_ge(soft_exp, 3)
            segment_totals(8, score[:, :, :], f3, H, "sum")
            step(dve.tensor_scalar(f3, f3, 1e-16, None, ALU.max))
            step(dve.reciprocal(f3, f3))
            step(dve.tensor_tensor(score[:, :, :], score[:, :, :], f3, ALU.mult))
            dve.sem_inc(end3, 1)
            beats3c = Beats(dve, work3c, 2 + K)

            def edges3c(i, h, first):
                g = i * 2 + h
                beats3c.group(g)
                dve.wait_ge(rows_in["3c"][h], i * 16 + 16)
                dve.wait_ge(ring_in["3c"][h], i * 16 + 16)
                beats3c.wait()
                weights = score[:, :, bass.ds(g * K, K)].rearrange("p h k -> p k h")
                beats3c.done(dve.tensor_tensor(y3.rearrange("p k (h c) -> p k h c", c=D),
                                               gc3[:, h, :, 0:HD].rearrange("p k (h c) -> p k h c", c=D),
                                               spread(weights.unsqueeze(3), P, K, H, D), ALU.mult))
                beats3c.add(dve.tensor_reduce(ys3, y3.rearrange("p k (h c) -> p k c h", c=D), AX.X, ALU.add))
                if not first:
                    dve.wait_ge(kept["3c"][h], i * 16)
                segment_sum(beats3c, st3, ys3, h, zero[:, 0:D] if first and h == 0 else st3[:, 1 - h, K - 1, :])
            passes(dve, edges3c)
            dve.wait_ge(work3c, NG * (2 + K))
            over_partitions(10, st3, D, "sum")
            dve.sem_inc(end3, 1)
            dve.wait_ge(agg_in[3], 16 * 2 * NT)
            step(dve.tensor_tensor(agg[:, :, :], agg[:, :, :], cg, ALU.add))
            step(dve.scalar_tensor_tensor(out=agg[:, :, :], in0=agg[:, :, :], scalar=1.0 / H, in1=hn[:, :, :], op0=ALU.mult, op1=ALU.add))
            step(dve.tensor_tensor(agg[:, :, :], agg[:, :, :], spread(row["bias_gat"].unsqueeze(1), P, NT, D), ALU.add))

            def batch_norm(n, gamma, beta):
                col = [bnv[:, k, :] for k in range(6)]

                def over_nodes(rows, use):
                    step(dve.tensor_reduce(col[0], rows.rearrange("p i c -> p c i"), AX.X, ALU.add))
                    dve.sem_inc(bn_in, 1)
                    dve.wait_ge(bn_sum, use + 1)
                over_nodes(agg[:, :, :], 2 * n)
                step(dve.tensor_scalar(col[1], bank(0)[:, 0:D], 1.0 / N, None, ALU.mult))
                step(dve.tensor_tensor(agg[:, :, :], agg[:, :, :], spread(col[1].unsqueeze(1), P, NT, D), ALU.subtract))
                step(dve.tensor_tensor(cg, agg[:, :, :], agg[:, :, :], ALU.mult))
                over_nodes(cg, 2 * n + 1)
                step(dve.tensor_scalar(col[2], bank(0)[:, 0:D], 1.0 / N, EPS, ALU.mult, ALU.add))
                dve.sem_inc(bn_var, 1)
                dve.wait_ge(bn_std, n + 1)
                step(dve.reciprocal(col[4], col[3]))
                step(dve.tensor_tensor(col[4], col[4], row[gamma], ALU.mult))
                step(dve.tensor_tensor(agg[:, :, :], agg[:, :, :], spread(col[4].unsqueeze(1), P, NT, D), ALU.mult))
                step(dve.tensor_tensor(agg[:, :, :], agg[:, :, :], spread(row[beta].unsqueeze(1), P, NT, D), ALU.add))
            batch_norm(0, "gamma1", "beta1")
            beats3n = Beats(dve, node_vec[6], 1)

            def nodes3b(b):
                beats3n.group(b)
                stage(6, b, agg).then_inc(staged, 1)
                dve.wait_ge(mixed, 30 + b + 1)
                beats3n.done(dve.tensor_tensor(red3, bank(4)[:, 0:NB * D].rearrange("p (j c) -> p j c", c=D),
                                               spread(row["b_f2"].unsqueeze(1), P, NB, D), ALU.add))
                dve.tensor_tensor(agg[:, bass.ds(b * NB, NB), :], agg[:, bass.ds(b * NB, NB), :], red3, ALU.add).then_inc(taken, 1)
            batches(dve, nodes3b)
            dve.wait_ge(taken, 7 * NBATCH)
            batch_norm(1, "gamma2", "beta2")
            tally.done(dve.tensor_tensor(xn[:, :, :], xn[:, :, :], agg[:, :, :], ALU.add), result_set)


_INS = ["x", "src", "dst", "edge_type_8", "edge_weight", "edge_weight_n2", "L0_gnn_W", "L0_gnn_b", "L0_gnn_deg_coeff",
        "L0_gnn_coeff_param", "L0_gnn_scale_param", "L1_gnn_W_self", "L1_gnn_b_self", "L1_gnn_W", "L1_gnn_att_src",
        "L1_gnn_att_dst", "L1_gnn_bias", "L2_gnn_We1", "L2_gnn_be1", "L2_gnn_We2", "L2_gnn_be2", "L2_gnn_Wn1", "L2_gnn_bn1",
        "L2_gnn_Wn2", "L2_gnn_bn2", "L3_gnn_W_l", "L3_gnn_b_l", "L3_gnn_W_r", "L3_gnn_b_r", "L3_gnn_att", "L3_gnn_bias_gat",
        "L3_gnn_gamma1", "L3_gnn_beta1", "L3_gnn_W1", "L3_gnn_b1", "L3_gnn_W2", "L3_gnn_b2", "L3_gnn_gamma2", "L3_gnn_beta2"]


def kernel(**inputs):
    import numpy as np
    import concourse.bacc as bacc
    from concourse.bass_utils import run_bass_kernel_spmd

    nc = bacc.Bacc("TRN2", target_bir_lowering=False, num_devices=1)
    arrays, args = {}, []
    for name in _INS:
        array = np.ascontiguousarray(inputs[name])
        arrays[f"in_{name}_dram"] = array
        args.append(nc.dram_tensor(f"in_{name}_dram", array.shape, mybir.dt.from_np(array.dtype), kind="ExternalInput").ap())
    args.append(nc.dram_tensor("out_0_dram", (N, D), F32, kind="ExternalOutput").ap())
    gnn_program(nc, *args)
    result = run_bass_kernel_spmd(nc, [arrays], core_ids=[0])
    return result.results[0]["out_0_dram"]
```

```python
from contextlib import ExitStack

import concourse.bass as bass
from concourse import mybir

ALU = mybir.AluOpType
ACT = mybir.ActivationFunctionType
AX = mybir.AxisListType
F32 = mybir.dt.float32
I32 = mybir.dt.int32
BF16 = mybir.dt.bfloat16

P = 128
N = 3125
NT = 25
NP = P * NT
NV = N // NT
E = 100000
K = 8
T = 784
EP = P * T
EL = E - (P - 1) * T
NG = T // K
LOOPS = NG // 2
D = 64
R = 8
H = 4
HD = H * D
HID = 128
FF = 256
NB = 5
NBATCH = NT // NB
BC = NB * P
BIG = 1.0e30
ROUND = 12582912.0
EPS = 1e-5
W = 7 * K
GW, NW = W // K, T // W
TILES = NT + 1
ROWS = TILES * P
CELLS = ROWS * NP
W1 = D + 1
W2 = HID + D
W3 = HD + H
SLOPE = 0.2

M_SRC, M_REL, M_W = 0, K, 2 * K
KD = 5
AREA = 27800


class Tally:

    def __init__(self, engine):
        self.engine, self.count = engine, {}

    def done(self, instruction, semaphore):
        self.count[semaphore.name] = self.count.get(semaphore.name, 0) + 1
        instruction.then_inc(semaphore, 1)
        self.engine.wait_ge(semaphore, self.count[semaphore.name])


class Beats:

    def __init__(self, engine, semaphore, each):
        self.engine, self.semaphore, self.each, self.g, self.k = engine, semaphore, each, 0, each

    def group(self, g):
        assert self.k == self.each, (self.semaphore.name, self.k)
        self.g, self.k = g, 0

    def add(self, instruction):
        instruction.then_inc(self.semaphore, 1)
        self.k += 1

    def wait(self, back=0):
        value = self.g * self.each + (self.k - back)
        if not isinstance(value, int) or value > 0:
            self.engine.wait_ge(self.semaphore, value)

    def done(self, instruction):
        self.add(instruction)
        self.wait()


def passes(engine, body):
    for h in range(2):
        body(0, h, True)
    with engine.Fori(1, LOOPS) as i:
        for h in range(2):
            body(i, h, False)


def quads(engine, body):
    for g in range(6):
        body(g, g % 4, (g // 4, g // 2))
    with engine.Fori(0, (NG - 6) // 4) as i:
        for u in range(4):
            body(i * 4 + (6 + u), (6 + u) % 4, (i + (6 + u) // 4, i * 2 + (6 + u) // 2))


def gnn_program(nc, x, src, dst, etype, adj_v, deg_v, w0, b0, deg_coeff, coeff_param, scale_param,
                w_self, b_self, w_rel, a_src, a_dst, bias_rel, we1, be1, we2, be2, wn1, bn1, wn2, bn2,
                w_l, b_l, w_r, b_r, att, bias_gat, gamma1, beta1, w_f1, b_f1, w_f2, b_f2, gamma2, beta2,
                out):
    with ExitStack() as ctx:
        def sb(name, shape, dt=F32):
            return ctx.enter_context(nc.sbuf_tensor(name, shape, dt))

        def sem(name):
            return ctx.enter_context(nc.semaphore(name))

        def dram(name, shape):
            return nc.dram_tensor(name, shape, F32).ap()

        tab0, tab1 = dram("tab0", [NP, D]), dram("tab1", [NP * R, W1])
        weights0 = dram("weights0", [CELLS + P * W, 1])
        tab2, tab3 = dram("tab2", [NP, W2]), dram("tab3", [NP, W3])
        put1 = dram("put1", [EP + NP, 2 * R])
        put2, put3 = dram("put2", [EP + NP, HID]), dram("put3", [EP + NP, W3])
        rows1, rows2, rows3 = dram("rows1", [NP, 2 * R]), dram("rows2", [NP, HID]), dram("rows3", [NP, W3])
        spill1, spill3 = dram("spill1", [EP, W1]), dram("spill3", [EP, W3])
        state1, state2, state3 = dram("state1", [EP + 1, D]), dram("state2", [EP + 1, 2 * D]), dram("state3", [EP + 1, D])
        betas = dram("betas", [EP + 1, R])
        carry1, carry2, carry3 = dram("carry1", [P + 1, D]), dram("carry2", [P + 1, 2 * D]), dram("carry3", [P + 1, D])

        meta = sb("meta", [P, NG, M_W], I32)
        ring = sb("ring", [P, GW, M_W], I32)
        ringf = ring[:, :, :].bitcast(F32)
        base_sb = sb("base", [P, NP // 4])
        base = base_sb[:, 0:T]
        etypef = sb("etypef", [P, T])
        ns = sb("ns", [P, T])
        neg = sb("neg", [P, T])
        nl = sb("nl", [P, T])
        last = sb("last", [P, T])
        first_last = sb("first_last", [P, T])
        score_sb = sb("score", [P, NP])
        score = score_sb[:, 0:H * T].rearrange("p (h t) -> p h t", t=T)
        dst0 = sb("dst0", [P, 1], I32)
        zidx, eidx, cidx = sb("zidx", [P, NT], I32), sb("eidx", [P, NT], I32), sb("cidx", [P, NT], I32)
        nodev = sb("nodev", [P, 8, NT])
        xn, hn, agg = (sb(n, [P, NT, D]) for n in ("xn", "hn", "agg"))
        lnv = sb("lnv", [P, 4, NT])
        wh_own = sb("wh_own", [P, 4, D])
        per_dst, rnv = sb("per_dst", [P, TILES]), sb("rnv", [P, 2])
        hst = sb("hst", [P, NB, D])
        hT = sb("hT", [D, NB, P])
        ident, lower, upper, ones, valid = (sb(n, [P, P]) for n in ("ident", "lower", "upper", "ones", "valid"))
        zero = sb("zero", [P, K * W3 // 2])
        iota_row = sb("iota_row", [P, P])
        piece_row = sb("piece_row", [P, 1])
        trash = sb("trash", [P, W])
        node_trash = sb("node_trash", [P, NT])
        nhs_row, hneg_row, nhl_row = sb("nhs_row", [P, P]), sb("hneg_row", [P, P]), sb("nhl_row", [P, P])
        flags = sb("flags", [P, 2])
        tails, heads, cin = sb("tails", [P, R]), sb("heads", [P, R]), sb("cin", [P, P])
        cT = sb("cT", [P, P + 2])
        par = sb("par", [P, 16])
        sc = sb("sc", [P, 16])
        w0_sb, wself_sb, wrel_sb = sb("w0_sb", [D, 2, D]), sb("wself_sb", [D, D]), sb("wrel_sb", [D, R, D])
        we1_sb = sb("we1_sb", [D, 2, HID])
        wn1m_sb, wn1h_sb, wn2_sb = sb("wn1m_sb", [2 * D, HID]), sb("wn1h_sb", [D, HID]), sb("wn2_sb", [HID, D])
        wlr_sb = sb("wlr_sb", [D, 2, HD])
        wf1_sb, wf2_sb = sb("wf1_sb", [D, FF]), sb("wf2_sb", [P, 2, D])
        rowb = sb("rowb", [P, 3520])
        colb = sb("colb", [P, 4])
        wa = sb("wa", [D, 2, R])
        lowest = sb("lowest", [P, D])
        arena = sb("arena", [P, AREA])
        psum = ctx.enter_context(nc.psum_tensor("psum", [P, 8, 512], F32))

        def area(at, *shape):
            n = 1
            for s in shape:
                n *= s
            assert at + n <= AREA
            v = arena[:, at:at + n]
            if len(shape) == 2:
                v = v.rearrange("p (a b) -> p a b", b=shape[1])
            if len(shape) == 3:
                v = v.rearrange("p (a b c) -> p a b c", b=shape[1], c=shape[2])
            return v

        def pair(at, width):
            return area(at, 2 * K, width).rearrange("p (s k) c -> p s k c", k=K)

        def quad(at, width):
            return area(at, 4 * K, width).rearrange("p (s k) c -> p s k c", k=K)

        def bank(b, n=1):
            return psum[:, b:b + n, :].rearrange("p a b -> p (a b)")

        names = [("b0", D, b0), ("b_self", D, b_self), ("bias_rel", R * D, bias_rel), ("be1", HID, be1),
                 ("we2", HID, we2), ("bn2", D, bn2), ("b_l", HD, b_l), ("b_r", HD, b_r), ("att", HD, att),
                 ("bias_gat", D, bias_gat), ("gamma1", D, gamma1), ("beta1", D, beta1), ("gamma2", D, gamma2),
                 ("beta2", D, beta2), ("b_f2", D, b_f2), ("a_src", R * D, a_src), ("a_dst", R * D, a_dst)]
        row, row_loads, at = {}, [], 0
        for name, width, source in names:
            row[name] = rowb[:, at:at + width]
            row_loads.append((row[name], source.flatten() if len(source.shape) > 1 else source))
            at += width
        assert at <= 3520

        def over(ap, *shape):
            return ap.to_broadcast(list(shape))

        dext = area(0, T + 2)
        ints = arena[:, 800:800 + T + 2].bitcast(I32)
        srci = arena[:, 1600:1600 + T].bitcast(I32)
        typei = arena[:, 2400:2400 + T].bitcast(I32)
        adj_sb, deg_sb = area(3200, T), area(4000, T)
        tmpa, tmpb, srcf = area(4800, T), area(5600, T + 1), area(6400, T)
        pn, im = area(7200, T), area(8000, T)
        hot_p = arena[:, 8800:8800 + 2 * K * P // 2].bitcast(BF16).rearrange("p (a c) -> p a c", c=P)
        hot_i = arena[:, 9900:9900 + 2 * K * NT // 2].bitcast(BF16).rearrange("p (a c) -> p a c", c=NT)
        words0 = arena[:, 10200:10200 + NG * 2 * K].bitcast(I32).rearrange("p (g w) -> p g w", w=2 * K)
        words0f = area(10200, NG, 2 * K)
        key = area(11800, T)
        alike, alike_by = area(12800, W, W), area(16000, W, W)
        earlier = area(19328, W, W)
        merged0 = area(24460, 4, W)
        cells, per_src, whT = area(0, 4, NP), area(12800, NP), area(16000, TILES, P)

        def halves(at, n=TILES):
            return arena[:, at:at + n * P // 2].bitcast(BF16).rearrange("p (j n) -> p j n", n=P)
        high, middle, low = halves(0), halves(TILES * P // 2), halves(24460)
        high_middle, middle_high, low_high = halves(16000), halves(16000 + TILES * P // 2), halves(24460 + TILES * P // 2)
        signed = area(19328, 4, NP // 4).rearrange("p (a b) c -> p a b c", b=2)
        squares = area(19328, NP)[0:D, :]
        wh = area(22528, TILES, D)
        wh_lhs = arena[:, 24192:24192 + 2 * P].bitcast(BF16).rearrange("p (s a n) -> p s a n", a=2, n=P)
        parts0 = [hn[:, :, :].rearrange("p i c -> p (i c)")[:, 0:NP // 4], hn[:, :, :].rearrange("p i c -> p (i c)")[:, NP // 4:NP // 2],
                  base_sb[:, :]]
        per_pair = score_sb[:, :]
        total0 = agg[:, :, :].rearrange("p i c -> p (i c)")
        hst_parts = hst[:, :, :].rearrange("p j c -> p (j c)").bitcast(BF16).rearrange("p (a n) -> p a n", n=P)
        g1, ds = area(0, 2, K, W1), area(12600, T, 2 * R)
        alpha1 = score[:, 0, :]
        v1, f1 = area(0, R, T), area(6300, R, T)
        betae = area(0, T, R)
        tb1 = area(0, NB, R * W1).rearrange("p j (r c) -> p j r c", c=W1)
        dn1 = area(3000, NT, 2 * R)
        dinit1 = area(3500, 2 * R)
        gc1, y1, st1 = quad(0, W1), quad(2200, D), pair(4300, D)
        cg = area(0, NT, D)
        beta_n = area(5500, NT, R)
        prod1 = area(2000, NB * R, D).rearrange("p (j r) c -> p j r c", r=R)
        red1 = area(4700, NB, D)
        tb2 = area(0, NB, W2)
        bn_rows = area(1000, NT, HID)
        g2, z2, hold2 = quad(0, W2), quad(6200, HID), area(10300, HID)
        pr2, e2, m2, st2 = area(10500, K, HID), area(11600, 4, K), pair(11700, D), pair(12800, 2 * D)
        agg2, cg2 = area(0, NT, 2 * D), area(3300, NT, 2 * D)
        mst2, mT2, hidT2 = area(6600, NB, 2 * D), area(7300, BC), area(8000, BC)
        tb3 = area(0, NB, W3)
        xr_rows = area(1400, NT, W3)
        g3, z3, hold3 = quad(0, W3), quad(8400, W3), area(16800, W3)
        pr3, rs3, zl3 = area(17100, K, HD), area(19200, K, H), area(19300, K, H)
        f3 = area(0, H, T)
        gc3, y3, st3 = quad(0, W3), pair(8400, HD), pair(12600, D)
        hid3 = area(1700, 2, BC)
        red3 = area(3100, NB, D)
        bnv = area(3500, 6, D)

        x_in, edges_in, params_in = sem("x_in"), sem("edges_in"), sem("params_in")
        zero0_out, zero_out, zero3_out = sem("zero0_out"), sem("zero_out"), sem("zero3_out")
        tab_out = sem("tab_out")
        rows_out = sem("rows_out")
        put_out = sem("put_out")
        hold_in = sem("hold_in")
        ring_in = {n: [sem(f"ring_in{n}_{h}") for h in range(w)] for n, w in (("0", GW), ("1a", 2), ("2", 4), ("3a", 4))}
        loaded = [sem(f"loaded{s}") for s in range(4)]
        rows_in = {n: [sem(f"rows_in{n}_{h}") for h in range(w)] for n, w in (("2", 4), ("3a", 4))}
        got = {n: [sem(f"got{n}_{h}") for h in range(w)] for n, w in (("1a", 2), ("2", 4), ("3a", 4))}
        kept = {n: [sem(f"kept{n}_{h}") for h in range(w)] for n, w in (("1a", 2), ("3a", 4))}
        states_out = [sem(f"states_out{h}") for h in range(2)]
        added = [sem(f"added{u}") for u in range(GW)]
        cells_in = [sem(f"cells_in{s}") for s in range(4)]
        ds_in, beta_out = sem("ds_in"), sem("beta_out")
        carry_out = sem("carry_out")
        agg_in = sem("agg_in")
        result_out = sem("result_out")
        padded, zeroed, consts = sem("padded"), sem("zeroed"), sem("consts")
        vec, turns = sem("vec"), sem("turns")
        plus_in, plus_exp, plus_ln = (sem(n) for n in ("plus_in", "plus_exp", "plus_ln"))
        hot, counted, tallied, indices = (sem(n) for n in ("hot", "counted", "tallied", "indices"))
        to_spread, spread_up = sem("to_spread"), sem("spread_up")
        ln_var, ln_std = sem("ln_var"), sem("ln_std")
        staged, turned, lifted, mixed, taken = (sem(n) for n in ("staged", "turned", "lifted", "mixed", "taken"))
        hidden, hidden_up, lifted_m, turned_m = sem("hidden"), sem("hidden_up"), sem("lifted_m"), sem("turned_m")
        flags_read = sem("flags_read")
        BACKWARD = (1, 3, 7, 9)
        node_vec = {n: sem(f"node_vec{n}") for n in range(1, 7)}
        norm_in, norm_out = sem("norm_in"), sem("norm_out")
        wa_set = sem("wa_set")
        merging, apart, squared, norms_up, piece_up, piece_turned, piece_set, sums_turned = (
            sem(n) for n in ("merging", "apart", "squared", "norms_up", "piece_up", "piece_turned", "piece_set", "sums_turned"))
        lhs_set, similar, signs, pairs, weighted, work0, summed0, sums_taken = (
            sem(n) for n in ("lhs_set", "similar", "signs", "pairs", "weighted", "work0", "summed0", "sums_taken"))
        dn_set = sem("dn_set")
        taken1, made1, work1c, weights_set = sem("taken1"), sem("made1"), sem("work1c"), sem("weights_set")
        filled2, summed2, work2, gate2, made2, scan2 = (sem(n) for n in ("filled2", "summed2", "work2", "gate2", "made2", "scan2"))
        filled3, summed3, work3, scored = (sem(n) for n in ("filled3", "summed3", "work3", "scored"))
        made3, made3b, heads3, work3c = sem("made3"), sem("made3b"), sem("heads3"), sem("work3c")
        ended = sem("ended")
        soft_in, soft_exp = sem("soft_in"), sem("soft_exp")
        c_tail, c_turn, c_scan, c_back, c_in = (sem(n) for n in ("c_tail", "c_turn", "c_scan", "c_back", "c_in"))
        bn_in, bn_sum, bn_var, bn_std = (sem(n) for n in ("bn_in", "bn_sum", "bn_var", "bn_std"))
        result_set = sem("result_set")

        ZEROS = 8 + 2 * NW

        def need(engine, semaphore, value):
            if not isinstance(value, int) or value > 0:
                engine.wait_ge(semaphore, value)

        def after(n, s):
            return (NG - s + 3) // 4 if n == 3 else 0

        def tiles(engine, body):
            for j in range(6):
                body(j, j % 4, j // 4)
            with engine.Fori(0, (TILES - 6) // 4) as i:
                for u in range(4):
                    body(i * 4 + (6 + u), (6 + u) % 4, i + (6 + u) // 4)

        def late(j, n):
            return not isinstance(j, int) or j >= n

        def batches(engine, body):
            body(0)
            with engine.Fori(1, NBATCH) as b:
                body(b)

        by_node = "(p i) c -> p i c"
        by_edge = "(p t) c -> p t c"

        def group_rows(table, g):
            return table[0:EP, :].rearrange(by_edge, t=T)[:, bass.ds(g * K, K), :]

        def clear(engine, table, count, width, semaphore):
            engine.dma_start(table.rearrange("p (n w) -> p n w", w=width),
                             over(zero[:, 0:width].unsqueeze(1), P, count, width)).then_inc(semaphore, 16)

        block = ctx.enter_context(nc.Block())

        @block.sync
        def _(sp):
            sp.wait_ge(padded, 7)
            sp.dma_start(ints[0:P - 1, 1:T + 1], dst[0:EP - T].rearrange("(p t) -> p t", t=T)).then_inc(edges_in, 16)
            sp.dma_start(ints[P - 1:P, 1:EL + 1], dst[EP - T:E].unsqueeze(0)).then_inc(edges_in, 16)
            with nc.allow_non_contiguous_dma(reason="one neighbour of each partition's edges"):
                sp.dma_start(ints[1:P, 0:1], dst[T - 1::T].unsqueeze(1)).then_inc(edges_in, 16)
                sp.dma_start(ints[0:P - 1, T + 1:T + 2], dst[T::T].unsqueeze(1)).then_inc(edges_in, 16)
            for tile, array in ((srci, src), (typei, etype), (adj_sb, adj_v), (deg_sb, deg_v)):
                sp.dma_start(tile[0:P - 1, :], array[0:EP - T].rearrange("(p t) -> p t", t=T)).then_inc(edges_in, 16)
                sp.dma_start(tile[P - 1:P, 0:EL], array[EP - T:E].unsqueeze(0)).then_inc(edges_in, 16)
            sp.dma_start(xn[0:NV, :, :], x.rearrange(by_node, i=NT)).then_inc(x_in, 16)
            for tile, array in ((w0_sb[:, 0, :], w0), (w0_sb[:, 1, :], w0), (wself_sb[:, :], w_self), (wn1m_sb[0:D, :], wn1[D:2 * D, :]), (wn1m_sb[D:2 * D, :], wn1[0:D, :]), (wn1h_sb[:, :], wn1[2 * D:, :]),
                                (wn2_sb[:, :], wn2), (wf1_sb[:, :], w_f1)):
                sp.dma_start(tile, array).then_inc(params_in, 16)
            sp.dma_start(wrel_sb[:, :, :], w_rel.rearrange("r d f -> d r f")).then_inc(params_in, 16)
            sp.dma_start(we1_sb[:, :, :], we1.rearrange("(a d) f -> d a f", a=2)).then_inc(params_in, 16)
            sp.dma_start(wf2_sb[:, :, :], w_f2.rearrange("(a d) f -> d a f", a=2)).then_inc(params_in, 16)
            sp.dma_start(wlr_sb[:, 0, :], w_l).then_inc(params_in, 16)
            sp.dma_start(wlr_sb[:, 1, :], w_r).then_inc(params_in, 16)
            for tile, array in row_loads:
                sp.dma_start(tile, array.partition_broadcast(P)).then_inc(params_in, 16)
            for at, array in ((0, deg_coeff), (2, coeff_param), (5, scale_param), (6, be2)):
                sp.dma_start(par[:, at:at + array.shape[0]], array.partition_broadcast(P)).then_inc(params_in, 16)
            with nc.allow_non_contiguous_dma(reason="bias columns"):
                sp.dma_start(colb[:, 0:1], bn1.unsqueeze(1)).then_inc(params_in, 16)
                sp.dma_start(colb[:, 1:3], b_f1.rearrange("(a p) -> p a", a=2)).then_inc(params_in, 16)
                for half in range(2):
                    sp.dma_start(colb[half * D:(half + 1) * D, 3:4], b0.unsqueeze(1)).then_inc(params_in, 16)

            sp.wait_ge(zeroed, 2)
            table = weights0.rearrange("e c -> (e c)")
            clear(sp, table[0:CELLS].rearrange("(p t) -> p t", p=P), CELLS // P // 1040, 1040, zero0_out)
            clear(sp, table[CELLS:].rearrange("(p t) -> p t", p=P), 1, W, zero0_out)

            def ring_load(n, g, s, *used):
                for semaphore, value in used:
                    need(sp, semaphore, value)
                sp.dma_start(ring[:, s, :], meta[:, bass.ds(g, 1), :].rearrange("p a w -> p (a w)")).then_inc(ring_in[n][s], 16)

            def load0(w):
                sp.wait_ge(merging, w * 8 + 8)
                for u in range(GW):
                    if late(w, 1):
                        sp.wait_ge(added[u], w * 16 * K)
                    sp.dma_start(ring[:, u, :], words0[:, bass.ds(w * GW + u, 1), :].rearrange("p a w -> p (a w)")).then_inc(ring_in["0"][u], 16)
            load0(0)
            with sp.Fori(1, NW) as w:
                load0(w)
            for u in range(GW):
                sp.wait_ge(added[u], NW * 16 * K)
            sp.wait_ge(indices, 1)

            def load_cells(j, s, uses):
                if late(j, 4):
                    sp.wait_ge(summed0, j - 3)
                sp.dma_start(cells[:, s, :], weights0[0:CELLS, :].rearrange("(r n) c -> r (n c)", n=NP)[bass.ds(j * P, P), :]
                             ).then_inc(cells_in[s], 16)
            tiles(sp, load_cells)

            def table1(b):
                sp.wait_ge(taken, 5 + b + 1)
                sp.sem_inc(turns, 1)
                sp.dma_start(tab1.rearrange("(p i r) c -> p i r c", i=NT, r=R)[:, bass.ds(b * NB, NB), :, :], tb1).then_inc(tab_out, 16)
            batches(sp, table1)
            sp.wait_ge(dn_set, 1)
            sp.dma_start(rows1.rearrange(by_node, i=NT), dn1).then_inc(rows_out, 16)
            sp.wait_ge(put_out, 16 * 1 * NT)
            sp.dma_start(ds, put1[0:EP, :].rearrange(by_edge, t=T)).then_inc(ds_in, 16)

            def load1a(i, h, first):
                g = i * 2 + h
                ring_load("1a", g, h, *(() if first else ((got["1a"][h], i * 16 * K),)))
            passes(sp, load1a)
            sp.wait_ge(weights_set, 1)
            sp.dma_start(betas[0:EP, :].rearrange(by_edge, t=T), betae).then_inc(beta_out, 16)
            sp.wait_ge(beta_out, 16)

            def load1c(g, s, uses):
                if not isinstance(g, int) or g >= 4:
                    sp.wait_ge(made1, g - 3)
                sp.dma_start(gc1[:, s, :, :], group_rows(spill1, g)).then_inc(loaded[s], 16)
            quads(sp, load1c)

            def carry_store(n, uses, table, width):
                sp.wait_ge(c_in, uses)
                sp.dma_start(table[0:P, :], cin[:, 0:width]).then_inc(carry_out, 16)
            carry_store(1, 5, carry1, D)

            def table2(b):
                sp.wait_ge(taken, 15 + b + 1)
                sp.sem_inc(turns, 1)
                sp.dma_start(tab2.rearrange(by_node, i=NT)[:, bass.ds(b * NB, NB), :], tb2).then_inc(tab_out, 16)
            batches(sp, table2)
            sp.dma_start(rows2.rearrange(by_node, i=NT), bn_rows).then_inc(rows_out, 16)
            sp.wait_ge(put_out, 16 * 2 * NT)
            sp.wait_ge(rows_out, 16 * 2)

            def load_group(n, put_rows, rows, filled_to, summed, g, s, uses):
                again = not isinstance(g, int) or g >= 4
                ring_load(n, g, s, *(((got[n][s], uses[0] * 16 * K),) if again else ()))
                if again:
                    sp.wait_ge(filled_to, (g - 3) * (K + 1))
                    sp.wait_ge(summed, g - 3)
                    if n == "3a":
                        sp.wait_ge(work3, (g - 3) * 5 - 2)
                sp.dma_start(rows[:, s, :, :], group_rows(put_rows, g)).then_inc(rows_in[n][s], 16)
            quads(sp, lambda g, s, uses: load_group("2", put2, z2, filled2, summed2, g, s, uses))
            carry_store(2, 6, carry2, 2 * D)

            def table3(b):
                sp.wait_ge(taken, 25 + b + 1)
                sp.sem_inc(turns, 1)
                sp.dma_start(tab3.rearrange(by_node, i=NT)[:, bass.ds(b * NB, NB), :], tb3).then_inc(tab_out, 16)
            batches(sp, table3)
            sp.dma_start(rows3.rearrange(by_node, i=NT), xr_rows).then_inc(rows_out, 16)
            sp.wait_ge(put_out, 16 * 3 * NT)
            sp.wait_ge(rows_out, 16 * 3)

            quads(sp, lambda g, s, uses: load_group("3a", put3, z3, filled3, summed3, g, s, uses))

            def load3c(g, s, uses):
                if not isinstance(g, int) or g >= 4:
                    sp.wait_ge(made3, (g - 3) * KD)
                    sp.wait_ge(made3b, g - 3)
                sp.dma_start(gc3[:, s, :, :], group_rows(spill3, g)).then_inc(loaded[s], 16)
            sp.wait_ge(ended, 3)
            quads(sp, load3c)
            carry_store(3, 11, carry3, D)
            sp.wait_ge(result_set, 1)
            sp.dma_start(out.rearrange(by_node, i=NT), xn[0:NV, :, :]).then_inc(result_out, 16)
            sp.wait_ge(result_out, 16)

        @block.gpsimd
        def _(pool):
            tally = Tally(pool)
            tally.done(pool.memset(ones[:, :], 1.0), consts)
            tally.done(pool.memset(ident[:, :], 0.0), consts)
            tally.done(pool.affine_select(out=ident[:, :], in_=ident[:, :], compare_op=ALU.not_equal, fill=1.0, base=0,
                                          pattern=[[-1, P]], channel_multiplier=1), consts)
            tally.done(pool.affine_select(out=lower[:, :], in_=ones[:, :], compare_op=ALU.is_gt, fill=0.0, base=0,
                                          pattern=[[-1, P]], channel_multiplier=1), consts)
            tally.done(pool.affine_select(out=upper[:, :], in_=ones[:, :], compare_op=ALU.is_gt, fill=0.0, base=0,
                                          pattern=[[1, P]], channel_multiplier=-1), consts)
            tally.done(pool.affine_select(out=valid[:, :], in_=ones[:, :], compare_op=ALU.is_ge, fill=0.0, base=NV - 1,
                                          pattern=[[0, P]], channel_multiplier=-1), consts)
            tally.done(pool.iota(iota_row[:, :], pattern=[[1, P]], base=0, channel_multiplier=0,
                                 allow_small_or_imprecise_dtypes=True), consts)
            tally.done(pool.iota(piece_row[:, :], pattern=[[1, 1]], base=NP, channel_multiplier=1,
                                 allow_small_or_imprecise_dtypes=True), consts)
            tally.done(pool.iota(trash[:, :], pattern=[[1, W]], base=CELLS, channel_multiplier=W,
                                 allow_small_or_imprecise_dtypes=True), consts)
            tally.done(pool.memset(earlier, 1.0), consts)
            tally.done(pool.affine_select(out=earlier, in_=earlier, compare_op=ALU.is_gt, fill=0.0, base=0,
                                          pattern=[[1, W], [-1, W]], channel_multiplier=0), consts)
            tally.done(pool.iota(node_trash[:, :], pattern=[[1, NT]], base=EP, channel_multiplier=NT,
                                 allow_small_or_imprecise_dtypes=True), consts)

            def ready(*waits):
                for semaphore, value in waits:
                    need(pool, semaphore, value)
                pool.sem_inc(turns, 1)

            def put(n, table, rows):
                for i in range(NT):
                    pool.indirect_dma_start(out=table[:, :], out_offset=bass.IndirectOffsetOnAxis(ap=zidx[:, i:i + 1], axis=0),
                                            in_=rows[:, i, :], in_offset=None).then_inc(put_out, 16)

            def hold(n, table, rows):
                pool.indirect_dma_start(out=rows, out_offset=None, in_=table[:, :],
                                        in_offset=bass.IndirectOffsetOnAxis(ap=dst0[:, :], axis=0)).then_inc(hold_in, 16)

            def gather(n, table, rows, word, h):
                for k in range(K):
                    pool.indirect_dma_start(out=rows[:, h, k, :], out_offset=None, in_=table[:, :],
                                            in_offset=bass.IndirectOffsetOnAxis(ap=ring[:, h, word + k:word + k + 1], axis=0)
                                            ).then_inc(got[n][h], 16)

            def collect(n, table, index, rows):
                for i in range(NT):
                    pool.indirect_dma_start(out=rows[:, i, :], out_offset=None, in_=table[:, :],
                                            in_offset=bass.IndirectOffsetOnAxis(ap=index[:, i:i + 1], axis=0)).then_inc(agg_in, 16)

            def add0(w):
                for u in range(GW):
                    before = [(added[v], w * 16 * K) for v in range(GW)] if u == 0 and late(w, 1) else []
                    ready((ring_in["0"][u], w * 16 + 16), *before)
                    for k in range(K):
                        pool.indirect_dma_start(out=weights0[:, :], out_offset=bass.IndirectOffsetOnAxis(ap=ring[:, u, k:k + 1], axis=0),
                                                in_=ringf[:, u, K + k:K + k + 1], in_offset=None, compute_op=ALU.add).then_inc(added[u], 16)
            pool.wait_ge(zero0_out, 32)
            add0(0)
            with pool.Fori(1, NW) as w:
                add0(w)
            ready((tab_out, 16))
            hold(0, tab0, wh[:, NT, :])

            def weigh(j, s, uses):
                pool.wait_ge(cells_in[s], uses * 16 + 16)
                pool.wait_ge(pairs, j + 1)
                pool.tensor_tensor(cells[:, s, :], cells[:, s, :], per_pair, ALU.mult).then_inc(weighted, 1)
            tiles(pool, weigh)

            ready((dn_set, 1), (zero_out, 16 * ZEROS))
            put(1, put1, dn1)
            ready((rows_out, 16 * 1))
            hold(1, rows1, dinit1)
            ready((tab_out, 16 * (1 + 1 * NBATCH)))

            def gather1(i, h, first):
                g = i * 2 + h
                ready((ring_in["1a"][h], i * 16 + 16), *(() if first else ((taken1, g - 1), (kept["1a"][h], i * 16))))
                gather("1a", tab1, g1, M_REL, h)
            passes(pool, gather1)
            pool.wait_ge(weights_set, 1)

            def messages1(g, s, uses):
                ready((loaded[s], uses[0] * 16 + 16), *(((work1c, (g - 3) * K),) if late(g, 4) else ()))
                pool.tensor_tensor(y1[:, s, :, :], gc1[:, s, :, 0:D],
                                   over(alpha1[:, bass.ds(g * K, K)].unsqueeze(2), P, K, D), ALU.mult).then_inc(made1, 1)
            quads(pool, messages1)
            ready((beta_out, 16))
            collect(1, betas, eidx, beta_n)
            ready((ended, 1), (states_out[0], 16 * 1 * LOOPS), (states_out[1], 16 * 1 * LOOPS), (carry_out, 16 * 1))
            collect(1, state1, eidx, agg)
            collect(1, carry1, cidx, cg)

            ready((taken, 20))
            put(2, put2, bn_rows)
            ready((rows_out, 16 * 2), (tab_out, 16 * (1 + 2 * NBATCH)), (put_out, 16 * 2 * NT))
            hold(2, rows2, hold2)

            def gather2(g, s, uses):
                ready((ring_in["2"][s], uses[0] * 16 + 16),
                      *(((summed2, g - 3), (made2, g - 3)) if not isinstance(g, int) or g >= 4 else ()))
                gather("2", tab2, g2, M_SRC, s)
            quads(pool, gather2)
            ready((ended, 2), (states_out[0], 16 * 2 * LOOPS), (states_out[1], 16 * 2 * LOOPS), (carry_out, 16 * 2))
            collect(2, state2, eidx, agg2)
            collect(2, carry2, cidx, cg2)

            ready((taken, 30), (zero3_out, 16 * NG))
            put(3, put3, xr_rows)
            ready((rows_out, 16 * 3), (tab_out, 16 * (1 + 3 * NBATCH)), (put_out, 16 * 3 * NT))
            hold(3, rows3, hold3)

            def gather3(g, s, uses):
                ready((ring_in["3a"][s], uses[0] * 16 + 16),
                      *(((summed3, g - 3), (work3, (g - 3) * 5 - 2), (kept["3a"][s], uses[0] * 16)) if not isinstance(g, int) or g >= 4 else ()))
                gather("3a", tab3, g3, M_SRC, s)
            quads(pool, gather3)
            pool.wait_ge(weights_set, 2)

            def messages3(g, s, uses):
                ready((loaded[s], uses[0] * 16 + 16 * (1 + after(3, s))), *(((heads3, g - 1),) if late(g, 2) else ()))
                for k in range(KD, K):
                    message = pool.tensor_tensor(y3[:, s % 2, k, :].rearrange("p (h c) -> p h c", c=D),
                                                 gc3[:, s, k, 0:HD].rearrange("p (h c) -> p h c", c=D),
                                                 over(score[:, :, bass.ds(g * K, K)][:, :, k:k + 1], P, H, D), ALU.mult)
                message.then_inc(made3b, 1)
            quads(pool, messages3)
            ready((ended, 4), (states_out[0], 16 * 3 * LOOPS), (states_out[1], 16 * 3 * LOOPS), (carry_out, 16 * 3))
            collect(3, state3, eidx, agg)
            collect(3, carry3, cidx, cg)

        PARAMS = 16 * (7 + 5 + len(row_loads) + 4 + 5)

        @block.scalar
        def _(act):
            act.wait_ge(zeroed, 2)
            for table, at, line in ((state1, EP, zero[0:1, 0:D]), (state2, EP, zero[0:1, 0:2 * D]), (state3, EP, zero[0:1, 0:D]),
                                    (carry1, P, zero[0:1, 0:D]), (carry3, P, zero[0:1, 0:D])):
                act.dma_start(table[at:at + 1, :], line).then_inc(zero_out, 16)
            act.dma_start(carry2[P:P + 1, 0:D], zero[0:1, 0:D]).then_inc(zero_out, 16)
            act.dma_start(carry2[P:P + 1, D:2 * D], lowest[0:1, :]).then_inc(zero_out, 16)
            act.wait_ge(consts, 1)
            act.dma_start(betas[EP:EP + 1, :], ones[0:1, 0:R]).then_inc(zero_out, 16)

            for n, ax in ((0, tmpb[:, 0:T]), (1, sc[:, 1:2])):
                act.wait_ge(plus_in, n + 1)
                act.activation(ax, ax, ACT.Exp, scale=-1.0).then_inc(plus_exp, 1)
                act.wait_ge(plus_exp, n + 1)
                act.activation(ax, ax, ACT.Ln, bias=1.0).then_inc(plus_ln, 1)
            act.wait_ge(plus_in, 3)
            act.activation(sc[:, 4:7], sc[:, 4:7], ACT.Exp).then_inc(plus_ln, 1)

            def deviation(n):
                act.wait_ge(ln_var, n + 1)
                act.activation(lnv[:, 2, :], lnv[:, 1, :], ACT.Sqrt).then_inc(ln_std, 1)

            def lift(s, b):
                act.wait_ge(turned, 5 * s + b + 1)
                need(act, mixed, 5 * s + b)
                act.activation(hT[:, :, :], bank(6, 2)[0:D, 0:BC].rearrange("d (j n) -> d j n", n=P), ACT.Copy).then_inc(lifted, 1)

            def lift_only(s):
                batches(act, lambda b: lift(s, b))

            deviation(0)
            lift_only(0)
            act.wait_ge(norm_in, 1)
            act.activation(lnv[:, 1, :], lnv[:, 0, :], ACT.Sqrt).then_inc(norm_out, 1)
            act.dma_start(tab0.rearrange(by_node, i=NT), wh[:, 0:NT, :]).then_inc(tab_out, 16)
            act.wait_ge(norms_up, 1)
            act.activation(per_src, bank(0, 7)[:, 0:NP], ACT.Sqrt).then_inc(norm_out, 1)

            def clear_columns(table, at, columns, parts, semaphore):
                act.dma_start(table[0:EP, :].rearrange(by_edge, t=T)[:, bass.ds(at, columns), :].rearrange("p t c -> p (t c)").rearrange("p (n w) -> p n w", n=parts),
                              over(zero[:, 0:columns * table.shape[1] // parts].unsqueeze(1), P, parts, columns * table.shape[1] // parts)).then_inc(semaphore, 16)

            def clear_window(w):
                act.wait_ge(added[GW - 1], w * 16 * K + 16 * K)
                clear_columns(put1, w * W, W, 1, zero_out)
                clear_columns(put2, w * W, W, GW, zero_out)
            clear_window(0)
            with act.Fori(1, NW) as w:
                clear_window(w)
            act.wait_ge(norm_in, 2)
            act.activation(rnv[:, 1:2], rnv[:, 0:1], ACT.Sqrt).then_inc(norm_out, 1)

            act.wait_ge(piece_set, 1)

            def sign(j, s, uses):
                if late(j, 2):
                    act.wait_ge(similar, (j - 1) * 4)
                act.sem_inc(turns, 1)
                own = wh_lhs[:, s % 2, :, :]
                act.activation(own[:, 0, :], high_middle[:, bass.ds(j, 1), :].rearrange("p a n -> p (a n)"), ACT.Copy)
                act.activation(own[0:D, 1, :], high_middle[0:D, bass.ds(j, 1), :].rearrange("p a n -> p (a n)"), ACT.Copy)
                act.activation(own[D:P, 1, :], low[D:P, bass.ds(j, 1), :].rearrange("p a n -> p (a n)"), ACT.Copy)
                act.activation(wh_own[:, s, :], wh[:, bass.ds(j, 1), :].rearrange("p a c -> p (a c)"), ACT.Copy).then_inc(lhs_set, 1)
                for c in range(4):
                    act.wait_ge(similar, j * 4 + c + 1)
                    if c > 1 or late(j, 1):
                        act.wait_ge(work0, j * 8 + (-4, -2, 1, 2)[c])
                    dots = psum[:, 4 + c % 2 * 2:6 + c % 2 * 2, 0:NP // 8]
                    act.activation(signed[:, c % 2, 0, :].rearrange("p (b n) -> p b n", b=2), dots, ACT.Relu, scale=sc[:, 4:5])
                    act.activation(signed[:, c % 2, 1, :].rearrange("p (b n) -> p b n", b=2), dots, ACT.Relu, scale=sc[:, 9:10]).then_inc(signs, 1)
            tiles(act, sign)

            deviation(1)
            lift_only(1)

            def keep1a(i, h, first):
                act.wait_ge(got["1a"][h], i * 16 * K + 16 * K)
                act.dma_start(group_rows(spill1, i * 2 + h), g1[:, h, :, :]).then_inc(kept["1a"][h], 16)
                clear_columns(put3, (i * 2 + h) * K, K, 2, zero3_out)
            passes(act, keep1a)
            for h in range(2):
                act.wait_ge(kept["1a"][h], 16 * LOOPS)
            act.wait_ge(soft_in, 1)
            act.activation(v1, v1, ACT.Exp).then_inc(soft_exp, 1)
            act.activation(ds[:, :, R:2 * R], ds[:, :, R:2 * R], ACT.Exp).then_inc(soft_exp, 1)

            def keep1c(g, s, uses):
                act.wait_ge(work1c, g * K + K)
                act.dma_start(group_rows(state1, g), st1[:, s % 2, :, :]).then_inc(states_out[s % 2], 16)
            quads(act, keep1c)
            lift_only(2)

            deviation(2)
            lift_only(3)

            def keep2(g, h):
                act.wait_ge(scan2, g * 2 * K + 2 * K)
                act.dma_start(group_rows(state2, g), st2[:, h, :, :]).then_inc(states_out[h], 16)

            def gate(g, s, uses):
                h = s % 2
                if not isinstance(g, int) or g >= 2:
                    keep2(g - 2, h)
                act.wait_ge(work2, g * 2 + 2)
                act.activation(e2[:, 2 + h, :], e2[:, h, :], ACT.Sigmoid, bias=par[:, 6:7]).then_inc(gate2, 1)
                act.wait_ge(gate2, g + 1)
                for k in range(K):
                    message = act.activation(m2[:, h, k, :], g2[:, s, k, HID:W2], ACT.Copy, scale=e2[:, 2 + h, k:k + 1])
                message.then_inc(made2, 1)
            quads(act, gate)
            keep2(NG - 2, 0)
            keep2(NG - 1, 1)

            def lift2(b):
                lift(4, b)
                act.wait_ge(turned_m, b + 1)
                act.activation(mT2, bank(4, 2)[:, 0:BC], ACT.Copy).then_inc(lifted_m, 1)
                act.wait_ge(hidden, b + 1)
                act.activation(hidT2, bank(0, 2)[:, 0:BC], ACT.Relu, bias=colb[:, 0:1]).then_inc(hidden_up, 1)
            batches(act, lift2)

            deviation(3)
            lift_only(5)

            def keep3a(g, s, uses):
                act.wait_ge(got["3a"][s], uses[0] * 16 * K + 16 * K)
                act.dma_start(group_rows(spill3, g), g3[:, s, :, :]).then_inc(kept["3a"][s], 16)
            quads(act, keep3a)
            for s in range(4):
                act.wait_ge(kept["3a"][s], 16 * ((NG - s + 3) // 4))
            act.wait_ge(soft_in, 2)
            act.activation(score[:, :, :], score[:, :, :], ACT.Exp).then_inc(soft_exp, 1)

            def keep3c(g, s, uses):
                act.wait_ge(work3c, g * K + K)
                act.dma_start(group_rows(state3, g), st3[:, s % 2, :, :]).then_inc(states_out[s % 2], 16)
            quads(act, keep3c)
            act.wait_ge(bn_var, 1)
            act.activation(bnv[:, 3, :], bnv[:, 2, :], ACT.Sqrt).then_inc(bn_std, 1)

            def lift3(b):
                lift(6, b)
                for c in range(2):
                    act.wait_ge(hidden, NBATCH + 2 * b + c + 1)
                    act.activation(hid3[:, c, :], bank(2 * c, 2)[:, 0:BC], ACT.Relu, bias=colb[:, 1 + c:2 + c]).then_inc(hidden_up, 1)
            batches(act, lift3)
            act.wait_ge(bn_var, 2)
            act.activation(bnv[:, 3, :], bnv[:, 2, :], ACT.Sqrt).then_inc(bn_std, 1)

        @block.tensor
        def _(pe):
            pe.wait_ge(consts, 9)
            pe.wait_ge(params_in, PARAMS)

            def turn(s, b):
                pe.wait_ge(staged, 5 * s + b + 1)
                need(pe, lifted, 5 * s + b)
                pe.sem_inc(turns, 1)
                for j in range(NB):
                    mm = pe.transpose(bank(6, 2)[0:D, j * P:(j + 1) * P], hst[:, j, :], ident[:, :])
                return mm

            def mix(s, b, products):
                turn(s, b).then_inc(turned, 1)
                pe.wait_ge(lifted, 5 * s + b + 1)
                need(pe, taken, 5 * s + b)
                for j in range(NB):
                    for at, rhs in products:
                        width = rhs.shape[1]
                        mm = pe.matmul(bank(0, 6)[:, at + j * width:at + (j + 1) * width], lhsT=hT[:, j, :], rhs=rhs,
                                       start=True, stop=True)
                mm.then_inc(mixed, 1)

            def spread(column, b, at):
                return pe.matmul(bank(b)[:, at:at + P], lhsT=over(column, P, P), rhs=ident[:, :], start=True, stop=True)

            def carry(use, tail, width):
                pe.wait_ge(c_tail, use + 1)
                pe.transpose(bank(0)[0:width, 0:P], tail, ident[:, :]).then_inc(c_turn, 1)
                pe.wait_ge(c_scan, use + 1)
                pe.transpose(bank(1)[:, 0:width], cT[0:width, 1:P + 1] if use in BACKWARD else cT[0:width, 0:P],
                             ident[0:width, 0:width]).then_inc(c_back, 1)

            def rows0(b):
                turn(0, b).then_inc(turned, 1)
                pe.wait_ge(lifted, b + 1)
                need(pe, taken, b)
                for j in range(NB):
                    pe.matmul(bank(0)[:, j * D:(j + 1) * D], lhsT=hT[:, j, :], rhs=w0_sb[:, 0, :], start=True, stop=True)
                for lo, hi in ((0, 512), (512, BC)):
                    mm = pe.matmul(bank(2, 2)[:, lo:hi], lhsT=w0_sb[:, :, :].rearrange("d a f -> d (a f)"), rhs=hT[:, :, :].rearrange("d j n -> d (j n)")[:, lo:hi],
                                   start=True, stop=True)
                mm.then_inc(mixed, 1)
            batches(pe, rows0)
            pe.wait_ge(squared, 1)
            for at in range(0, NP, 512):
                mm = pe.matmul(bank(at // 512)[:, 0:min(512, NP - at)], lhsT=ones[0:D, :], rhs=squares[:, at:min(at + 512, NP)],
                               start=True, stop=True)
            mm.then_inc(norms_up, 1)
            pe.wait_ge(norm_out, 2)

            pe.wait_ge(taken, NBATCH)

            def count(i, h, first):
                g = i * 2 + h
                pe.wait_ge(hot, i * 4 + 2 * h + 2)
                if not first:
                    pe.wait_ge(tallied, g)
                for k in range(K):
                    mm = pe.matmul(bank(h)[:, 0:NT], lhsT=hot_p[:, h * K + k, :], rhs=hot_i[:, h * K + k, :], start=(k == 0),
                                   stop=(k == K - 1))
                mm.then_inc(counted, 1)
            passes(pe, count)
            pe.wait_ge(to_spread, 3)
            pe.matmul(bank(1)[:, 0:1], lhsT=upper[:, :], rhs=nodev[:, 1, NT - 1:NT], start=True, stop=True).then_inc(spread_up, 1)
            spread(flags[:, 0:1], 2, 0).then_inc(spread_up, 1)
            spread(flags[:, 1:2], 2, P).then_inc(spread_up, 1)

            pe.wait_ge(flags_read, 3)
            pe.wait_ge(piece_up, 2)
            pe.transpose(bank(7)[:, 0:P], cin[:, :], ident[:, :]).then_inc(piece_turned, 1)
            pe.wait_ge(piece_set, 1)

            def sum_up(j, s, uses):
                pe.wait_ge(work0, j * 8 + 8)
                if s % 2 == 0 and late(j, 2):
                    pe.wait_ge(sums_taken, uses * 2 + s // 2)
                for c in range(8):
                    mm = pe.matmul(bank(c % 4)[c // 4 * D:(c // 4 + 1) * D, 0:NP // 8], lhsT=wh_own[:, s, :],
                                   rhs=cells[:, s, c * NP // 8:(c + 1) * NP // 8], start=(s % 2 == 0), stop=(s % 2 == 1))
                mm.then_inc(summed0, 1)

            def dots0(j, s, uses):
                pe.wait_ge(lhs_set, j + 1)
                for c in range(4):
                    if late(j * 4 + c, 2):
                        pe.wait_ge(signs, j * 4 + c - 1)
                    for half in range(2):
                        at = (2 * c + half) * NP // 8
                        for n, (own, rows) in enumerate(((0, high_middle), (0, middle_high), (1, low_high))):
                            mm = pe.matmul(bank(4 + c % 2 * 2 + half)[:, 0:NP // 8], lhsT=wh_lhs[:, s % 2, own, :],
                                           rhs=rows[:, 0:NT, :].rearrange("p j n -> p (j n)")[:, at:at + NP // 8],
                                           start=(n == 0), stop=(n == 2))
                    mm.then_inc(similar, 1)
                if late(j, 1):
                    sum_up(j - 1, (s - 1) % 4, (j - 1) // 4 if isinstance(j, int) else uses - (1 if s == 0 else 0))
            tiles(pe, dots0)
            sum_up(TILES - 1, (TILES - 1) % 4, (TILES - 1) // 4)
            pe.wait_ge(sums_taken, TILES // 2)
            for half in range(2):
                side, first = slice(half * D, half * D + D), half * NP // 2
                for i in range(NT):
                    place, lo, hi = bank(0, 4)[:, i * D:(i + 1) * D], max(i * P, first), min((i + 1) * P, first + NP // 2)
                    if hi <= lo:
                        continue
                    rows = total0[side, lo - first:hi - first]
                    if hi - lo == P:
                        mm = pe.transpose(place, rows, ident[side, side])
                    else:
                        mm = pe.matmul(place[lo - i * P:hi - i * P, :], lhsT=rows, rhs=ident[side, side], start=True, stop=True)
                mm.then_inc(sums_turned, 1)
                pe.wait_ge(sums_turned, half + 1)

            pe.wait_ge(sums_taken, TILES // 2)
            pe.wait_ge(wa_set, 2)
            wrel_all = wrel_sb[:, :, :].rearrange("d r f -> d (r f)")
            batches(pe, lambda b: mix(1, b, [(0, wrel_all), (5 * 512, wa[:, :, :].rearrange("d a r -> d (a r)"))]))
            pe.wait_ge(taken, 2 * NBATCH)
            carry(0, tails[:, :], R)
            carry(1, heads[:, :], R)
            carry(2, tails[:, :], R)
            carry(3, heads[:, :], R)
            carry(4, st1[:, 1, K - 1, :], D)
            pe.wait_ge(c_in, 5)
            batches(pe, lambda b: mix(2, b, [(0, wrel_all), (5 * 512, wself_sb[:, :])]))

            batches(pe, lambda b: mix(3, b, [(0, we1_sb[:, :, :].rearrange("d a f -> d (a f)"))]))
            pe.wait_ge(taken, 4 * NBATCH)

            def add_up(n, rows_of, banks, per_bank, width, g, s, uses, filled, steps, used, each, reads, summed):
                pe.wait_ge(got[n][s], uses[0] * 16 * K + 16 * K)
                pe.wait_ge(filled, g * steps + K)
                if not isinstance(g, int) or g >= 2:
                    pe.wait_ge(used, (g - 2) * each + reads)
                for j in range(banks):
                    columns = slice(j * per_bank, (j + 1) * per_bank)
                    place = bank(s % 2 * banks + j).rearrange("p (k c) -> p k c", c=width)
                    pe.matmul(place, lhsT=ident[:, :], rhs=rows_of[0][:, s, columns, 0:width], start=True, stop=False)
                    mm = pe.matmul(place, lhsT=ident[:, :], rhs=rows_of[1][:, s, columns, 0:width], start=False, stop=True)
                mm.then_inc(summed, 1)
            quads(pe, lambda g, s, uses: add_up("2", (g2, z2), 2, 4, HID, g, s, uses, filled2, K + 1, work2, 2, 1, summed2))
            carry(5, st2[:, 1, K - 1, :], 2 * D)
            pe.wait_ge(c_in, 6)

            def mlp2(b):
                turn(4, b).then_inc(turned, 1)
                need(pe, lifted_m, b)
                for j in range(NB):
                    mm = pe.transpose(bank(4, 2)[:, j * P:(j + 1) * P], mst2[:, j, :], ident[:, :])
                mm.then_inc(turned_m, 1)
                pe.wait_ge(lifted, 20 + b + 1)
                pe.wait_ge(lifted_m, b + 1)
                need(pe, hidden_up, b)
                for lo, hi in ((0, 512), (512, BC)):
                    pe.matmul(bank(0, 2)[:, lo:hi], lhsT=wn1m_sb[:, :], rhs=mT2[:, lo:hi], start=True, stop=False)
                    mm = pe.matmul(bank(0, 2)[:, lo:hi], lhsT=wn1h_sb[:, :], rhs=hT[:, :, :].rearrange("d j n -> d (j n)")[:, lo:hi],
                                   start=False, stop=True)
                mm.then_inc(hidden, 1)
                pe.wait_ge(hidden_up, b + 1)
                need(pe, taken, 20 + b)
                for j in range(NB):
                    mm = pe.matmul(bank(2)[:, j * D:(j + 1) * D], lhsT=hidT2[:, j * P:(j + 1) * P], rhs=wn2_sb[:, :], start=True, stop=True)
                mm.then_inc(mixed, 1)
            batches(pe, mlp2)

            pe.wait_ge(taken, 5 * NBATCH)
            batches(pe, lambda b: mix(5, b, [(0, wlr_sb[:, :, :].rearrange("d a f -> d (a f)"))]))
            pe.wait_ge(taken, 6 * NBATCH)
            quads(pe, lambda g, s, uses: add_up("3a", (g3, z3), 4, 2, HD, g, s, uses, filled3, K + 1, work3, 5, 2, summed3))
            carry(6, tails[:, 0:H], H)
            carry(7, heads[:, 0:H], H)
            carry(8, tails[:, 0:H], H)
            carry(9, heads[:, 0:H], H)

            def head_sum(g, s, uses):
                h = s % 2
                pe.wait_ge(made3, g * KD + KD)
                pe.wait_ge(made3b, g + 1)
                if not isinstance(g, int) or g >= 2:
                    pe.wait_ge(work3c, (g - 1) * K)
                for head in range(H):
                    mm = pe.matmul(bank(h).rearrange("p (k c) -> p k c", c=D), lhsT=ident[:, :],
                                   rhs=y3[:, h, :, head * D:(head + 1) * D], start=(head == 0), stop=(head == H - 1))
                mm.then_inc(heads3, 1)
            quads(pe, head_sum)
            carry(10, st3[:, 1, K - 1, :], D)
            pe.wait_ge(c_in, 11)

            def node_sum(n):
                pe.wait_ge(bn_in, n + 1)
                pe.matmul(bank(0)[:, 0:D], lhsT=valid[:, :], rhs=bnv[:, 0, :], start=True, stop=True).then_inc(bn_sum, 1)
            node_sum(0)
            node_sum(1)

            def mlp3(b):
                turn(6, b).then_inc(turned, 1)
                pe.wait_ge(lifted, 30 + b + 1)
                need(pe, hidden_up, NBATCH + 2 * b)
                for c in range(2):
                    for lo, hi in ((0, 512), (512, BC)):
                        mm = pe.matmul(bank(2 * c, 2)[:, lo:hi], lhsT=wf1_sb[:, c * P:(c + 1) * P],
                                       rhs=hT[:, :, :].rearrange("d j n -> d (j n)")[:, lo:hi], start=True, stop=True)
                    mm.then_inc(hidden, 1)
                pe.wait_ge(hidden_up, NBATCH + 2 * b + 2)
                need(pe, taken, 30 + b)
                for j in range(NB):
                    for c in range(2):
                        mm = pe.matmul(bank(4)[:, j * D:(j + 1) * D], lhsT=hid3[:, c, j * P:(j + 1) * P], rhs=wf2_sb[:, c, :],
                                       start=(c == 0), stop=(c == 1))
                mm.then_inc(mixed, 1)
            batches(pe, mlp3)
            pe.wait_ge(taken, 7 * NBATCH)
            node_sum(2)
            node_sum(3)

        @block.vector
        def _(dve):
            tally = Tally(dve)

            def step(instruction):
                tally.done(instruction, vec)

            def spread(ap, *shape):
                return ap.to_broadcast(list(shape))

            for tile, value in ((ints[:, 0:T + 1], N), (ints[:, T + 1:T + 2], -1), (srci, N), (typei, 0)):
                dve.memset(tile, value).then_inc(padded, 1)
            for tile in (adj_sb, deg_sb, xn[:, :, :]):
                dve.memset(tile, 0.0).then_inc(padded, 1)
            dve.memset(zero[:, :], 0.0).then_inc(zeroed, 1)
            dve.memset(lowest[:, :], -BIG).then_inc(zeroed, 1)
            dve.wait_ge(zeroed, 2)

            dve.wait_ge(edges_in, 16 * 12)
            dve.wait_ge(padded, 7)
            step(dve.tensor_copy(dext, ints))
            mid = dext[:, 1:T + 1]
            step(dve.tensor_tensor(ns[:, :], mid, dext[:, 0:T], ALU.is_equal))
            step(dve.tensor_tensor(nl[:, :], mid, dext[:, 2:T + 2], ALU.is_equal))
            step(dve.tensor_scalar(neg[:, :], ns[:, :], -1.0, BIG, ALU.add, ALU.mult))
            step(dve.tensor_scalar(last[:, :], nl[:, :], -1.0, 1.0, ALU.mult, ALU.add))
            tally.done(dve.tensor_reduce(flags[:, 0:1], ns[:, :], AX.X, ALU.min), to_spread)
            tally.done(dve.tensor_reduce(flags[:, 1:2], nl[:, :], AX.X, ALU.min), to_spread)
            step(dve.memset(tmpb[:, 0:1], 1.0))
            step(dve.tensor_tensor_scan(tmpb[:, 1:T + 1], nl[:, :], zero[:, 0:T], 1.0, ALU.mult, ALU.add))
            step(dve.tensor_tensor(first_last[:, :], tmpb[:, 0:T], tmpb[:, 1:T + 1], ALU.subtract))
            step(dve.tensor_copy(srcf, srci))
            step(dve.tensor_copy(etypef[:, :], typei))
            step(dve.tensor_copy(dst0[:, :], dext[:, 1:2]))

            def by_group(ap):
                return ap.rearrange("p (g k) -> p g k", k=K)
            step(dve.tensor_copy(meta[:, :, M_SRC:M_SRC + K], by_group(srci)))
            step(dve.scalar_tensor_tensor(out=tmpa, in0=srcf, scalar=float(R), in1=etypef[:, :], op0=ALU.mult, op1=ALU.add))
            step(dve.tensor_copy(meta[:, :, M_REL:M_REL + K], by_group(tmpa)))

            dve.wait_ge(params_in, PARAMS)

            def softplus(x, ax, result, uses):
                step(dve.scalar_tensor_tensor(out=ax, in0=x, scalar=-1.0, in1=x, op0=ALU.mult, op1=ALU.max))
                dve.sem_inc(plus_in, 1)
                dve.wait_ge(plus_ln, uses)
                step(dve.scalar_tensor_tensor(out=result, in0=x, scalar=0.0, in1=ax, op0=ALU.max, op1=ALU.add))
            step(dve.tensor_scalar(tmpa, deg_sb, par[:, 0:1], par[:, 1:2], ALU.mult, ALU.add))
            softplus(tmpa, tmpb[:, 0:T], base, 1)
            step(dve.tensor_tensor(base, base, adj_sb, ALU.mult))
            step(dve.tensor_tensor(tmpa, srcf, mid, ALU.not_equal))
            step(dve.tensor_tensor(base, base, tmpa, ALU.mult))
            softplus(par[:, 5:6], sc[:, 1:2], sc[:, 2:3], 2)
            step(dve.tensor_reduce(sc[:, 3:4], par[:, 2:5], AX.X, ALU.max))
            step(dve.tensor_scalar(sc[:, 4:7], par[:, 2:5], sc[:, 3:4], None, ALU.subtract))
            dve.sem_inc(plus_in, 1)
            dve.wait_ge(plus_ln, 3)
            step(dve.tensor_reduce(sc[:, 7:8], sc[:, 4:7], AX.X, ALU.add))
            step(dve.reciprocal(sc[:, 8:9], sc[:, 7:8]))
            step(dve.tensor_scalar(sc[:, 4:7], sc[:, 4:7], sc[:, 8:9], None, ALU.mult))
            step(dve.tensor_scalar(sc[:, 9:10], sc[:, 5:6], -1.0, None, ALU.mult))

            def node_place(node, place, column):
                step(dve.tensor_scalar(place, node, 1.0 / NT, -(NT - 1) / 2 / NT, ALU.mult, ALU.add))
                step(dve.tensor_scalar(place, place, ROUND, -ROUND, ALU.add, ALU.add))
                step(dve.scalar_tensor_tensor(out=column, in0=place, scalar=-float(NT), in1=node, op0=ALU.mult, op1=ALU.add))
            node_place(srcf, tmpa, tmpb[:, 0:T])
            step(dve.scalar_tensor_tensor(out=key, in0=tmpb[:, 0:T], scalar=float(P), in1=tmpa, op0=ALU.mult, op1=ALU.add))
            node_place(mid, pn, im)
            step(dve.scalar_tensor_tensor(out=tmpa, in0=im, scalar=float(P), in1=pn, op0=ALU.mult, op1=ALU.add))
            dve.wait_ge(consts, 12)
            step(dve.tensor_tensor_scan(tmpb[:, 0:T], ns[:, :], zero[:, 0:T], 1.0, ALU.mult, ALU.add))
            step(dve.scalar_tensor_tensor(out=tmpb[:, 0:T], in0=tmpa, scalar=piece_row[:, 0:1], in1=tmpb[:, 0:T],
                                          op0=ALU.subtract, op1=ALU.mult))
            step(dve.tensor_tensor(tmpa, tmpa, tmpb[:, 0:T], ALU.subtract))
            step(dve.scalar_tensor_tensor(out=key, in0=tmpa, scalar=float(NP), in1=key, op0=ALU.mult, op1=ALU.add))

            merge = Beats(dve, merging, 8)

            def merge0(w):
                merge.group(w)
                keys, weights = key[:, bass.ds(w * W, W)], base[:, bass.ds(w * W, W)]
                before, first, total = (merged0[:, k, :] for k in range(3))
                merge.done(dve.tensor_tensor(alike, spread(keys.unsqueeze(1), P, W, W), spread(keys.unsqueeze(2), P, W, W), ALU.is_equal))
                merge.done(dve.tensor_tensor(alike_by, alike, earlier, ALU.mult))
                merge.done(dve.tensor_reduce(before, alike_by, AX.X, ALU.add))
                merge.add(dve.tensor_tensor(alike_by, alike, spread(weights.unsqueeze(1), P, W, W), ALU.mult))
                merge.done(dve.scalar_tensor_tensor(out=first, in0=before, scalar=0.5, in1=ones[:, 0:W], op0=ALU.is_lt, op1=ALU.mult))
                merge.done(dve.tensor_reduce(total, alike_by, AX.X, ALU.add))
                dve.tensor_tensor(before, keys, trash[:, :], ALU.subtract).then_inc(apart, 1)
                dve.wait_ge(apart, w * 2 + 1)
                dve.tensor_tensor(before, before, first, ALU.mult).then_inc(apart, 1)
                dve.wait_ge(apart, w * 2 + 2)
                cells_out = words0[:, bass.ds(w * GW, GW), 0:K]
                merge.add(dve.tensor_tensor(cells_out, by_group(before), by_group(trash[:, :]), ALU.add))
                merge.done(dve.tensor_scalar(words0f[:, bass.ds(w * GW, GW), K:2 * K], by_group(total), 1.0, None, ALU.mult))
            merge0(0)
            with dve.Fori(1, NW) as w:
                merge0(w)

            def norm_relu(n):
                col = [lnv[:, k, :] for k in range(4)]
                step(dve.tensor_reduce(col[0], xn[:, :, :], AX.X, ALU.add))
                step(dve.tensor_scalar(col[0], col[0], 1.0 / D, None, ALU.mult))
                step(dve.tensor_tensor(hn[:, :, :], xn[:, :, :], spread(col[0].unsqueeze(2), P, NT, D), ALU.subtract))
                step(dve.tensor_tensor(agg[:, :, :], hn[:, :, :], hn[:, :, :], ALU.mult))
                step(dve.tensor_reduce(col[0], agg[:, :, :], AX.X, ALU.add))
                step(dve.tensor_scalar(col[1], col[0], 1.0 / D, EPS, ALU.mult, ALU.add))
                dve.sem_inc(ln_var, 1)
                dve.wait_ge(ln_std, n + 1)
                step(dve.reciprocal(col[3], col[2]))
                step(dve.tensor_tensor(hn[:, :, :], hn[:, :, :], spread(col[3].unsqueeze(2), P, NT, D), ALU.mult))
                step(dve.tensor_scalar(hn[:, :, :], hn[:, :, :], 0.0, None, ALU.max))

            def stage(s, b, rows):
                need(dve, turned, 5 * s + b)
                return dve.tensor_scalar(hst[:, :, :], rows[:, bass.ds(b * NB, NB), :], 1.0, None, ALU.mult)

            def product(first, n, width):
                return bank(0, 6)[:, first:first + n].rearrange("p (j c) -> p j c", c=width)

            dve.wait_ge(x_in, 16)
            norm_relu(0)

            def nodes0(b):
                stage(0, b, hn).then_inc(staged, 1)
                dve.wait_ge(mixed, b + 1)
                dve.tensor_scalar(whT[:, bass.ds(b * NB, NB), :], bank(2, 2)[:, 0:BC].rearrange("d (j n) -> d j n", n=P),
                                  colb[:, 3:4], None, ALU.add)
                dve.tensor_tensor(wh[:, bass.ds(b * NB, NB), :], bank(0)[:, 0:NB * D].rearrange("p (j c) -> p j c", c=D),
                                  spread(row["b0"].unsqueeze(1), P, NB, D), ALU.add).then_inc(taken, 1)
            batches(dve, nodes0)
            dve.wait_ge(taken, NBATCH)
            rows_T = whT[0:D, 0:NT, :].rearrange("d j n -> d (j n)")
            tally.done(dve.tensor_tensor(squares, rows_T, rows_T, ALU.mult), squared)
            step(dve.tensor_tensor(agg[:, :, :], wh[:, 0:NT, :], wh[:, 0:NT, :], ALU.mult))
            tally.done(dve.tensor_reduce(lnv[:, 0, :], agg[:, :, :], AX.X, ALU.add), norm_in)
            dve.wait_ge(norm_out, 1)
            step(dve.reciprocal(per_dst[:, 0:NT], lnv[:, 1, :]))
            dve.wait_ge(norm_out, 2)
            step(dve.reciprocal(per_src, per_src))

            def split(x, hi, mid, lo):
                step(dve.tensor_copy(hi, x))
                step(dve.tensor_tensor(x, x, hi, ALU.subtract))
                step(dve.tensor_copy(mid, x))
                step(dve.tensor_tensor(x, x, mid, ALU.subtract))
                step(dve.tensor_copy(lo, x))
            real = slice(0, NT)
            split(whT[:, real, :], high[:, real, :], middle[:, real, :], low[:, real, :])
            for pairs_to, lower_part, upper_part in ((high_middle, high, middle), (middle_high, middle, high), (low_high, low, high)):
                step(dve.tensor_copy(pairs_to[0:D, real, :], lower_part[0:D, real, :]))
                step(dve.tensor_copy(pairs_to[D:P, real, :], upper_part[D:P, real, :]))

            dve.wait_ge(consts, 12)

            deg, cum, end, first_edge, has, at, from_before = (nodev[:, k, :] for k in range(7))
            dve.memset(deg, 0.0).then_inc(tallied, 1)

            def tally_counts(done, h):
                dve.wait_ge(counted, done)
                dve.wait_ge(tallied, done)
                dve.tensor_tensor(deg, bank(h)[:, 0:NT], deg, ALU.add).then_inc(tallied, 1)

            def one_hot(i, h, first):
                g = i * 2 + h
                if not first:
                    tally_counts(g - 1, h)
                for hots, place, width in ((hot_p, pn, P), (hot_i, im, NT)):
                    dve.tensor_tensor(hots[:, h * K:h * K + K, :], spread(iota_row[:, 0:width].unsqueeze(1), P, K, width),
                                      spread(place[:, bass.ds(g * K, K)].unsqueeze(2), P, K, width), ALU.is_equal).then_inc(hot, 1)
            passes(dve, one_hot)
            for h in range(2):
                tally_counts(NG - 1 + h, h)
            dve.wait_ge(tallied, 1 + NG)
            tally.done(dve.tensor_tensor_scan(cum, ones[:, 0:NT], deg, 0.0, ALU.mult, ALU.add), to_spread)
            dve.wait_ge(spread_up, 1)
            step(dve.tensor_scalar(end, cum, bank(1)[:, 0:1], None, ALU.add))
            step(dve.tensor_tensor(first_edge, end, deg, ALU.subtract))
            step(dve.tensor_scalar(has, deg, 0.0, None, ALU.is_gt))
            step(dve.tensor_tensor(at, first_edge, node_trash[:, :], ALU.subtract))
            step(dve.tensor_tensor(at, at, has, ALU.mult))
            step(dve.tensor_tensor(zidx[:, :], at, node_trash[:, :], ALU.add))
            step(dve.scalar_tensor_tensor(out=at, in0=end, scalar=-1.0 - EP, in1=has, op0=ALU.add, op1=ALU.mult))
            step(dve.tensor_scalar(eidx[:, :], at, float(EP), None, ALU.add))
            step(dve.tensor_scalar(at, end, 1.0 / T, -(1 + (T - 1) / 2) / T, ALU.mult, ALU.add))
            step(dve.tensor_scalar(at, at, ROUND, -ROUND, ALU.add, ALU.add))
            step(dve.scalar_tensor_tensor(out=from_before, in0=at, scalar=float(T), in1=first_edge, op0=ALU.mult, op1=ALU.is_gt))
            step(dve.tensor_tensor(from_before, from_before, has, ALU.mult))
            step(dve.scalar_tensor_tensor(out=at, in0=at, scalar=-float(P), in1=from_before, op0=ALU.add, op1=ALU.mult))
            tally.done(dve.tensor_scalar(cidx[:, :], at, float(P), None, ALU.add), indices)
            dve.wait_ge(spread_up, 3)
            tally.done(dve.tensor_copy(nhs_row[:, :], bank(2)[:, 0:P]), flags_read)
            tally.done(dve.tensor_copy(nhl_row[:, :], bank(2)[:, P:2 * P]), flags_read)
            tally.done(dve.tensor_scalar(hneg_row[:, :], nhs_row[:, :], -1.0, BIG, ALU.add, ALU.mult), flags_read)

            def mark(marks, g, k):
                return marks[:, bass.ds(g * K, K)][:, k:k + 1]

            def fill(beats, rows, hold, g, s, k):
                beats.wait()
                beats.add(dve.scalar_tensor_tensor(out=rows[:, s, k, :], in0=hold if k == 0 else rows[:, s, k - 1, :], scalar=mark(ns, g, k),
                                                   in1=rows[:, s, k, :], op0=ALU.mult, op1=ALU.add))

            def fill_hold(beats, rows, hold, s):
                beats.wait()
                beats.done(dve.tensor_scalar(hold, rows[:, s, K - 1, :], 1.0, None, ALU.mult))

            def before_of(g, s, uses, back=1):
                if isinstance(g, int):
                    return (g - back) // 4, (g - back) // 2
                return uses[0] - (1 if s < back else 0), uses[1] - (back + 1 - s % 2) // 2

            dve.wait_ge(hold_in, 16)
            step(dve.tensor_tensor(agg[:, 0, :], wh[:, NT, :], wh[:, NT, :], ALU.mult))
            tally.done(dve.tensor_reduce(rnv[:, 0:1], agg[:, 0, :], AX.X, ALU.add), norm_in)
            dve.wait_ge(norm_out, 3)
            step(dve.reciprocal(per_dst[:, NT:TILES], rnv[:, 1:2]))
            for half in range(2):
                tally.done(dve.tensor_copy(cin[:, half * D:(half + 1) * D], wh[:, NT, :]), piece_up)
            dve.wait_ge(piece_turned, 1)
            step(dve.tensor_copy(cT[:, 0:P], bank(7)[:, 0:P]))
            split(cT[:, 0:P], hst_parts[:, 0, :], hst_parts[:, 1, :], low[:, NT, :])
            step(dve.tensor_copy(high_middle[0:D, NT, :], hst_parts[0:D, 0, :]))
            tally.done(dve.tensor_copy(high_middle[D:P, NT, :], hst_parts[D:P, 1, :]), piece_set)
            works0 = Beats(dve, work0, 8)

            def sums0(pair):
                dve.wait_ge(summed0, pair * 2 + 2)
                if late(pair, 1):
                    dve.wait_ge(sums_taken, pair)
                sums, total = psum[:, 0:4, 0:NP // 8], total0.rearrange("d (c n) -> d c n", c=4)
                if late(pair, 1):
                    dve.tensor_tensor(total, sums, total, ALU.add).then_inc(sums_taken, 1)
                else:
                    dve.tensor_scalar(total, sums, 1.0, None, ALU.mult).then_inc(sums_taken, 1)

            def similarity0(j, s):
                works0.group(j)
                works0.wait()
                dve.wait_ge(weighted, j + 1)
                def part(c):
                    dve.wait_ge(signs, j * 4 + c + 1)
                    works0.add(dve.tensor_tensor(parts0[c % 3], signed[:, c % 2, 0, :], signed[:, c % 2, 1, :], ALU.subtract))

                def weigh(c, back):
                    at = c * NP // 4
                    works0.wait(back)
                    works0.add(dve.tensor_tensor(cells[:, s, at:at + NP // 4], cells[:, s, at:at + NP // 4], parts0[c % 3], ALU.mult))
                part(0)
                part(1)
                weigh(0, 1)
                part(2)
                weigh(1, 2)
                works0.wait(2)
                part(3)
                weigh(2, 2)
                weigh(3, 1)

            def edges0(j, s, uses):
                if late(j, 1):
                    dve.wait_ge(weighted, j)
                dve.tensor_scalar(per_pair, per_src, per_dst[:, bass.ds(j, 1)], 1e8, ALU.mult, ALU.min).then_inc(pairs, 1)
                if late(j, 4) and s % 2 == 0:
                    sums0(j // 2 - 2 if isinstance(j, int) else uses * 2 + (s // 2 - 2))
                if late(j, 1):
                    similarity0(j - 1, (s - 1) % 4)
            tiles(dve, edges0)
            similarity0(TILES - 1, (TILES - 1) % 4)
            sums0(TILES // 2 - 2)
            sums0(TILES // 2 - 1)
            dve.wait_ge(sums_taken, TILES // 2)
            dve.wait_ge(sums_turned, 2)
            sums = bank(0, 4)[:, 0:NT * D].rearrange("p (i c) -> p i c", c=D)
            step(dve.scalar_tensor_tensor(out=agg[:, :, :], in0=wh[:, 0:NT, :], scalar=sc[:, 6:7], in1=sums, op0=ALU.mult, op1=ALU.add))
            step(dve.scalar_tensor_tensor(out=xn[:, :, :], in0=agg[:, :, :], scalar=sc[:, 2:3], in1=xn[:, :, :], op0=ALU.mult, op1=ALU.add))

            for side, name in ((0, "a_src"), (1, "a_dst")):
                prod = area(5300, R, D)[0:D, :, :]
                step(dve.tensor_tensor(prod, wrel_sb[:, :, :], row[name][0:D, :].rearrange("p (r f) -> p r f", f=D), ALU.mult))
                tally.done(dve.tensor_reduce(wa[:, side, :], prod, AX.X, ALU.add), wa_set)
            norm_relu(1)
            beats1 = Beats(dve, node_vec[1], 3)

            def nodes1(b):
                beats1.group(b)
                stage(1, b, hn).then_inc(staged, 1)
                dve.wait_ge(mixed, 5 + b + 1)
                dve.wait_ge(tab_out, b * 16 + 16 * (1 + 0 * NBATCH))
                scores = product(5 * 512, NB * 2 * R, 2 * R)
                beats1.add(dve.tensor_copy(tb1.rearrange("p j r c -> p (j r) c")[:, :, 0:D], product(0, NB * R * D, D)))
                beats1.add(dve.tensor_copy(tb1[:, :, :, D], scores[:, :, 0:R]))
                beats1.done(dve.tensor_scalar(dn1[:, bass.ds(b * NB, NB), 0:R], scores[:, :, R:2 * R], 1.0, None, ALU.mult))
                dve.tensor_tensor(dn1[:, bass.ds(b * NB, NB), R:2 * R], dn1[:, bass.ds(b * NB, NB), 0:R], scores[:, :, 0:R],
                                  ALU.add).then_inc(taken, 1)
            batches(dve, nodes1)
            dve.wait_ge(taken, 2 * NBATCH)
            loops = dn1[:, :, R:2 * R]
            tally.done(dve.scalar_tensor_tensor(out=loops, in0=loops, scalar=SLOPE, in1=loops, op0=ALU.mult, op1=ALU.max), dn_set)

            dve.wait_ge(ds_in, 16)
            dve.wait_ge(hold_in, 16 * 2)
            for c in range(2 * R):
                step(dve.tensor_tensor_scan(ds[:, :, c], ns[:, :], ds[:, :, c], dinit1[:, c:c + 1], ALU.mult, ALU.add))
            s_src, ev, dsel, tmp = (score[:, k, :] for k in range(4))
            step(dve.scalar_tensor_tensor(out=dsel, in0=etypef[:, :], scalar=0.0, in1=ds[:, :, 0], op0=ALU.is_equal, op1=ALU.mult))
            for r in range(1, R):
                step(dve.scalar_tensor_tensor(out=tmp, in0=etypef[:, :], scalar=float(r), in1=ds[:, :, r], op0=ALU.is_equal, op1=ALU.mult))
                step(dve.tensor_tensor(dsel, dsel, tmp, ALU.add))

            def take1(i, h, first):
                dve.wait_ge(got["1a"][h], i * 16 * K + 16 * K)
                dve.tensor_scalar(s_src[:, bass.ds((i * 2 + h) * K, K)], g1[:, h, :, D], 1.0, None, ALU.mult).then_inc(taken1, 1)
            passes(dve, take1)
            dve.wait_ge(taken1, NG)
            for h in range(2):
                dve.wait_ge(kept["1a"][h], 16 * LOOPS)

            def over_partitions(use, source, width, op):
                flag = {"sum": nhs_row, "max": hneg_row, "back": nhl_row}[op]
                neutral = -BIG if op == "max" else 0.0
                ops = (ALU.add, ALU.max) if op == "max" else (ALU.mult, ALU.add)
                back = op == "back"
                assert back == (use in BACKWARD)
                dve.sem_inc(c_tail, 1)
                step(dve.memset(cT[:, P:P + 1] if back else cT[:, 0:1], neutral))
                dve.wait_ge(c_turn, use + 1)
                rows, flag = bank(0)[0:width, 0:P], flag[0:width, :]
                if back:
                    step(dve.tensor_tensor_scan(cT[0:width, 0:P][:, ::-1], flag[:, ::-1], rows[:, ::-1], neutral, *ops))
                else:
                    step(dve.tensor_tensor_scan(cT[0:width, 1:P + 1], flag, rows, neutral, *ops))
                dve.sem_inc(c_scan, 1)
                dve.wait_ge(c_back, use + 1)
                step(dve.tensor_copy(cin[:, 0:width], bank(1)[:, 0:width]))
                dve.sem_inc(c_in, 1)

            def segment_totals(use, values, totals, n, op):
                marks, neutral = (neg, -BIG) if op == "max" else (ns, 0.0)
                ops = (ALU.add, ALU.max) if op == "max" else (ALU.mult, ALU.add)
                for r in range(n):
                    step(dve.tensor_tensor_scan(totals[:, r, :], marks[:, :], values[:, r, :], neutral, *ops))
                step(dve.tensor_copy(tails[:, 0:n], totals[:, :, T - 1]))
                over_partitions(use, tails, n, op)
                for r in range(n):
                    step(dve.tensor_tensor_scan(totals[:, r, :], marks[:, :], values[:, r, :], cin[:, r:r + 1], *ops))
                step(dve.tensor_tensor(totals, totals, spread(last[:, :].unsqueeze(1), P, n, T), ALU.mult))
                for r in range(n):
                    step(dve.tensor_tensor(back_tmp, totals[:, r, :], first_last[:, :], ALU.mult))
                    step(dve.tensor_reduce(heads[:, r:r + 1], back_tmp, AX.X, ALU.add))
                over_partitions(use + 1, heads, n, "back")
                for r in range(n):
                    step(dve.tensor_tensor_scan(totals[:, r, ::-1], nl[:, ::-1], totals[:, r, ::-1], cin[:, r:r + 1], ALU.mult, ALU.add))

            back_tmp = tmp
            step(dve.tensor_tensor(ev, s_src, dsel, ALU.add))
            step(dve.scalar_tensor_tensor(out=ev, in0=ev, scalar=SLOPE, in1=ev, op0=ALU.mult, op1=ALU.max))
            for r in range(R):
                step(dve.scalar_tensor_tensor(out=v1[:, r, :], in0=etypef[:, :], scalar=float(r), in1=ev, op0=ALU.is_equal, op1=ALU.mult))
                step(dve.tensor_scalar(tmp, etypef[:, :], float(r), -BIG, ALU.not_equal, ALU.mult))
                step(dve.tensor_tensor(v1[:, r, :], v1[:, r, :], tmp, ALU.add))
            segment_totals(0, v1, f1, R, "max")
            loop_of_edge = ds[:, :, R:2 * R].rearrange("p t r -> p r t")
            step(dve.tensor_tensor(f1, f1, loop_of_edge, ALU.max))
            step(dve.tensor_tensor(v1, v1, f1, ALU.subtract))
            step(dve.tensor_tensor(loop_of_edge, loop_of_edge, f1, ALU.subtract))
            dve.sem_inc(soft_in, 1)
            dve.wait_ge(soft_exp, 2)
            segment_totals(2, v1, f1, R, "sum")
            step(dve.tensor_tensor(f1, f1, loop_of_edge, ALU.add))
            step(dve.reciprocal(f1, f1))
            step(dve.tensor_tensor(v1, v1, f1, ALU.mult))
            step(dve.tensor_reduce(alpha1, v1.rearrange("p r t -> p t r"), AX.X, ALU.add))
            tally.done(dve.tensor_tensor(betae, ds[:, :, R:2 * R], f1.rearrange("p r t -> p t r"), ALU.mult), weights_set)

            sums1 = Beats(dve, work1c, K)

            def sum1(g, s, uses):
                h = s % 2
                sums1.group(g)
                dve.wait_ge(made1, g + 1)
                need(dve, states_out[h], uses[1] * 16)
                for k in range(K):
                    sums1.wait()
                    before = st1[:, h, k - 1, :] if k else zero[:, 0:D] if isinstance(g, int) and g == 0 else st1[:, 1 - h, K - 1, :]
                    sums1.add(dve.scalar_tensor_tensor(out=st1[:, h, k, :], in0=before, scalar=mark(ns, g, k),
                                                       in1=y1[:, s, k, :], op0=ALU.mult, op1=ALU.add))
            quads(dve, sum1)
            dve.wait_ge(work1c, NG * K)
            over_partitions(4, st1, D, "sum")
            dve.sem_inc(ended, 1)
            for r in range(R):
                step(dve.tensor_tensor(row["b_self"], row["b_self"], row["bias_rel"][:, r * D:(r + 1) * D], ALU.add))
            dve.wait_ge(agg_in, 16 * 3 * NT)
            beats1n = Beats(dve, node_vec[2], 4)

            def nodes1b(b):
                beats1n.group(b)
                stage(2, b, hn).then_inc(staged, 1)
                dve.wait_ge(mixed, 10 + b + 1)
                beats1n.done(dve.tensor_tensor(prod1, bank(0, 5).rearrange("p (j r c) -> p j r c", r=R, c=D),
                                               spread(beta_n[:, bass.ds(b * NB, NB), :].unsqueeze(3), P, NB, R, D), ALU.mult))
                beats1n.done(dve.tensor_reduce(red1, prod1.rearrange("p j r c -> p j c r"), AX.X, ALU.add))
                beats1n.done(dve.tensor_tensor(red1, red1, product(5 * 512, NB * D, D), ALU.add))
                beats1n.done(dve.tensor_tensor(red1, red1, spread(row["b_self"].unsqueeze(1), P, NB, D), ALU.add))
                dve.tensor_tensor(xn[:, bass.ds(b * NB, NB), :], xn[:, bass.ds(b * NB, NB), :], red1, ALU.add).then_inc(taken, 1)
            batches(dve, nodes1b)
            dve.wait_ge(taken, 3 * NBATCH)
            step(dve.tensor_tensor(agg[:, :, :], agg[:, :, :], cg, ALU.add))
            step(dve.tensor_tensor(xn[:, :, :], xn[:, :, :], agg[:, :, :], ALU.add))

            norm_relu(2)
            beats2t = Beats(dve, node_vec[3], 2)

            def nodes2(b):
                beats2t.group(b)
                stage(3, b, hn).then_inc(staged, 1)
                dve.wait_ge(mixed, 15 + b + 1)
                dve.wait_ge(tab_out, b * 16 + 16 * (1 + 1 * NBATCH))
                halves = product(0, NB * 2 * HID, 2 * HID)
                beats2t.add(dve.tensor_copy(tb2[:, :, 0:HID], halves[:, :, 0:HID]))
                beats2t.add(dve.tensor_scalar(tb2[:, :, HID:W2], hn[:, bass.ds(b * NB, NB), :], 1.0, None, ALU.mult))
                beats2t.wait()
                dve.tensor_tensor(bn_rows[:, bass.ds(b * NB, NB), :], halves[:, :, HID:2 * HID], spread(row["be1"].unsqueeze(1), P, NB, HID),
                                  ALU.add).then_inc(taken, 1)
            batches(dve, nodes2)
            dve.wait_ge(taken, 4 * NBATCH)

            dve.wait_ge(hold_in, 16 * 3)
            fills2, beats2, scans2 = Beats(dve, filled2, K + 1), Beats(dve, work2, 2), Beats(dve, scan2, 2 * K)

            def gate2_in(g, h):
                beats2.group(g)
                dve.wait_ge(summed2, g + 1)
                need(dve, gate2, g - 1 if not isinstance(g, int) else max(g - 1, 0))
                beats2.done(dve.scalar_tensor_tensor(out=pr2, in0=bank(2 * h, 2).rearrange("p (k c) -> p k c", c=HID), scalar=0.0,
                                                     in1=spread(row["we2"].unsqueeze(1), P, K, HID), op0=ALU.max, op1=ALU.mult))
                beats2.done(dve.tensor_reduce(e2[:, h, :], pr2, AX.X, ALU.add))

            def sum2(g, s, uses, k):
                h = s % 2
                if k == 0:
                    scans2.group(g)
                    dve.wait_ge(made2, g + 1)
                    need(dve, states_out[h], uses[1] * 16 + 16 * LOOPS)
                start = isinstance(g, int) and g == 0 and k == 0
                prior = st2[:, h, k - 1, :] if k else st2[:, 1 - h, K - 1, :]
                scans2.wait(1 if k else 0)
                scans2.add(dve.scalar_tensor_tensor(out=st2[:, h, k, 0:D], in0=zero[:, 0:D] if start else prior[:, 0:D],
                                                    scalar=mark(ns, g, k), in1=m2[:, h, k, :],
                                                    op0=ALU.mult, op1=ALU.add))
                scans2.wait(1)
                scans2.add(dve.scalar_tensor_tensor(out=st2[:, h, k, D:2 * D], in0=lowest[:, :] if start else prior[:, D:2 * D],
                                                    scalar=mark(neg, g, k), in1=m2[:, h, k, :],
                                                    op0=ALU.add, op1=ALU.max))

            def edges2(g, s, uses):
                if not isinstance(g, int) or g >= 2:
                    gate2_in(g - 2, s % 2)
                dve.wait_ge(rows_in["2"][s], uses[0] * 16 + 16)
                fills2.group(g)
                for k in range(K):
                    fill(fills2, z2, hold2, g, s, k)
                    if not isinstance(g, int) or g >= 3:
                        sum2(g - 3, (s - 3) % 4, before_of(g, s, uses, 3), k)
                fill_hold(fills2, z2, hold2, s)
            quads(dve, edges2)
            for g in range(NG - 3, NG):
                if g > NG - 3:
                    gate2_in(g, g % 2)
                for k in range(K):
                    sum2(g, g % 4, (g // 4, g // 2), k)
            dve.wait_ge(scan2, NG * 2 * K)
            dve.sem_inc(c_tail, 1)
            step(dve.memset(cT[0:D, 0:1], 0.0))
            step(dve.memset(cT[D:2 * D, 0:1], -BIG))
            dve.wait_ge(c_turn, 6)
            step(dve.tensor_tensor_scan(cT[0:D, 1:P + 1], nhs_row[0:D, :], bank(0)[0:D, 0:P], 0.0, ALU.mult, ALU.add))
            step(dve.tensor_tensor_scan(cT[D:2 * D, 1:P + 1], hneg_row[D:2 * D, :], bank(0)[D:2 * D, 0:P], -BIG, ALU.add, ALU.max))
            dve.sem_inc(c_scan, 1)
            dve.wait_ge(c_back, 6)
            step(dve.tensor_copy(cin[:, :], bank(1)[:, 0:2 * D]))
            dve.sem_inc(c_in, 1)
            dve.sem_inc(ended, 1)
            dve.wait_ge(agg_in, 16 * 5 * NT)
            step(dve.tensor_tensor(agg2[:, :, 0:D], agg2[:, :, 0:D], cg2[:, :, 0:D], ALU.add))
            step(dve.tensor_tensor(agg2[:, :, D:2 * D], agg2[:, :, D:2 * D], cg2[:, :, D:2 * D], ALU.max))
            step(dve.tensor_tensor(xn[:, :, :], xn[:, :, :], hn[:, :, :], ALU.add))
            beats2n = Beats(dve, node_vec[4], 2)

            def nodes2b(b):
                beats2n.group(b)
                beats2n.done(stage(4, b, hn))
                need(dve, turned_m, b)
                dve.tensor_scalar(mst2, agg2[:, bass.ds(b * NB, NB), :], 1.0, None, ALU.mult).then_inc(staged, 1)
                dve.wait_ge(mixed, 20 + b + 1)
                red = area(9000, NB, D)
                beats2n.done(dve.tensor_tensor(red, bank(2)[:, 0:NB * D].rearrange("p (j c) -> p j c", c=D),
                                               spread(row["bn2"].unsqueeze(1), P, NB, D), ALU.add))
                dve.tensor_tensor(xn[:, bass.ds(b * NB, NB), :], xn[:, bass.ds(b * NB, NB), :], red, ALU.add).then_inc(taken, 1)
            batches(dve, nodes2b)
            dve.wait_ge(taken, 5 * NBATCH)

            norm_relu(3)
            step(dve.tensor_scalar(rowb[:, 0:HD], row["att"], 1.0 - SLOPE, None, ALU.mult))
            att_relu = rowb[:, 0:HD]
            step(dve.tensor_scalar(row["att"], row["att"], SLOPE, None, ALU.mult))
            lin, xs = area(8000, NB, HD), area(9300, NB, W3)
            beats3t = Beats(dve, node_vec[5], 6)

            def nodes3(b):
                beats3t.group(b)
                stage(5, b, hn).then_inc(staged, 1)
                dve.wait_ge(mixed, 25 + b + 1)
                dve.wait_ge(tab_out, b * 16 + 16 * (1 + 2 * NBATCH))
                sides = product(0, NB * 2 * HD, 2 * HD)
                beats3t.wait()
                need(dve, taken, 25 + b)
                for side, rows, name in ((0, tb3, "b_l"), (1, xs, "b_r")):
                    beats3t.done(dve.tensor_tensor(rows[:, :, 0:HD], sides[:, :, side * HD:(side + 1) * HD],
                                                   spread(row[name].unsqueeze(1), P, NB, HD), ALU.add))
                    beats3t.done(dve.tensor_tensor(lin, rows[:, :, 0:HD], spread(row["att"].unsqueeze(1), P, NB, HD), ALU.mult))
                    beats3t.done(dve.tensor_reduce(rows[:, :, HD:W3], lin.rearrange("p j (h c) -> p j h c", c=D), AX.X, ALU.add))
                dve.tensor_scalar(xr_rows[:, bass.ds(b * NB, NB), :], xs, 1.0, None, ALU.mult).then_inc(taken, 1)
            batches(dve, nodes3)
            dve.wait_ge(taken, 6 * NBATCH)

            dve.wait_ge(hold_in, 16 * 4)
            fills3, beats3 = Beats(dve, filled3, K + 1), Beats(dve, work3, 5)
            halves3 = [slice(0, K // 2), slice(K // 2, K)]

            def relu3(g, h, part):
                if part == 0:
                    beats3.group(g)
                    dve.wait_ge(summed3, g + 1)
                    need(dve, scored, g)
                columns = halves3[part]
                beats3.add(dve.scalar_tensor_tensor(out=pr3[:, columns, :], in0=bank(4 * h + 2 * part, 2).rearrange("p (k c) -> p k c", c=HD),
                                                    scalar=0.0, in1=spread(att_relu.unsqueeze(1), P, K // 2, HD), op0=ALU.max, op1=ALU.mult))

            def reduce3(part):
                columns = halves3[part]
                beats3.wait()
                beats3.add(dve.tensor_reduce(rs3[:, columns, :], pr3[:, columns, :].rearrange("p k (h c) -> p k h c", c=D), AX.X, ALU.add))

            def linear3(g, s):
                beats3.add(dve.tensor_tensor(zl3, g3[:, s, :, HD:W3], z3[:, s, :, HD:W3], ALU.add))

            def score3(g):
                beats3.wait()
                dve.tensor_tensor(score[:, :, bass.ds(g * K, K)].rearrange("p h k -> p k h"), rs3, zl3, ALU.add).then_inc(scored, 1)

            def edges3(g, s, uses):
                h, behind = s % 2, not isinstance(g, int) or g >= 2
                dve.wait_ge(rows_in["3a"][s], uses[0] * 16 + 16)
                fills3.group(g)
                for k in range(K):
                    fill(fills3, z3, hold3, g, s, k)
                    if behind and k in (1, 3):
                        relu3(g - 2, h, k // 2)
                    if behind and k == 4:
                        linear3(g - 2, (s - 2) % 4)
                    if behind and k in (5, 7):
                        reduce3(k // 2 - 2)
                fill_hold(fills3, z3, hold3, s)
                if behind:
                    score3(g - 2)
            quads(dve, edges3)
            for g in (NG - 2, NG - 1):
                relu3(g, g % 2, 0)
                relu3(g, g % 2, 1)
                linear3(g, g % 4)
                reduce3(0)
                reduce3(1)
                score3(g)
            dve.wait_ge(scored, NG)
            for s in range(4):
                dve.wait_ge(kept["3a"][s], 16 * ((NG - s + 3) // 4))

            back_tmp = area(3200, T)
            segment_totals(6, score, f3, H, "max")
            step(dve.tensor_tensor(score, score, f3, ALU.subtract))
            dve.sem_inc(soft_in, 1)
            dve.wait_ge(soft_exp, 3)
            segment_totals(8, score, f3, H, "sum")
            step(dve.tensor_scalar(f3, f3, 1e-16, None, ALU.max))
            step(dve.reciprocal(f3, f3))
            step(dve.tensor_tensor(score, score, f3, ALU.mult))
            dve.sem_inc(ended, 1)
            makes3, sums3 = Beats(dve, made3, KD), Beats(dve, work3c, K)
            dve.sem_inc(weights_set, 1)

            def sum3(g, s, uses, k):
                h = s % 2
                if k == 0:
                    sums3.group(g)
                    dve.wait_ge(heads3, g + 1)
                    need(dve, states_out[h], uses[1] * 16 + 32 * LOOPS)
                sums3.wait()
                before = st3[:, h, k - 1, :] if k else zero[:, 0:D] if isinstance(g, int) and g == 0 else st3[:, 1 - h, K - 1, :]
                sums3.add(dve.scalar_tensor_tensor(out=st3[:, h, k, :], in0=before, scalar=mark(ns, g, k),
                                                   in1=bank(h)[:, k * D:(k + 1) * D], op0=ALU.mult, op1=ALU.add))

            def edges3c(g, s, uses):
                makes3.group(g)
                dve.wait_ge(loaded[s], uses[0] * 16 + 16 * (1 + after(3, s)))
                if not isinstance(g, int) or g >= 2:
                    dve.wait_ge(heads3, g - 1)
                for k in range(K):
                    if k < KD:
                        makes3.add(dve.tensor_tensor(y3[:, s % 2, k, :].rearrange("p (h c) -> p h c", c=D),
                                                     gc3[:, s, k, 0:HD].rearrange("p (h c) -> p h c", c=D),
                                                     spread(score[:, :, bass.ds(g * K, K)][:, :, k:k + 1], P, H, D), ALU.mult))
                    if not isinstance(g, int) or g >= 2:
                        sum3(g - 2, (s - 2) % 4, before_of(g, s, uses, 2), k)
            quads(dve, edges3c)
            for g in (NG - 2, NG - 1):
                for k in range(K):
                    sum3(g, g % 4, (g // 4, g // 2), k)
            dve.wait_ge(work3c, NG * K)
            over_partitions(10, st3, D, "sum")
            dve.sem_inc(ended, 1)
            dve.wait_ge(agg_in, 16 * 7 * NT)
            step(dve.tensor_tensor(agg[:, :, :], agg[:, :, :], cg, ALU.add))
            step(dve.scalar_tensor_tensor(out=agg[:, :, :], in0=agg[:, :, :], scalar=1.0 / H, in1=hn[:, :, :], op0=ALU.mult, op1=ALU.add))
            step(dve.tensor_tensor(agg[:, :, :], agg[:, :, :], spread(row["bias_gat"].unsqueeze(1), P, NT, D), ALU.add))

            def batch_norm(n, gamma, beta):
                col = [bnv[:, k, :] for k in range(6)]

                def over_nodes(rows, use):
                    step(dve.tensor_reduce(col[0], rows.rearrange("p i c -> p c i"), AX.X, ALU.add))
                    dve.sem_inc(bn_in, 1)
                    dve.wait_ge(bn_sum, use + 1)
                over_nodes(agg[:, :, :], 2 * n)
                step(dve.tensor_scalar(col[1], bank(0)[:, 0:D], 1.0 / N, None, ALU.mult))
                step(dve.tensor_tensor(agg[:, :, :], agg[:, :, :], spread(col[1].unsqueeze(1), P, NT, D), ALU.subtract))
                step(dve.tensor_tensor(cg, agg[:, :, :], agg[:, :, :], ALU.mult))
                over_nodes(cg, 2 * n + 1)
                step(dve.tensor_scalar(col[2], bank(0)[:, 0:D], 1.0 / N, EPS, ALU.mult, ALU.add))
                dve.sem_inc(bn_var, 1)
                dve.wait_ge(bn_std, n + 1)
                step(dve.reciprocal(col[4], col[3]))
                step(dve.tensor_tensor(col[4], col[4], row[gamma], ALU.mult))
                step(dve.tensor_tensor(agg[:, :, :], agg[:, :, :], spread(col[4].unsqueeze(1), P, NT, D), ALU.mult))
                step(dve.tensor_tensor(agg[:, :, :], agg[:, :, :], spread(row[beta].unsqueeze(1), P, NT, D), ALU.add))
            batch_norm(0, "gamma1", "beta1")
            beats3n = Beats(dve, node_vec[6], 1)

            def nodes3b(b):
                beats3n.group(b)
                stage(6, b, agg).then_inc(staged, 1)
                dve.wait_ge(mixed, 30 + b + 1)
                beats3n.done(dve.tensor_tensor(red3, bank(4)[:, 0:NB * D].rearrange("p (j c) -> p j c", c=D),
                                               spread(row["b_f2"].unsqueeze(1), P, NB, D), ALU.add))
                dve.tensor_tensor(agg[:, bass.ds(b * NB, NB), :], agg[:, bass.ds(b * NB, NB), :], red3, ALU.add).then_inc(taken, 1)
            batches(dve, nodes3b)
            dve.wait_ge(taken, 7 * NBATCH)
            batch_norm(1, "gamma2", "beta2")
            tally.done(dve.tensor_tensor(xn[:, :, :], xn[:, :, :], agg[:, :, :], ALU.add), result_set)


_INS = ["x", "src", "dst", "edge_type_8", "edge_weight", "edge_weight_n2", "L0_gnn_W", "L0_gnn_b", "L0_gnn_deg_coeff",
        "L0_gnn_coeff_param", "L0_gnn_scale_param", "L1_gnn_W_self", "L1_gnn_b_self", "L1_gnn_W", "L1_gnn_att_src",
        "L1_gnn_att_dst", "L1_gnn_bias", "L2_gnn_We1", "L2_gnn_be1", "L2_gnn_We2", "L2_gnn_be2", "L2_gnn_Wn1", "L2_gnn_bn1",
        "L2_gnn_Wn2", "L2_gnn_bn2", "L3_gnn_W_l", "L3_gnn_b_l", "L3_gnn_W_r", "L3_gnn_b_r", "L3_gnn_att", "L3_gnn_bias_gat",
        "L3_gnn_gamma1", "L3_gnn_beta1", "L3_gnn_W1", "L3_gnn_b1", "L3_gnn_W2", "L3_gnn_b2", "L3_gnn_gamma2", "L3_gnn_beta2"]


def kernel(**inputs):
    import numpy as np
    import concourse.bacc as bacc
    from concourse.bass_utils import run_bass_kernel_spmd

    nc = bacc.Bacc("TRN2", target_bir_lowering=False, num_devices=1)
    arrays, args = {}, []
    for name in _INS:
        array = np.ascontiguousarray(inputs[name])
        arrays[f"in_{name}_dram"] = array
        args.append(nc.dram_tensor(f"in_{name}_dram", array.shape, mybir.dt.from_np(array.dtype), kind="ExternalInput").ap())
    args.append(nc.dram_tensor("out_0_dram", (N, D), F32, kind="ExternalOutput").ap())
    gnn_program(nc, *args)
    result = run_bass_kernel_spmd(nc, [arrays], core_ids=[0])
    return result.results[0]["out_0_dram"]
```

```python
from contextlib import ExitStack

import concourse.bass as bass
from concourse import mybir

ALU = mybir.AluOpType
ACT = mybir.ActivationFunctionType
AX = mybir.AxisListType
F32 = mybir.dt.float32
I32 = mybir.dt.int32
BF16 = mybir.dt.bfloat16

P = 128
N = 3125
NT = 25
NP = P * NT
NV = N // NT
E = 100000
K = 8
T = 784
EP = P * T
EL = E - (P - 1) * T
NG = T // K
LOOPS = NG // 2
D = 64
R = 8
H = 4
HD = H * D
HID = 128
FF = 256
NB = 5
NBATCH = NT // NB
BC = NB * P
BIG = 1.0e30
ROUND = 12582912.0
EPS = 1e-5
W = 7 * K
GW, NW = W // K, T // W
TILES = NT + 1
ROWS = TILES * P
CELLS = ROWS * NP
W1 = D + 1
W2 = HID + D
W3 = HD + H
SLOPE = 0.2

M_SRC, M_REL, M_W = 0, K, 2 * K
SPREAD = 112
STEPS3 = 7
READS3 = 3
KD = 5
AREA = 27800


class Tally:

    def __init__(self, engine):
        self.engine, self.count = engine, {}

    def done(self, instruction, semaphore):
        self.count[semaphore.name] = self.count.get(semaphore.name, 0) + 1
        instruction.then_inc(semaphore, 1)
        self.engine.wait_ge(semaphore, self.count[semaphore.name])


class Beats:

    def __init__(self, engine, semaphore, each):
        self.engine, self.semaphore, self.each, self.g, self.k = engine, semaphore, each, 0, each

    def group(self, g):
        assert self.k == self.each, (self.semaphore.name, self.k)
        self.g, self.k = g, 0

    def add(self, instruction):
        instruction.then_inc(self.semaphore, 1)
        self.k += 1

    def wait(self, back=0):
        value = self.g * self.each + (self.k - back)
        if not isinstance(value, int) or value > 0:
            self.engine.wait_ge(self.semaphore, value)

    def done(self, instruction):
        self.add(instruction)
        self.wait()


def passes(engine, body):
    for h in range(2):
        body(0, h, True)
    with engine.Fori(1, LOOPS) as i:
        for h in range(2):
            body(i, h, False)


def quads(engine, body):
    for g in range(6):
        body(g, g % 4, (g // 4, g // 2))
    with engine.Fori(0, (NG - 6) // 4) as i:
        for u in range(4):
            body(i * 4 + (6 + u), (6 + u) % 4, (i + (6 + u) // 4, i * 2 + (6 + u) // 2))


def gnn_program(nc, x, src, dst, etype, adj_v, deg_v, w0, b0, deg_coeff, coeff_param, scale_param,
                w_self, b_self, w_rel, a_src, a_dst, bias_rel, we1, be1, we2, be2, wn1, bn1, wn2, bn2,
                w_l, b_l, w_r, b_r, att, bias_gat, gamma1, beta1, w_f1, b_f1, w_f2, b_f2, gamma2, beta2,
                out):
    with ExitStack() as ctx:
        def sb(name, shape, dt=F32):
            return ctx.enter_context(nc.sbuf_tensor(name, shape, dt))

        def sem(name):
            return ctx.enter_context(nc.semaphore(name))

        def dram(name, shape):
            return nc.dram_tensor(name, shape, F32).ap()

        tab0, tab1 = dram("tab0", [NP, D]), dram("tab1", [NP * R, W1])
        weights0 = dram("weights0", [CELLS + P * W, 1])
        tab2, tab3 = dram("tab2", [NP, W2]), dram("tab3", [NP, W3])
        put1 = dram("put1", [EP + NP, 2 * R])
        put2, put3 = dram("put2", [EP + NP, HID]), dram("put3", [EP + NP, W3])
        rows1, rows2, rows3 = dram("rows1", [NP, 2 * R]), dram("rows2", [NP, HID]), dram("rows3", [NP, W3])
        spill1, spill3 = dram("spill1", [EP, W1]), dram("spill3", [EP, HD])
        state1, state2, state3 = (
            dram(f"state{n}", [EP + 1 + P, width]) for n, width in ((1, D), (2, 2 * D), (3, D)))
        betas = dram("betas", [EP + 1, 2 * R])

        meta = sb("meta", [P, NG, M_W], I32)
        ring = sb("ring", [P, GW, M_W], I32)
        ringf = ring[:, :, :].bitcast(F32)
        base_sb = sb("base", [P, NP // 4])
        base = base_sb[:, 0:T]
        etypef = sb("etypef", [P, T])
        ns = sb("ns", [P, T])
        neg = sb("neg", [P, T])
        nl = sb("nl", [P, T])
        neg_last = sb("neg_last", [P, T])
        first_last = sb("first_last", [P, T])
        score_sb = sb("score", [P, NP])
        score = score_sb[:, 0:H * T].rearrange("p (h t) -> p h t", t=T)
        dst0 = sb("dst0", [P, 1], I32)
        zidx, eidx = sb("zidx", [P, NT], I32), sb("eidx", [P, NT], I32)
        open_end = sb("open_end", [P, 1], I32)
        open_sum = sb("open_sum", [P, 2 * D])
        opened = sb("opened", [P, 4])
        nodev = sb("nodev", [P, 8, NT])
        xn, hn, agg = (sb(n, [P, NT, D]) for n in ("xn", "hn", "agg"))
        lnv = sb("lnv", [P, 4, NT])
        wh_own = sb("wh_own", [P, 4, D])
        per_dst, rnv = sb("per_dst", [P, TILES]), sb("rnv", [P, 2])
        hst = sb("hst", [P, NB, D])
        hT = sb("hT", [D, NB, P])
        ident, lower, upper, ones, valid = (sb(n, [P, P]) for n in ("ident", "lower", "upper", "ones", "valid"))
        zero = sb("zero", [P, K * W3 // 2])
        iota_row = sb("iota_row", [P, P])
        piece_row = sb("piece_row", [P, 1])
        trash = sb("trash", [P, W])
        node_trash = sb("node_trash", [P, NT])
        nhs_row, hneg_row, nhl_row = sb("nhs_row", [P, P]), sb("hneg_row", [P, P]), sb("nhl_row", [P, P])
        flags = sb("flags", [P, 2])
        tails, heads, cin = sb("tails", [P, R]), sb("heads", [P, R]), sb("cin", [P, P])
        cT = sb("cT", [P, P + 2])
        par = sb("par", [P, 16])
        sc = sb("sc", [P, 16])
        w0_sb, wself_sb, wrel_sb = sb("w0_sb", [D, 2, D]), sb("wself_sb", [D, D]), sb("wrel_sb", [D, R, D])
        we1_sb = sb("we1_sb", [D, 2, HID])
        wn1m_sb, wn1h_sb, wn2_sb = sb("wn1m_sb", [2 * D, HID]), sb("wn1h_sb", [D, HID]), sb("wn2_sb", [HID, D])
        wlr_sb = sb("wlr_sb", [D, 2, HD])
        wf1_sb, wf2_sb = sb("wf1_sb", [D, FF]), sb("wf2_sb", [P, 2, D])
        rowb = sb("rowb", [P, 3520])
        colb = sb("colb", [P, 4])
        wa = sb("wa", [D, 2, R])
        lowest = sb("lowest", [P, D])
        arena = sb("arena", [P, AREA])
        psum = ctx.enter_context(nc.psum_tensor("psum", [P, 8, 512], F32))

        def area(at, *shape):
            n = 1
            for s in shape:
                n *= s
            assert at + n <= AREA
            v = arena[:, at:at + n]
            if len(shape) == 2:
                v = v.rearrange("p (a b) -> p a b", b=shape[1])
            if len(shape) == 3:
                v = v.rearrange("p (a b c) -> p a b c", b=shape[1], c=shape[2])
            return v

        def pair(at, width):
            return area(at, 2 * K, width).rearrange("p (s k) c -> p s k c", k=K)

        def quad(at, width):
            return area(at, 4 * K, width).rearrange("p (s k) c -> p s k c", k=K)

        def bank(b, n=1):
            return psum[:, b:b + n, :].rearrange("p a b -> p (a b)")

        names = [("b0", D, b0), ("b_self", D, b_self), ("bias_rel", R * D, bias_rel), ("be1", HID, be1),
                 ("we2", HID, we2), ("bn2", D, bn2), ("b_l", HD, b_l), ("b_r", HD, b_r), ("att", HD, att),
                 ("bias_gat", D, bias_gat), ("gamma1", D, gamma1), ("beta1", D, beta1), ("gamma2", D, gamma2),
                 ("beta2", D, beta2), ("b_f2", D, b_f2), ("a_src", R * D, a_src), ("a_dst", R * D, a_dst)]
        row, row_loads, at = {}, [], 0
        for name, width, source in names:
            row[name] = rowb[:, at:at + width]
            row_loads.append((row[name], source.flatten() if len(source.shape) > 1 else source))
            at += width
        assert at <= 3520

        def over(ap, *shape):
            return ap.to_broadcast(list(shape))

        dext = area(0, T + 2)
        ints = arena[:, 800:800 + T + 2].bitcast(I32)
        srci = arena[:, 1600:1600 + T].bitcast(I32)
        typei = arena[:, 2400:2400 + T].bitcast(I32)
        adj_sb, deg_sb = area(3200, T), area(4000, T)
        tmpa, tmpb, srcf = area(4800, T), area(5600, T + 1), area(6400, T)
        pn, im = area(7200, T), area(8000, T)
        hot_p = arena[:, 8800:8800 + 2 * K * P // 2].bitcast(BF16).rearrange("p (a c) -> p a c", c=P)
        hot_i = arena[:, 9900:9900 + 2 * K * NT // 2].bitcast(BF16).rearrange("p (a c) -> p a c", c=NT)
        words0 = arena[:, 10200:10200 + NG * 2 * K].bitcast(I32).rearrange("p (g w) -> p g w", w=2 * K)
        words0f = area(10200, NG, 2 * K)
        key = area(11800, T)
        alike, alike_by = area(12800, W, W), area(16000, W, W)
        earlier = area(19328, W, W)
        merged0 = area(24460, 4, W)
        cells, per_src, whT = area(0, 4, NP), area(12800, NP), area(16000, TILES, P)

        def halves(at, n=TILES):
            return arena[:, at:at + n * P // 2].bitcast(BF16).rearrange("p (j n) -> p j n", n=P)
        high, middle, low = halves(0), halves(TILES * P // 2), halves(24460)
        high_middle, middle_high, low_high = halves(16000), halves(16000 + TILES * P // 2), halves(24460 + TILES * P // 2)
        signed = area(19328, 4, NP // 4).rearrange("p (a b) c -> p a b c", b=2)
        squares = area(19328, NP)[0:D, :]
        wh = area(22528, TILES, D)
        wh_lhs = arena[:, 24192:24192 + 2 * P].bitcast(BF16).rearrange("p (s a n) -> p s a n", a=2, n=P)
        parts0 = [hn[:, :, :].rearrange("p i c -> p (i c)")[:, 0:NP // 4], hn[:, :, :].rearrange("p i c -> p (i c)")[:, NP // 4:NP // 2],
                  base_sb[:, :]]
        per_pair = score_sb[:, :]
        total0 = agg[:, :, :].rearrange("p i c -> p (i c)")
        hst_parts = hst[:, :, :].rearrange("p j c -> p (j c)").bitcast(BF16).rearrange("p (a n) -> p a n", n=P)
        g1, ds = area(0, 2, K, W1), area(12600, T, 2 * R)
        alpha1 = score[:, 0, :]
        v1, f1 = area(0, R, T), area(6300, R, T)
        tb1 = area(0, NB, R * W1).rearrange("p j (r c) -> p j r c", c=W1)
        dn1 = area(3000, NT, 2 * R)
        dinit1 = area(3500, 2 * R)
        gc1, y1, st1 = quad(0, W1), area(2200, 4, D, K), quad(4300, D)
        run1, reset1 = area(6400, 4, D, K), area(8500, 4, D, K)
        cg = area(0, NT, D)
        beta_n = area(10600, NT, 2 * R)
        prod1 = area(2000, NB * R, D).rearrange("p (j r) c -> p j r c", r=R)
        red1 = area(4700, NB, D)
        tb2 = area(0, NB, W2)
        bn_rows = area(1000, NT, HID)
        g2, z2, hold2 = quad(0, W2), quad(6200, HID), area(10300, HID)
        pr2, e2, m2, st2 = area(10500, K, HID), area(11600, 4, K), pair(11700, D), pair(12800, 2 * D)
        agg2 = area(0, NT, 2 * D)
        mst2, mT2, hidT2 = area(6600, NB, 2 * D), area(7300, BC), area(8000, BC)
        tb3 = area(0, NB, W3)
        xr_rows = area(1400, NT, W3)
        g3, z3, hold3 = quad(0, W3), quad(8400, W3), area(16800, W3)
        pr3, rs3, zl3 = area(17100, K, HD), area(19200, K, H), area(19300, K, H)
        f3 = area(0, H, T)
        gc3, y3, st3 = quad(0, HD), pair(8400, HD), quad(12600, D)
        run3, reset3 = area(14700, 4, D, K), area(16800, 4, D, K)
        hid3 = area(1700, 2, BC)
        red3 = area(3100, NB, D)
        bnv = area(3500, 6, D)

        x_in, edges_in, params_in = sem("x_in"), sem("edges_in"), sem("params_in")
        zero0_out, zero_out, zero3_out = sem("zero0_out"), sem("zero_out"), sem("zero3_out")
        tab_out = sem("tab_out")
        rows_out = sem("rows_out")
        put_out = sem("put_out")
        hold_in = sem("hold_in")
        ring_in = {n: [sem(f"ring_in{n}_{h}") for h in range(w)] for n, w in (("0", GW), ("1a", 2), ("2", 4), ("3a", 4))}
        loaded = [sem(f"loaded{s}") for s in range(4)]
        rows_in = {n: [sem(f"rows_in{n}_{h}") for h in range(w)] for n, w in (("2", 4), ("3a", 4))}
        got = {n: [sem(f"got{n}_{h}") for h in range(w)] for n, w in (("1a", 2), ("2", 4), ("3a", 4))}
        kept = {n: [sem(f"kept{n}_{h}") for h in range(w)] for n, w in (("1a", 2), ("3a", 4))}
        states_out = [sem(f"states_out{s}") for s in range(4)]
        added = [sem(f"added{u}") for u in range(GW)]
        cells_in = [sem(f"cells_in{s}") for s in range(4)]
        ds_in, beta_out = sem("ds_in"), sem("beta_out")
        open_moved = sem("open_moved")
        agg_in = sem("agg_in")
        result_out = sem("result_out")
        padded, zeroed, consts = sem("padded"), sem("zeroed"), sem("consts")
        vec, turns = sem("vec"), sem("turns")
        plus_in, plus_out = sem("plus_in"), sem("plus_out")
        hot, counted, tallied, indices = (sem(n) for n in ("hot", "counted", "tallied", "indices"))
        to_spread, spread_up = sem("to_spread"), sem("spread_up")
        root_in, root_out = sem("root_in"), sem("root_out")
        staged, turned, lifted, mixed, taken = (sem(n) for n in ("staged", "turned", "lifted", "mixed", "taken"))
        mixed_a, taken_a = sem("mixed_a"), sem("taken_a")
        staged_m, hidden, hidden_up, lifted_m, turned_m = sem("staged_m"), sem("hidden"), sem("hidden_up"), sem("lifted_m"), sem("turned_m")
        flags_read = sem("flags_read")
        BACKWARD = (1, 3, 7, 9)
        node_vec = {n: sem(f"node_vec{n}") for n in range(1, 7)}
        norm_in, norm_out = sem("norm_in"), sem("norm_out")
        wa_set = sem("wa_set")
        merging, apart, squared, norms_up, piece_up, piece_set, turned0 = (
            sem(n) for n in ("merging", "apart", "squared", "norms_up", "piece_up", "piece_set", "turned0"))
        lhs_set, similar, signs, pairs, weighted, work0, summed0, sums_taken = (
            sem(n) for n in ("lhs_set", "similar", "signs", "pairs", "weighted", "work0", "summed0", "sums_taken"))
        taken1, made1, work1c, weights_set = sem("taken1"), sem("made1"), sem("work1c"), sem("weights_set")
        filled2, summed2, work2, gate2, made2, scan2 = (sem(n) for n in ("filled2", "summed2", "work2", "gate2", "made2", "scan2"))
        filled3, summed3, work3, scored = (sem(n) for n in ("filled3", "summed3", "work3", "scored"))
        made3, made3b, heads3, work3c = sem("made3"), sem("made3b"), sem("heads3"), sem("work3c")
        resets, state_rows = sem("resets"), sem("state_rows")
        ended = sem("ended")
        soft_in, soft_exp = sem("soft_in"), sem("soft_exp")
        c_tail, c_turn, c_scan, c_back, c_in = (sem(n) for n in ("c_tail", "c_turn", "c_scan", "c_back", "c_in"))
        result_set = sem("result_set")

        ZEROS = 7 + 2 * NW

        def need(engine, semaphore, value):
            if not isinstance(value, int) or value > 0:
                engine.wait_ge(semaphore, value)

        def groups_at(s):
            return (NG - s + 3) // 4

        def after(n, s):
            return groups_at(s) if n == 3 else 0

        def tiles(engine, body):
            for j in range(6):
                body(j, j % 4, j // 4)
            with engine.Fori(0, (TILES - 6) // 4) as i:
                for u in range(4):
                    body(i * 4 + (6 + u), (6 + u) % 4, i + (6 + u) // 4)

        def late(j, n):
            return not isinstance(j, int) or j >= n

        def before_of(g, s, uses, back=1):
            if isinstance(g, int):
                return (g - back) // 4, (g - back) // 2
            return uses[0] - (1 if s < back else 0), uses[1] - (back + 1 - s % 2) // 2

        def batches(engine, body):
            body(0)
            with engine.Fori(1, NBATCH) as b:
                body(b)

        def parts(s):
            return ((0, 3, mixed_a, taken_a, {1: 0, 2: 5, 5: 10}[s]), (3, NB, mixed, taken, 5 * s))

        def batches_ahead(engine, prepare, body, early=False, finish=None):
            def one(b, more):
                if more and early:
                    prepare(b + 1)
                body(b)
                if more and not early:
                    prepare(b + 1)
                if finish:
                    finish(b)
            prepare(0)
            one(0, True)
            with engine.Fori(1, NBATCH - 1) as b:
                one(b, True)
            one(NBATCH - 1, False)

        by_node = "(p i) c -> p i c"
        by_edge = "(p t) c -> p t c"

        def group_rows(table, g, groups=1):
            return table[0:EP, :].rearrange(by_edge, t=T)[:, bass.ds(g * K, groups * K), :]

        def states_before(n, s):
            return groups_at(s) * (n if s % 2 == 0 else n // 2)

        def clear(engine, table, count, width, semaphore):
            engine.dma_start(table.rearrange("p (n w) -> p n w", w=width),
                             over(zero[:, 0:width].unsqueeze(1), P, count, width)).then_inc(semaphore, 16)

        block = ctx.enter_context(nc.Block())

        @block.sync
        def _(sp):
            sp.wait_ge(padded, 6)
            def edge_load(tile, array):
                for lo, hi in ((0, SPREAD), (SPREAD, P - 1)):
                    sp.dma_start(tile[lo:hi, 0:T], array[lo * T:hi * T].rearrange("(p t) -> p t", t=T)).then_inc(edges_in, 16)
                sp.dma_start(tile[P - 1:P, 0:EL], array[EP - T:E].unsqueeze(0)).then_inc(edges_in, 16)
            edge_load(ints[:, 1:T + 1], dst)
            with nc.allow_non_contiguous_dma(reason="one neighbour of each partition's edges"):
                sp.dma_start(ints[1:P, 0:1], dst[T - 1::T].unsqueeze(1)).then_inc(edges_in, 16)
                sp.dma_start(ints[0:P - 1, T + 1:T + 2], dst[T::T].unsqueeze(1)).then_inc(edges_in, 16)
            for tile, array in ((srci, src), (typei, etype), (adj_sb, adj_v), (deg_sb, deg_v)):
                edge_load(tile, array)
            for at, array in ((0, deg_coeff), (2, coeff_param), (5, scale_param), (6, be2)):
                sp.dma_start(par[:, at:at + array.shape[0]], array.partition_broadcast(P)).then_inc(edges_in, 16)
            sp.wait_ge(zeroed, 2)
            table = weights0.rearrange("e c -> (e c)")
            clear(sp, table[0:CELLS].rearrange("(p t) -> p t", p=P), CELLS // P // 1040, 1040, zero0_out)
            clear(sp, table[CELLS:].rearrange("(p t) -> p t", p=P), 1, W, zero0_out)

            sp.wait_ge(padded, 7)
            sp.dma_start(xn[0:NV, :, :], x.rearrange(by_node, i=NT)).then_inc(x_in, 16)
            for tile, array in ((w0_sb[:, 0, :], w0), (w0_sb[:, 1, :], w0), (wself_sb[:, :], w_self), (wn1m_sb[0:D, :], wn1[D:2 * D, :]), (wn1m_sb[D:2 * D, :], wn1[0:D, :]), (wn1h_sb[:, :], wn1[2 * D:, :]),
                                (wn2_sb[:, :], wn2), (wf1_sb[:, :], w_f1)):
                sp.dma_start(tile, array).then_inc(params_in, 16)
            sp.dma_start(wrel_sb[:, :, :], w_rel.rearrange("r d f -> d r f")).then_inc(params_in, 16)
            sp.dma_start(we1_sb[:, :, :], we1.rearrange("(a d) f -> d a f", a=2)).then_inc(params_in, 16)
            sp.dma_start(wf2_sb[:, :, :], w_f2.rearrange("(a d) f -> d a f", a=2)).then_inc(params_in, 16)
            sp.dma_start(wlr_sb[:, 0, :], w_l).then_inc(params_in, 16)
            sp.dma_start(wlr_sb[:, 1, :], w_r).then_inc(params_in, 16)
            for tile, array in row_loads:
                sp.dma_start(tile, array.partition_broadcast(P)).then_inc(params_in, 16)
            with nc.allow_non_contiguous_dma(reason="bias columns"):
                sp.dma_start(colb[:, 0:1], bn1.unsqueeze(1)).then_inc(params_in, 16)
                sp.dma_start(colb[:, 1:3], b_f1.rearrange("(a p) -> p a", a=2)).then_inc(params_in, 16)
                for half in range(2):
                    sp.dma_start(colb[half * D:(half + 1) * D, 3:4], b0.unsqueeze(1)).then_inc(params_in, 16)

            def ring_load(n, g, s, *used):
                for semaphore, value in used:
                    need(sp, semaphore, value)
                sp.dma_start(ring[:, s, :], meta[:, bass.ds(g, 1), :].rearrange("p a w -> p (a w)")).then_inc(ring_in[n][s], 16)

            def load0(w):
                sp.wait_ge(merging, w * 8 + 8)
                for u in range(GW):
                    if late(w, 1):
                        sp.wait_ge(added[u], w * 16 * K)
                    sp.dma_start(ring[:, u, :], words0[:, bass.ds(w * GW + u, 1), :].rearrange("p a w -> p (a w)")).then_inc(ring_in["0"][u], 16)
            load0(0)
            with sp.Fori(1, NW) as w:
                load0(w)
            for u in range(GW):
                sp.wait_ge(added[u], NW * 16 * K)
            sp.wait_ge(indices, 1)

            def load_cells(j, s, uses):
                if late(j, 4):
                    sp.wait_ge(summed0, j - 3)
                sp.dma_start(cells[:, s, :], weights0[0:CELLS, :].rearrange("(r n) c -> r (n c)", n=NP)[bass.ds(j * P, P), :]
                             ).then_inc(cells_in[s], 16)
            tiles(sp, load_cells)

            def table1(b):
                sp.wait_ge(taken, 5 + b + 1)
                sp.sem_inc(turns, 1)
                sp.dma_start(tab1.rearrange("(p i r) c -> p i r c", i=NT, r=R)[:, bass.ds(b * NB, NB), :, :], tb1).then_inc(tab_out, 16)
            batches(sp, table1)
            sp.wait_ge(taken, 2 * NBATCH)
            sp.dma_start(rows1.rearrange(by_node, i=NT), dn1).then_inc(rows_out, 16)
            sp.wait_ge(put_out, 16 * 1 * NT)
            sp.dma_start(ds, put1[0:EP, :].rearrange(by_edge, t=T)).then_inc(ds_in, 16)

            def load1a(i, h, first):
                g = i * 2 + h
                ring_load("1a", g, h, *(() if first else ((got["1a"][h], i * 16 * K),)))
            passes(sp, load1a)
            sp.wait_ge(soft_exp, 3)
            sp.dma_start(betas[0:EP, :].rearrange(by_edge, t=T), ds).then_inc(beta_out, 16)
            sp.wait_ge(weights_set, 1)

            def load1c(g, s, uses):
                if not isinstance(g, int) or g >= 4:
                    sp.wait_ge(made1, g - 3)
                sp.dma_start(gc1[:, s, :, :], group_rows(spill1, g)).then_inc(loaded[s], 16)
            quads(sp, load1c)


            def table2(b):
                sp.wait_ge(taken, 15 + b + 1)
                sp.sem_inc(turns, 1)
                sp.dma_start(tab2.rearrange(by_node, i=NT)[:, bass.ds(b * NB, NB), :], tb2).then_inc(tab_out, 16)
            batches(sp, table2)
            sp.dma_start(rows2.rearrange(by_node, i=NT), bn_rows).then_inc(rows_out, 16)
            sp.wait_ge(put_out, 16 * 2 * NT)
            sp.wait_ge(rows_out, 16 * 2)

            def load_group(n, put_rows, rows, filled_to, summed, g, s, uses):
                again = not isinstance(g, int) or g >= 4
                ring_load(n, g, s, *(((got[n][s], uses[0] * 16 * K),) if again else ()))
                if again:
                    sp.wait_ge(filled_to, (g - 3) * K + 1)
                    sp.wait_ge(summed, g - 3)
                    if n == "3a":
                        sp.wait_ge(work3, (g - 4) * STEPS3 + READS3)
                sp.dma_start(rows[:, s, :, :], group_rows(put_rows, g)).then_inc(rows_in[n][s], 16)
            quads(sp, lambda g, s, uses: load_group("2", put2, z2, filled2, summed2, g, s, uses))

            def table3(b):
                sp.wait_ge(taken, 25 + b + 1)
                sp.sem_inc(turns, 1)
                sp.dma_start(tab3.rearrange(by_node, i=NT)[:, bass.ds(b * NB, NB), :], tb3).then_inc(tab_out, 16)
            batches(sp, table3)
            sp.dma_start(rows3.rearrange(by_node, i=NT), xr_rows).then_inc(rows_out, 16)
            sp.wait_ge(put_out, 16 * 3 * NT)
            sp.wait_ge(rows_out, 16 * 3)

            quads(sp, lambda g, s, uses: load_group("3a", put3, z3, filled3, summed3, g, s, uses))

            def load3c(g, s, uses):
                if not isinstance(g, int) or g >= 4:
                    sp.wait_ge(made3, (g - 3) * KD)
                    sp.wait_ge(made3b, g - 3)
                sp.dma_start(gc3[:, s, :, :], group_rows(spill3, g)).then_inc(loaded[s], 16)
            sp.wait_ge(ended, 3)
            quads(sp, load3c)
            sp.wait_ge(result_set, 1)
            for lo, hi in ((0, SPREAD), (SPREAD, NV)):
                sp.dma_start(out.rearrange(by_node, i=NT)[lo:hi, :, :], xn[lo:hi, :, :]).then_inc(result_out, 16)
            sp.wait_ge(result_out, 32)

        @block.gpsimd
        def _(pool):
            tally = Tally(pool)
            tally.done(pool.memset(ones[:, :], 1.0), consts)
            tally.done(pool.memset(ident[:, :], 0.0), consts)
            tally.done(pool.affine_select(out=ident[:, :], in_=ident[:, :], compare_op=ALU.not_equal, fill=1.0, base=0,
                                          pattern=[[-1, P]], channel_multiplier=1), consts)
            tally.done(pool.affine_select(out=lower[:, :], in_=ones[:, :], compare_op=ALU.is_gt, fill=0.0, base=0,
                                          pattern=[[-1, P]], channel_multiplier=1), consts)
            tally.done(pool.affine_select(out=upper[:, :], in_=ones[:, :], compare_op=ALU.is_gt, fill=0.0, base=0,
                                          pattern=[[1, P]], channel_multiplier=-1), consts)
            tally.done(pool.affine_select(out=valid[:, :], in_=ones[:, :], compare_op=ALU.is_ge, fill=0.0, base=NV - 1,
                                          pattern=[[0, P]], channel_multiplier=-1), consts)
            tally.done(pool.iota(iota_row[:, :], pattern=[[1, P]], base=0, channel_multiplier=0,
                                 allow_small_or_imprecise_dtypes=True), consts)
            tally.done(pool.iota(piece_row[:, :], pattern=[[1, 1]], base=NP, channel_multiplier=1,
                                 allow_small_or_imprecise_dtypes=True), consts)
            tally.done(pool.iota(trash[:, :], pattern=[[1, W]], base=CELLS, channel_multiplier=W,
                                 allow_small_or_imprecise_dtypes=True), consts)
            tally.done(pool.memset(earlier, 1.0), consts)
            tally.done(pool.affine_select(out=earlier, in_=earlier, compare_op=ALU.is_gt, fill=0.0, base=0,
                                          pattern=[[1, W], [-1, W]], channel_multiplier=0), consts)
            tally.done(pool.iota(node_trash[:, :], pattern=[[1, NT]], base=EP, channel_multiplier=NT,
                                 allow_small_or_imprecise_dtypes=True), consts)

            def ready(*waits):
                for semaphore, value in waits:
                    need(pool, semaphore, value)
                pool.sem_inc(turns, 1)

            def put(n, table, rows, batch=None):
                for i in range(NT) if batch is None else range(batch * NB, batch * NB + NB):
                    pool.indirect_dma_start(out=table[:, :], out_offset=bass.IndirectOffsetOnAxis(ap=zidx[:, i:i + 1], axis=0),
                                            in_=rows[:, i, :], in_offset=None).then_inc(put_out, 16)

            def hold(n, table, rows):
                pool.indirect_dma_start(out=rows, out_offset=None, in_=table[:, :],
                                        in_offset=bass.IndirectOffsetOnAxis(ap=dst0[:, :], axis=0)).then_inc(hold_in, 16)

            def gather(n, table, rows, word, h):
                for k in range(K):
                    pool.indirect_dma_start(out=rows[:, h, k, :], out_offset=None, in_=table[:, :],
                                            in_offset=bass.IndirectOffsetOnAxis(ap=ring[:, h, word + k:word + k + 1], axis=0)
                                            ).then_inc(got[n][h], 16)

            def whole_segments(n, table, use, rows):
                last = bass.IndirectOffsetOnAxis(ap=open_end[:, :], axis=0)
                ready(*((states_out[s], 16 * states_before(n, s)) for s in range(4)))
                pool.indirect_dma_start(out=rows, out_offset=None, in_=table[:, :], in_offset=last).then_inc(open_moved, 16)
                ready((ended, use))
                pool.indirect_dma_start(out=table[:, :], out_offset=last, in_=rows, in_offset=None).then_inc(open_moved, 16)
                ready((open_moved, 32 * n))

            def collect(n, table, index, rows, before=None):
                for i in range(NT):
                    if before is not None and i and i % NB == 0:
                        ready((agg_in, 16 * (before + i)))
                    pool.indirect_dma_start(out=rows[:, i, :], out_offset=None, in_=table[:, :],
                                            in_offset=bass.IndirectOffsetOnAxis(ap=index[:, i:i + 1], axis=0)).then_inc(agg_in, 16)

            def add0(w):
                for u in range(GW):
                    before = [(added[v], w * 16 * K) for v in range(GW)] if u == 0 and late(w, 1) else []
                    ready((ring_in["0"][u], w * 16 + 16), *before)
                    for k in range(K):
                        pool.indirect_dma_start(out=weights0[:, :], out_offset=bass.IndirectOffsetOnAxis(ap=ring[:, u, k:k + 1], axis=0),
                                                in_=ringf[:, u, K + k:K + k + 1], in_offset=None, compute_op=ALU.add).then_inc(added[u], 16)
            pool.wait_ge(zero0_out, 32)
            add0(0)
            with pool.Fori(1, NW) as w:
                add0(w)
            ready((tab_out, 16))
            hold(0, tab0, wh[:, NT, :])

            def weigh(j, s, uses):
                pool.wait_ge(cells_in[s], uses * 16 + 16)
                pool.wait_ge(pairs, j + 1)
                pool.tensor_tensor(cells[:, s, :], cells[:, s, :], per_pair, ALU.mult).then_inc(weighted, 1)
            tiles(pool, weigh)

            for b in range(NBATCH):
                ready((taken, 5 + b + 1), *(((zero_out, 16 * ZEROS),) if b == 0 else ()))
                put(1, put1, dn1, b)
            ready((rows_out, 16 * 1))
            hold(1, rows1, dinit1)
            ready((tab_out, 16 * (1 + 1 * NBATCH)))

            def gather1(i, h, first):
                g = i * 2 + h
                ready((ring_in["1a"][h], i * 16 + 16), *(() if first else ((taken1, g - 1), (kept["1a"][h], i * 16))))
                gather("1a", tab1, g1, M_REL, h)
            passes(pool, gather1)
            pool.wait_ge(weights_set, 1)

            def messages1(g, s, uses):
                ready((loaded[s], uses[0] * 16 + 16), *(((work1c, (g - 3) * 2),) if late(g, 4) else ()))
                pool.tensor_tensor(y1[:, s, :, :].rearrange("p d k -> p k d"), gc1[:, s, :, 0:D],
                                   over(alpha1[:, bass.ds(g * K, K)].unsqueeze(2), P, K, D), ALU.mult).then_inc(made1, 1)
            quads(pool, messages1)
            whole_segments(1, state1, 1, open_sum[:, 0:D])
            ready((beta_out, 16))
            collect(1, betas, eidx, beta_n, before=0)
            ready((agg_in, 16 * NT))
            collect(1, state1, eidx, agg)

            for b in range(NBATCH):
                ready((taken, 15 + b + 1))
                put(2, put2, bn_rows, b)
            ready((rows_out, 16 * 2), (tab_out, 16 * (1 + 2 * NBATCH)), (put_out, 16 * 2 * NT))
            hold(2, rows2, hold2)

            def gather2(g, s, uses):
                ready((ring_in["2"][s], uses[0] * 16 + 16),
                      *(((summed2, g - 3), (made2, g - 3)) if not isinstance(g, int) or g >= 4 else ()))
                gather("2", tab2, g2, M_SRC, s)
            quads(pool, gather2)
            whole_segments(2, state2, 2, open_sum[:, 0:2 * D])
            collect(2, state2, eidx, agg2, before=2 * NT)

            for b in range(NBATCH):
                ready((taken, 25 + b + 1), *(((zero3_out, 16 * NG),) if b == 0 else ()))
                put(3, put3, xr_rows, b)
            ready((rows_out, 16 * 3), (tab_out, 16 * (1 + 3 * NBATCH)), (put_out, 16 * 3 * NT))
            hold(3, rows3, hold3)

            def gather3(g, s, uses):
                ready((ring_in["3a"][s], uses[0] * 16 + 16),
                      *(((summed3, g - 3), (work3, (g - 4) * STEPS3 + READS3), (kept["3a"][s], uses[0] * 16)) if not isinstance(g, int) or g >= 4 else ()))
                gather("3a", tab3, g3, M_SRC, s)
            quads(pool, gather3)
            pool.wait_ge(weights_set, 2)

            def messages3(g, s, uses):
                ready((loaded[s], uses[0] * 16 + 16 * (1 + after(3, s))), *(((heads3, g - 1),) if late(g, 2) else ()))
                for k in range(KD, K):
                    message = pool.tensor_tensor(y3[:, s % 2, k, :].rearrange("p (h c) -> p h c", c=D),
                                                 gc3[:, s, k, 0:HD].rearrange("p (h c) -> p h c", c=D),
                                                 over(score[:, :, bass.ds(g * K, K)][:, :, k:k + 1], P, H, D), ALU.mult)
                message.then_inc(made3b, 1)
            quads(pool, messages3)
            whole_segments(3, state3, 4, open_sum[:, 0:D])
            collect(3, state3, eidx, agg)

        PARAMS = 16 * (7 + 5 + len(row_loads) + 5)

        @block.scalar
        def _(act):
            act.wait_ge(zeroed, 2)
            for table in (state1, state2, state3):
                act.dma_start(table[EP:EP + P, :], zero[:, 0:table.shape[1]]).then_inc(zero_out, 16)
                act.dma_start(table[EP + P:, :], zero[0:1, 0:table.shape[1]]).then_inc(zero_out, 16)
            act.wait_ge(consts, 1)
            act.dma_start(betas[EP:EP + 1, :], ones[0:1, 0:2 * R]).then_inc(zero_out, 16)

            for n, ax in ((0, tmpb[:, 0:T]), (1, sc[:, 1:2])):
                act.wait_ge(plus_in, n + 1)
                act.activation(ax, ax, ACT.Exp, scale=-1.0).then_inc(plus_out, 1)
                act.wait_ge(plus_out, 2 * n + 1)
                act.activation(ax, ax, ACT.Ln, bias=1.0).then_inc(plus_out, 1)
            act.wait_ge(plus_in, 3)
            act.activation(sc[:, 4:7], sc[:, 4:7], ACT.Exp).then_inc(plus_out, 1)

            def deviation(n):
                act.wait_ge(root_in, n + 1)
                act.activation(lnv[:, 2, :], lnv[:, 1, :], ACT.Sqrt).then_inc(root_out, 1)

            def lift(s, b, read=None):
                act.wait_ge(turned, 5 * s + b + 1)
                if read is None or isinstance(b, int) and b == 0:
                    need(act, mixed, 5 * s + b)
                else:
                    act.wait_ge(hidden, read)
                act.activation(hT[:, :, :], bank(6, 2)[0:D, 0:BC].rearrange("d (j n) -> d j n", n=P), ACT.Copy).then_inc(lifted, 1)

            def lift_only(s):
                batches(act, lambda b: lift(s, b))

            deviation(0)
            lift_only(0)
            act.wait_ge(norm_in, 1)
            act.activation(lnv[:, 1, :], lnv[:, 0, :], ACT.Sqrt).then_inc(norm_out, 1)
            act.dma_start(tab0.rearrange(by_node, i=NT), wh[:, 0:NT, :]).then_inc(tab_out, 16)
            act.wait_ge(norms_up, 1)
            act.activation(per_src, bank(0, 7)[:, 0:NP], ACT.Sqrt).then_inc(norm_out, 1)

            def clear_columns(table, at, columns, parts, semaphore):
                act.dma_start(table[0:EP, :].rearrange(by_edge, t=T)[:, bass.ds(at, columns), :].rearrange("p t c -> p (t c)").rearrange("p (n w) -> p n w", n=parts),
                              over(zero[:, 0:columns * table.shape[1] // parts].unsqueeze(1), P, parts, columns * table.shape[1] // parts)).then_inc(semaphore, 16)

            def clear_window(w):
                act.wait_ge(added[GW - 1], w * 16 * K + 16 * K)
                clear_columns(put1, w * W, W, 1, zero_out)
                clear_columns(put2, w * W, W, GW, zero_out)
            clear_window(0)
            with act.Fori(1, NW) as w:
                clear_window(w)
            act.wait_ge(norm_in, 2)
            act.activation(rnv[:, 1:2], rnv[:, 0:1], ACT.Sqrt).then_inc(norm_out, 1)

            act.wait_ge(piece_set, 1)

            def sign(j, s, uses):
                if late(j, 2):
                    act.wait_ge(similar, (j - 1) * 4)
                act.sem_inc(turns, 1)
                own = wh_lhs[:, s % 2, :, :]
                act.activation(own[:, 0, :], high_middle[:, bass.ds(j, 1), :].rearrange("p a n -> p (a n)"), ACT.Copy)
                act.activation(own[0:D, 1, :], high_middle[0:D, bass.ds(j, 1), :].rearrange("p a n -> p (a n)"), ACT.Copy)
                act.activation(own[D:P, 1, :], low[D:P, bass.ds(j, 1), :].rearrange("p a n -> p (a n)"), ACT.Copy)
                act.activation(wh_own[:, s, :], wh[:, bass.ds(j, 1), :].rearrange("p a c -> p (a c)"), ACT.Copy).then_inc(lhs_set, 1)
                for c in range(4):
                    act.wait_ge(similar, j * 4 + c + 1)
                    if c > 1 or late(j, 1):
                        act.wait_ge(work0, j * 8 + (-4, -2, 1, 2)[c])
                    dots = psum[:, 4 + c % 2 * 2:6 + c % 2 * 2, 0:NP // 8]
                    act.activation(signed[:, c % 2, 0, :].rearrange("p (b n) -> p b n", b=2), dots, ACT.Relu, scale=sc[:, 4:5])
                    act.activation(signed[:, c % 2, 1, :].rearrange("p (b n) -> p b n", b=2), dots, ACT.Relu, scale=sc[:, 9:10]).then_inc(signs, 1)
            tiles(act, sign)

            deviation(1)
            lift_only(1)

            def keep1a(i, h, first):
                act.wait_ge(got["1a"][h], i * 16 * K + 16 * K)
                act.dma_start(group_rows(spill1, i * 2 + h), g1[:, h, :, :]).then_inc(kept["1a"][h], 16)
                clear_columns(put3, (i * 2 + h) * K, K, 2, zero3_out)
            passes(act, keep1a)
            for h in range(2):
                act.wait_ge(kept["1a"][h], 16 * LOOPS)
            act.wait_ge(soft_in, 1)
            act.activation(v1, v1, ACT.Exp).then_inc(soft_exp, 1)
            act.wait_ge(soft_in, 2)
            act.activation(ds[:, :, R:2 * R], ds[:, :, R:2 * R], ACT.Exp).then_inc(soft_exp, 1)
            act.wait_ge(soft_in, 3)
            act.activation(ds[:, :, 0:R], f1.rearrange("p r t -> p t r"), ACT.Copy).then_inc(soft_exp, 1)

            def keep_states(use, work, run, table, rows, g, s, uses):
                act.wait_ge(work, g * 2 + 4)
                need(act, states_out[s], (uses[0] + states_before(2 * use, s)) * 16)
                act.activation(rows[:, s:s + 2, :, :], run[:, s:s + 2, :, :].rearrange("p a d k -> p a k d"), ACT.Copy).then_inc(state_rows, 1)
                act.wait_ge(state_rows, uses[1] + (1 + NG // 2 * use))
                act.dma_start(group_rows(table, g, 2), rows[:, s:s + 2, :, :].rearrange("p a k d -> p (a k) d")).then_inc(states_out[s], 16)

            def pass_sums(use, work, run, reset, table, rows):
                def marks_and_states(g, s, uses):
                    if s % 2:
                        return
                    if late(g, 4):
                        act.wait_ge(work, (g - 2) * 2)
                    marks = ns[:, bass.ds(g * K, 2 * K)].rearrange("p (a k) -> p a k", k=K)[:, :, 1:K]
                    act.activation(reset[:, s:s + 2, :, 1:K], over(marks.unsqueeze(2), P, 2, D, K - 1), ACT.Copy).then_inc(resets, 1)
                    if late(g, 2):
                        keep_states(use, work, run, table, rows, g - 2, (s - 2) % 4, before_of(g, s, uses, 2))
                act.wait_ge(weights_set, use + 1)
                quads(act, marks_and_states)
                keep_states(use, work, run, table, rows, NG - 2, (NG - 2) % 4, ((NG - 2) // 4, (NG - 2) // 2))
            pass_sums(0, work1c, run1, reset1, state1, st1)
            lift_only(2)

            deviation(2)
            lift_only(3)

            def keep2(g, s):
                act.wait_ge(scan2, g * 2 * K + 2 * K)
                act.dma_start(group_rows(state2, g), st2[:, s % 2, :, :]).then_inc(states_out[s], 16)

            def gate(g, s, uses):
                h = s % 2
                if not isinstance(g, int) or g >= 2:
                    keep2(g - 2, (s - 2) % 4)
                act.wait_ge(work2, g * 2 + 2)
                act.activation(e2[:, 2 + h, :], e2[:, h, :], ACT.Sigmoid, bias=par[:, 6:7]).then_inc(gate2, 1)
                act.wait_ge(gate2, g + 1)
                for k in range(K):
                    message = act.activation(m2[:, h, k, :], g2[:, s, k, HID:W2], ACT.Copy, scale=e2[:, 2 + h, k:k + 1])
                message.then_inc(made2, 1)
            quads(act, gate)
            keep2(NG - 2, (NG - 2) % 4)
            keep2(NG - 1, (NG - 1) % 4)

            def lift2(b):
                lift(4, b, read=b)
                act.wait_ge(turned_m, b + 1)
                act.activation(mT2, bank(4, 2)[:, 0:BC], ACT.Copy).then_inc(lifted_m, 1)
                act.wait_ge(hidden, b + 1)
                act.wait_ge(mixed, 20 + b)
                act.activation(hidT2, bank(0, 2)[:, 0:BC], ACT.Relu, bias=colb[:, 0:1]).then_inc(hidden_up, 1)
            batches(act, lift2)

            deviation(3)
            lift_only(5)

            def keep3a(g, s, uses):
                act.wait_ge(got["3a"][s], uses[0] * 16 * K + 16 * K)
                act.dma_start(group_rows(spill3, g), g3[:, s, :, 0:HD]).then_inc(kept["3a"][s], 16)
            quads(act, keep3a)
            for s in range(4):
                act.wait_ge(kept["3a"][s], 16 * ((NG - s + 3) // 4))
            act.wait_ge(soft_in, 4)
            act.activation(score[:, :, :], score[:, :, :], ACT.Exp).then_inc(soft_exp, 1)

            pass_sums(1, work3c, run3, reset3, state3, st3)
            act.wait_ge(root_in, 5)
            act.activation(bnv[:, 3, :], bnv[:, 2, :], ACT.Sqrt).then_inc(root_out, 1)

            def lift3(b):
                lift(6, b, read=NBATCH + 2 * b)
                act.wait_ge(mixed, 30 + b)
                for c in range(2):
                    act.wait_ge(hidden, NBATCH + 2 * b + c + 1)
                    act.activation(hid3[:, c, :], bank(2 * c, 2)[:, 0:BC], ACT.Relu, bias=colb[:, 1 + c:2 + c]).then_inc(hidden_up, 1)
            batches(act, lift3)
            act.wait_ge(root_in, 6)
            act.activation(bnv[:, 3, :], bnv[:, 2, :], ACT.Sqrt).then_inc(root_out, 1)

        @block.tensor
        def _(pe):
            pe.wait_ge(consts, 9)
            pe.wait_ge(params_in, PARAMS)

            def turn(s, b):
                pe.wait_ge(staged, 5 * s + b + 1)
                need(pe, lifted, 5 * s + b)
                pe.sem_inc(turns, 1)
                for j in range(NB):
                    mm = pe.transpose(bank(6, 2)[0:D, j * P:(j + 1) * P], hst[:, j, :], ident[:, :])
                mm.then_inc(turned, 1)

            def products(s, body, finish=None):
                batches_ahead(pe, lambda b: turn(s, b), body, finish=finish)

            def mix(s, b, main, narrow=None, cut=True):
                pe.wait_ge(lifted, 5 * s + b + 1)

                def product(j, at, rhs):
                    width = rhs.shape[1]
                    return pe.matmul(bank(0, 6)[:, at + j * width:at + (j + 1) * width], lhsT=hT[:, j, :], rhs=rhs, start=True, stop=True)
                for lo, hi, done, used, base in parts(s) if cut else ((0, NB, mixed, taken, 5 * s),):
                    need(pe, used, base + b)
                    if narrow is not None and lo == 0:
                        for j in range(NB):
                            product(j, 5 * 512, narrow)
                    for j in range(lo, hi):
                        mm = product(j, 0, main)
                    mm.then_inc(done, 1)

            def spread(column, b, at):
                return pe.matmul(bank(b)[:, at:at + P], lhsT=over(column, P, P), rhs=ident[:, :], start=True, stop=True)

            def carry(use, tail, width):
                pe.wait_ge(c_tail, use + 1)
                pe.transpose(bank(0)[0:width, 0:P], tail, ident[:, :]).then_inc(c_turn, 1)
                pe.wait_ge(c_scan, use + 1)
                pe.transpose(bank(1)[:, 0:width], cT[0:width, 1:P + 1] if use in BACKWARD else cT[0:width, 0:P],
                             ident[0:width, 0:width]).then_inc(c_back, 1)

            def rows0(b):
                pe.wait_ge(lifted, b + 1)
                need(pe, taken, b)
                for j in range(NB):
                    pe.matmul(bank(0)[:, j * D:(j + 1) * D], lhsT=hT[:, j, :], rhs=w0_sb[:, 0, :], start=True, stop=True)
                for lo, hi in ((0, 512), (512, BC)):
                    mm = pe.matmul(bank(2, 2)[:, lo:hi], lhsT=w0_sb[:, :, :].rearrange("d a f -> d (a f)"), rhs=hT[:, :, :].rearrange("d j n -> d (j n)")[:, lo:hi],
                                   start=True, stop=True)
                mm.then_inc(mixed, 1)
            products(0, rows0)
            pe.wait_ge(squared, 1)
            for at in range(0, NP, 512):
                mm = pe.matmul(bank(at // 512)[:, 0:min(512, NP - at)], lhsT=ones[0:D, :], rhs=squares[:, at:min(at + 512, NP)],
                               start=True, stop=True)
            mm.then_inc(norms_up, 1)
            pe.wait_ge(norm_out, 2)

            pe.wait_ge(taken, NBATCH)

            def count(i, h, first):
                g = i * 2 + h
                pe.wait_ge(hot, i * 4 + 2 * h + 2)
                if not first:
                    pe.wait_ge(tallied, g)
                for k in range(K):
                    mm = pe.matmul(bank(h)[:, 0:NT], lhsT=hot_p[:, h * K + k, :], rhs=hot_i[:, h * K + k, :], start=(k == 0),
                                   stop=(k == K - 1))
                mm.then_inc(counted, 1)
            passes(pe, count)
            pe.wait_ge(to_spread, 3)
            pe.matmul(bank(1)[:, 0:1], lhsT=upper[:, :], rhs=nodev[:, 1, NT - 1:NT], start=True, stop=True).then_inc(spread_up, 1)
            spread(flags[:, 0:1], 2, 0).then_inc(spread_up, 1)
            spread(flags[:, 1:2], 2, P).then_inc(spread_up, 1)

            pe.wait_ge(flags_read, 3)
            pe.wait_ge(piece_up, 2)
            pe.transpose(bank(7)[:, 0:P], cin[:, :], ident[:, :]).then_inc(turned0, 1)
            pe.wait_ge(piece_set, 1)

            def sum_up(j, s, uses):
                pe.wait_ge(work0, j * 8 + 8)
                if s % 2 == 0 and late(j, 2):
                    pe.wait_ge(sums_taken, uses * 2 + s // 2)
                for c in range(8):
                    mm = pe.matmul(bank(c % 4)[c // 4 * D:(c // 4 + 1) * D, 0:NP // 8], lhsT=wh_own[:, s, :],
                                   rhs=cells[:, s, c * NP // 8:(c + 1) * NP // 8], start=(s % 2 == 0), stop=(s % 2 == 1))
                mm.then_inc(summed0, 1)

            def dots0(j, s, uses):
                pe.wait_ge(lhs_set, j + 1)
                for c in range(4):
                    if late(j * 4 + c, 2):
                        pe.wait_ge(signs, j * 4 + c - 1)
                    for half in range(2):
                        at = (2 * c + half) * NP // 8
                        for n, (own, rows) in enumerate(((0, high_middle), (0, middle_high), (1, low_high))):
                            mm = pe.matmul(bank(4 + c % 2 * 2 + half)[:, 0:NP // 8], lhsT=wh_lhs[:, s % 2, own, :],
                                           rhs=rows[:, 0:NT, :].rearrange("p j n -> p (j n)")[:, at:at + NP // 8],
                                           start=(n == 0), stop=(n == 2))
                    mm.then_inc(similar, 1)
                if late(j, 1):
                    sum_up(j - 1, (s - 1) % 4, (j - 1) // 4 if isinstance(j, int) else uses - (1 if s == 0 else 0))
            tiles(pe, dots0)
            sum_up(TILES - 1, (TILES - 1) % 4, (TILES - 1) // 4)
            pe.wait_ge(sums_taken, TILES // 2)
            for half in range(2):
                side, first = slice(half * D, half * D + D), half * NP // 2
                for i in range(NT):
                    place, lo, hi = bank(0, 4)[:, i * D:(i + 1) * D], max(i * P, first), min((i + 1) * P, first + NP // 2)
                    if hi <= lo:
                        continue
                    rows = total0[side, lo - first:hi - first]
                    if hi - lo == P:
                        mm = pe.transpose(place, rows, ident[side, side])
                    else:
                        mm = pe.matmul(place[lo - i * P:hi - i * P, :], lhsT=rows, rhs=ident[side, side], start=True, stop=True)
                mm.then_inc(turned0, 1)
                pe.wait_ge(turned0, half + 2)

            pe.wait_ge(sums_taken, TILES // 2)
            pe.wait_ge(wa_set, 2)
            wrel_all = wrel_sb[:, :, :].rearrange("d r f -> d (r f)")
            products(1, lambda b: mix(1, b, wrel_all, wa[:, :, :].rearrange("d a r -> d (a r)")))
            pe.wait_ge(taken, 2 * NBATCH)
            carry(0, tails[:, :], R)
            carry(1, heads[:, :], R)
            carry(2, tails[:, :], R)
            carry(3, heads[:, :], R)
            carry(4, run1[:, (NG - 1) % 4, :, K - 1], D)
            pe.wait_ge(c_in, 5)
            products(2, lambda b: mix(2, b, wrel_all, wself_sb[:, :]))

            products(3, lambda b: mix(3, b, we1_sb[:, :, :].rearrange("d a f -> d (a f)"), cut=False))
            pe.wait_ge(taken, 4 * NBATCH)

            def add_up(n, rows_of, banks, per_bank, width, g, s, uses, filled, steps, used, each, reads, summed):
                pe.wait_ge(got[n][s], uses[0] * 16 * K + 16 * K)
                pe.wait_ge(filled, g * steps + K)
                if not isinstance(g, int) or g >= 2:
                    pe.wait_ge(used, (g - 2) * each + reads)
                for j in range(banks):
                    columns = slice(j * per_bank, (j + 1) * per_bank)
                    place = bank(s % 2 * banks + j).rearrange("p (k c) -> p k c", c=width)
                    pe.matmul(place, lhsT=ident[:, :], rhs=rows_of[0][:, s, columns, 0:width], start=True, stop=False)
                    mm = pe.matmul(place, lhsT=ident[:, :], rhs=rows_of[1][:, s, columns, 0:width], start=False, stop=True)
                mm.then_inc(summed, 1)
            quads(pe, lambda g, s, uses: add_up("2", (g2, z2), 2, 4, HID, g, s, uses, filled2, K, work2, 2, 1, summed2))
            carry(5, st2[:, 1, K - 1, :], 2 * D)
            pe.wait_ge(c_in, 6)

            def turn2(b):
                turn(4, b)
                pe.wait_ge(staged_m, b + 1)
                need(pe, lifted_m, b)
                for j in range(NB):
                    mm = pe.transpose(bank(4, 2)[:, j * P:(j + 1) * P], mst2[:, j, :], ident[:, :])
                mm.then_inc(turned_m, 1)

            def mlp2(b):
                pe.wait_ge(lifted, 20 + b + 1)
                pe.wait_ge(lifted_m, b + 1)
                need(pe, hidden_up, b)
                for lo, hi in ((0, 512), (512, BC)):
                    pe.matmul(bank(0, 2)[:, lo:hi], lhsT=wn1m_sb[:, :], rhs=mT2[:, lo:hi], start=True, stop=False)
                    mm = pe.matmul(bank(0, 2)[:, lo:hi], lhsT=wn1h_sb[:, :], rhs=hT[:, :, :].rearrange("d j n -> d (j n)")[:, lo:hi],
                                   start=False, stop=True)
                mm.then_inc(hidden, 1)

            def out2(b):
                pe.wait_ge(hidden_up, b + 1)
                need(pe, taken, 20 + b)
                for j in range(NB):
                    mm = pe.matmul(bank(2)[:, j * D:(j + 1) * D], lhsT=hidT2[:, j * P:(j + 1) * P], rhs=wn2_sb[:, :], start=True, stop=True)
                mm.then_inc(mixed, 1)
            batches_ahead(pe, turn2, mlp2, finish=out2)

            pe.wait_ge(taken, 5 * NBATCH)
            products(5, lambda b: mix(5, b, wlr_sb[:, :, :].rearrange("d a f -> d (a f)")))
            pe.wait_ge(taken, 6 * NBATCH)
            quads(pe, lambda g, s, uses: add_up("3a", (g3, z3), 4, 2, HD, g, s, uses, filled3, K, work3, STEPS3, READS3, summed3))
            carry(6, tails[:, 0:H], H)
            carry(7, heads[:, 0:H], H)
            carry(8, tails[:, 0:H], H)
            carry(9, heads[:, 0:H], H)

            def head_sum(g, s, uses):
                h = s % 2
                pe.wait_ge(made3, g * KD + KD)
                pe.wait_ge(made3b, g + 1)
                if not isinstance(g, int) or g >= 2:
                    pe.wait_ge(work3c, (g - 1) * 2)
                for head in range(H):
                    mm = pe.matmul(bank(h).rearrange("p (c k) -> p k c", k=K), lhsT=ident[:, :],
                                   rhs=y3[:, h, :, head * D:(head + 1) * D], start=(head == 0), stop=(head == H - 1))
                mm.then_inc(heads3, 1)
            quads(pe, head_sum)
            carry(10, run3[:, (NG - 1) % 4, :, K - 1], D)
            pe.wait_ge(c_in, 11)

            def node_sum(n):
                pe.wait_ge(to_spread, 3 + n + 1)
                pe.matmul(bank(0)[:, 0:D], lhsT=valid[:, :], rhs=bnv[:, 0, :], start=True, stop=True).then_inc(spread_up, 1)
            node_sum(0)
            node_sum(1)

            def mlp3(b):
                pe.wait_ge(lifted, 30 + b + 1)
                need(pe, hidden_up, NBATCH + 2 * b)
                for c in range(2):
                    for lo, hi in ((0, 512), (512, BC)):
                        mm = pe.matmul(bank(2 * c, 2)[:, lo:hi], lhsT=wf1_sb[:, c * P:(c + 1) * P],
                                       rhs=hT[:, :, :].rearrange("d j n -> d (j n)")[:, lo:hi], start=True, stop=True)
                    mm.then_inc(hidden, 1)

            def out3(b):
                pe.wait_ge(hidden_up, NBATCH + 2 * b + 2)
                need(pe, taken, 30 + b)
                for j in range(NB):
                    for c in range(2):
                        mm = pe.matmul(bank(4)[:, j * D:(j + 1) * D], lhsT=hid3[:, c, j * P:(j + 1) * P], rhs=wf2_sb[:, c, :],
                                       start=(c == 0), stop=(c == 1))
                mm.then_inc(mixed, 1)
            products(6, mlp3, finish=out3)
            pe.wait_ge(taken, 7 * NBATCH)
            node_sum(2)
            node_sum(3)

        @block.vector
        def _(dve):
            tally = Tally(dve)

            def step(instruction):
                tally.done(instruction, vec)

            def spread(ap, *shape):
                return ap.to_broadcast(list(shape))

            for tile, value in ((ints[:, 0:T + 1], N), (ints[:, T + 1:T + 2], -1), (srci, N), (typei, 0)):
                dve.memset(tile, value).then_inc(padded, 1)
            for tile in (adj_sb, deg_sb):
                dve.memset(tile, 0.0).then_inc(padded, 1)
            dve.memset(zero[:, :], 0.0).then_inc(zeroed, 1)
            dve.memset(lowest[:, :], -BIG).then_inc(zeroed, 1)
            dve.memset(xn[:, :, :], 0.0).then_inc(padded, 1)
            dve.wait_ge(zeroed, 2)

            dve.wait_ge(edges_in, 16 * 21)
            dve.wait_ge(padded, 7)
            step(dve.tensor_copy(dext, ints))
            mid = dext[:, 1:T + 1]
            step(dve.tensor_tensor(ns[:, :], mid, dext[:, 0:T], ALU.is_equal))
            step(dve.tensor_tensor(nl[:, :], mid, dext[:, 2:T + 2], ALU.is_equal))
            step(dve.tensor_scalar(neg[:, :], ns[:, :], -1.0, BIG, ALU.add, ALU.mult))
            step(dve.tensor_scalar(neg_last[:, :], nl[:, :], -1.0, BIG, ALU.add, ALU.mult))
            tally.done(dve.tensor_reduce(flags[:, 0:1], ns[:, :], AX.X, ALU.min), to_spread)
            tally.done(dve.tensor_reduce(flags[:, 1:2], nl[:, :], AX.X, ALU.min), to_spread)
            step(dve.memset(tmpb[:, 0:1], 1.0))
            step(dve.tensor_tensor_scan(tmpb[:, 1:T + 1], nl[:, :], zero[:, 0:T], 1.0, ALU.mult, ALU.add))
            step(dve.tensor_tensor(first_last[:, :], tmpb[:, 0:T], tmpb[:, 1:T + 1], ALU.subtract))
            step(dve.tensor_reduce(opened[:, 0:1], tmpb[:, 0:T], AX.X, ALU.add))
            step(dve.tensor_scalar(opened[:, 1:2], tmpb[:, T:T + 1], -1.0, 1.0, ALU.mult, ALU.add))
            step(dve.tensor_tensor(opened[:, 1:2], opened[:, 1:2], ns[:, 0:1], ALU.mult))
            step(dve.tensor_copy(srcf, srci))
            step(dve.tensor_copy(etypef[:, :], typei))
            step(dve.tensor_copy(dst0[:, :], dext[:, 1:2]))

            def by_group(ap):
                return ap.rearrange("p (g k) -> p g k", k=K)
            step(dve.tensor_copy(meta[:, :, M_SRC:M_SRC + K], by_group(srci)))
            step(dve.scalar_tensor_tensor(out=tmpa, in0=srcf, scalar=float(R), in1=etypef[:, :], op0=ALU.mult, op1=ALU.add))
            step(dve.tensor_copy(meta[:, :, M_REL:M_REL + K], by_group(tmpa)))

            def softplus(x, ax, result, uses):
                step(dve.scalar_tensor_tensor(out=ax, in0=x, scalar=-1.0, in1=x, op0=ALU.mult, op1=ALU.max))
                dve.sem_inc(plus_in, 1)
                dve.wait_ge(plus_out, 2 * uses)
                step(dve.scalar_tensor_tensor(out=result, in0=x, scalar=0.0, in1=ax, op0=ALU.max, op1=ALU.add))
            step(dve.tensor_scalar(tmpa, deg_sb, par[:, 0:1], par[:, 1:2], ALU.mult, ALU.add))
            softplus(tmpa, tmpb[:, 0:T], base, 1)
            step(dve.tensor_tensor(base, base, adj_sb, ALU.mult))
            step(dve.tensor_tensor(tmpa, srcf, mid, ALU.not_equal))
            step(dve.tensor_tensor(base, base, tmpa, ALU.mult))
            softplus(par[:, 5:6], sc[:, 1:2], sc[:, 2:3], 2)
            step(dve.tensor_reduce(sc[:, 3:4], par[:, 2:5], AX.X, ALU.max))
            step(dve.tensor_scalar(sc[:, 4:7], par[:, 2:5], sc[:, 3:4], None, ALU.subtract))
            dve.sem_inc(plus_in, 1)
            dve.wait_ge(plus_out, 5)
            step(dve.tensor_reduce(sc[:, 7:8], sc[:, 4:7], AX.X, ALU.add))
            step(dve.reciprocal(sc[:, 8:9], sc[:, 7:8]))
            step(dve.tensor_scalar(sc[:, 4:7], sc[:, 4:7], sc[:, 8:9], None, ALU.mult))
            step(dve.tensor_scalar(sc[:, 9:10], sc[:, 5:6], -1.0, None, ALU.mult))

            def node_place(node, place, column):
                step(dve.tensor_scalar(place, node, 1.0 / NT, -(NT - 1) / 2 / NT, ALU.mult, ALU.add))
                step(dve.tensor_scalar(place, place, ROUND, -ROUND, ALU.add, ALU.add))
                step(dve.scalar_tensor_tensor(out=column, in0=place, scalar=-float(NT), in1=node, op0=ALU.mult, op1=ALU.add))
            node_place(srcf, tmpa, tmpb[:, 0:T])
            step(dve.scalar_tensor_tensor(out=key, in0=tmpb[:, 0:T], scalar=float(P), in1=tmpa, op0=ALU.mult, op1=ALU.add))
            node_place(mid, pn, im)
            step(dve.scalar_tensor_tensor(out=tmpa, in0=im, scalar=float(P), in1=pn, op0=ALU.mult, op1=ALU.add))
            dve.wait_ge(consts, 12)
            step(dve.tensor_tensor_scan(tmpb[:, 0:T], ns[:, :], zero[:, 0:T], 1.0, ALU.mult, ALU.add))
            step(dve.scalar_tensor_tensor(out=tmpb[:, 0:T], in0=tmpa, scalar=piece_row[:, 0:1], in1=tmpb[:, 0:T],
                                          op0=ALU.subtract, op1=ALU.mult))
            step(dve.tensor_tensor(tmpa, tmpa, tmpb[:, 0:T], ALU.subtract))
            step(dve.scalar_tensor_tensor(out=key, in0=tmpa, scalar=float(NP), in1=key, op0=ALU.mult, op1=ALU.add))

            merge = Beats(dve, merging, 8)

            def merge0(w):
                merge.group(w)
                keys, weights = key[:, bass.ds(w * W, W)], base[:, bass.ds(w * W, W)]
                before, first, total = (merged0[:, k, :] for k in range(3))
                merge.done(dve.tensor_tensor(alike, spread(keys.unsqueeze(1), P, W, W), spread(keys.unsqueeze(2), P, W, W), ALU.is_equal))
                merge.done(dve.tensor_tensor(alike_by, alike, earlier, ALU.mult))
                merge.done(dve.tensor_reduce(before, alike_by, AX.X, ALU.add))
                merge.add(dve.tensor_tensor(alike_by, alike, spread(weights.unsqueeze(1), P, W, W), ALU.mult))
                merge.done(dve.scalar_tensor_tensor(out=first, in0=before, scalar=0.5, in1=ones[:, 0:W], op0=ALU.is_lt, op1=ALU.mult))
                merge.done(dve.tensor_reduce(total, alike_by, AX.X, ALU.add))
                dve.tensor_tensor(before, keys, trash[:, :], ALU.subtract).then_inc(apart, 1)
                dve.wait_ge(apart, w * 2 + 1)
                dve.tensor_tensor(before, before, first, ALU.mult).then_inc(apart, 1)
                dve.wait_ge(apart, w * 2 + 2)
                cells_out = words0[:, bass.ds(w * GW, GW), 0:K]
                merge.add(dve.tensor_tensor(cells_out, by_group(before), by_group(trash[:, :]), ALU.add))
                merge.done(dve.tensor_scalar(words0f[:, bass.ds(w * GW, GW), K:2 * K], by_group(total), 1.0, None, ALU.mult))
            merge0(0)
            with dve.Fori(1, NW) as w:
                merge0(w)

            def norm_relu(n):
                col = [lnv[:, k, :] for k in range(4)]
                step(dve.tensor_reduce(col[0], xn[:, :, :], AX.X, ALU.add))
                step(dve.tensor_scalar(col[0], col[0], 1.0 / D, None, ALU.mult))
                step(dve.tensor_tensor(hn[:, :, :], xn[:, :, :], spread(col[0].unsqueeze(2), P, NT, D), ALU.subtract))
                step(dve.tensor_tensor(agg[:, :, :], hn[:, :, :], hn[:, :, :], ALU.mult))
                step(dve.tensor_reduce(col[0], agg[:, :, :], AX.X, ALU.add))
                step(dve.tensor_scalar(col[1], col[0], 1.0 / D, EPS, ALU.mult, ALU.add))
                dve.sem_inc(root_in, 1)
                dve.wait_ge(root_out, n + 1)
                step(dve.reciprocal(col[3], col[2]))
                step(dve.tensor_tensor(hn[:, :, :], hn[:, :, :], spread(col[3].unsqueeze(2), P, NT, D), ALU.mult))
                step(dve.tensor_scalar(hn[:, :, :], hn[:, :, :], 0.0, None, ALU.max))

            def stage(s, b, rows):
                need(dve, turned, 5 * s + b)
                dve.tensor_scalar(hst[:, :, :], rows[:, bass.ds(b * NB, NB), :], 1.0, None, ALU.mult).then_inc(staged, 1)

            def node_phase(s, rows, body):
                batches_ahead(dve, lambda b: stage(s, b, rows), body, early=True)

            def product(first, n, width):
                return bank(0, 6)[:, first:first + n].rearrange("p (j c) -> p j c", c=width)

            dve.wait_ge(x_in, 16)
            dve.wait_ge(params_in, PARAMS)
            norm_relu(0)

            def nodes0(b):
                dve.wait_ge(mixed, b + 1)
                dve.tensor_scalar(whT[:, bass.ds(b * NB, NB), :], bank(2, 2)[:, 0:BC].rearrange("d (j n) -> d j n", n=P),
                                  colb[:, 3:4], None, ALU.add)
                dve.tensor_tensor(wh[:, bass.ds(b * NB, NB), :], bank(0)[:, 0:NB * D].rearrange("p (j c) -> p j c", c=D),
                                  spread(row["b0"].unsqueeze(1), P, NB, D), ALU.add).then_inc(taken, 1)
            node_phase(0, hn, nodes0)
            dve.wait_ge(taken, NBATCH)
            rows_T = whT[0:D, 0:NT, :].rearrange("d j n -> d (j n)")
            tally.done(dve.tensor_tensor(squares, rows_T, rows_T, ALU.mult), squared)
            step(dve.tensor_tensor(agg[:, :, :], wh[:, 0:NT, :], wh[:, 0:NT, :], ALU.mult))
            tally.done(dve.tensor_reduce(lnv[:, 0, :], agg[:, :, :], AX.X, ALU.add), norm_in)
            dve.wait_ge(norm_out, 1)
            step(dve.reciprocal(per_dst[:, 0:NT], lnv[:, 1, :]))
            dve.wait_ge(norm_out, 2)
            step(dve.reciprocal(per_src, per_src))

            def split(x, hi, mid, lo):
                step(dve.tensor_copy(hi, x))
                step(dve.tensor_tensor(x, x, hi, ALU.subtract))
                step(dve.tensor_copy(mid, x))
                step(dve.tensor_tensor(x, x, mid, ALU.subtract))
                step(dve.tensor_copy(lo, x))
            real = slice(0, NT)
            split(whT[:, real, :], high[:, real, :], middle[:, real, :], low[:, real, :])
            for pairs_to, lower_part, upper_part in ((high_middle, high, middle), (middle_high, middle, high), (low_high, low, high)):
                step(dve.tensor_copy(pairs_to[0:D, real, :], lower_part[0:D, real, :]))
                step(dve.tensor_copy(pairs_to[D:P, real, :], upper_part[D:P, real, :]))

            dve.wait_ge(consts, 12)

            deg, cum, end, first_edge, has, at = (nodev[:, k, :] for k in range(6))
            dve.memset(deg, 0.0).then_inc(tallied, 1)

            def tally_counts(done, h):
                dve.wait_ge(counted, done)
                dve.wait_ge(tallied, done)
                dve.tensor_tensor(deg, bank(h)[:, 0:NT], deg, ALU.add).then_inc(tallied, 1)

            def one_hot(i, h, first):
                g = i * 2 + h
                if not first:
                    tally_counts(g - 1, h)
                for hots, place, width in ((hot_p, pn, P), (hot_i, im, NT)):
                    dve.tensor_tensor(hots[:, h * K:h * K + K, :], spread(iota_row[:, 0:width].unsqueeze(1), P, K, width),
                                      spread(place[:, bass.ds(g * K, K)].unsqueeze(2), P, K, width), ALU.is_equal).then_inc(hot, 1)
            passes(dve, one_hot)
            for h in range(2):
                tally_counts(NG - 1 + h, h)
            dve.wait_ge(tallied, 1 + NG)
            tally.done(dve.tensor_tensor_scan(cum, ones[:, 0:NT], deg, 0.0, ALU.mult, ALU.add), to_spread)
            dve.wait_ge(spread_up, 1)
            step(dve.tensor_scalar(end, cum, bank(1)[:, 0:1], None, ALU.add))
            step(dve.tensor_tensor(first_edge, end, deg, ALU.subtract))
            step(dve.tensor_scalar(has, deg, 0.0, None, ALU.is_gt))
            step(dve.tensor_tensor(at, first_edge, node_trash[:, :], ALU.subtract))
            step(dve.tensor_tensor(at, at, has, ALU.mult))
            step(dve.tensor_tensor(zidx[:, :], at, node_trash[:, :], ALU.add))
            step(dve.scalar_tensor_tensor(out=at, in0=end, scalar=-1.0 - EP, in1=has, op0=ALU.add, op1=ALU.mult))
            step(dve.tensor_scalar(eidx[:, :], at, float(EP), None, ALU.add))
            step(dve.tensor_scalar(opened[:, 2:3], piece_row[:, :], float(T - 1), float(-NP * (T - 1) - EP - 2), ALU.mult, ALU.add))
            step(dve.tensor_tensor(opened[:, 2:3], opened[:, 2:3], opened[:, 0:1], ALU.add))
            step(dve.tensor_tensor(opened[:, 2:3], opened[:, 2:3], opened[:, 1:2], ALU.mult))
            step(dve.tensor_scalar(opened[:, 3:4], piece_row[:, :], float(EP + 1 - NP), None, ALU.add))
            tally.done(dve.tensor_tensor(open_end[:, :], opened[:, 2:3], opened[:, 3:4], ALU.add), indices)
            dve.wait_ge(spread_up, 3)
            tally.done(dve.tensor_copy(nhs_row[:, :], bank(2)[:, 0:P]), flags_read)
            tally.done(dve.tensor_copy(nhl_row[:, :], bank(2)[:, P:2 * P]), flags_read)
            tally.done(dve.tensor_scalar(hneg_row[:, :], nhs_row[:, :], -1.0, BIG, ALU.add, ALU.mult), flags_read)

            def mark(marks, g, k):
                return marks[:, bass.ds(g * K, K)][:, k:k + 1]

            def fill(beats, rows, first, g, s, k):
                if k == 0:
                    beats.group(g)
                beats.wait()
                before = rows[:, s, k - 1, :] if k else first if isinstance(g, int) and g == 0 else rows[:, (s - 1) % 4, K - 1, :]
                beats.add(dve.scalar_tensor_tensor(out=rows[:, s, k, :], in0=before, scalar=mark(ns, g, k), in1=rows[:, s, k, :],
                                                   op0=ALU.mult, op1=ALU.add))

            dve.wait_ge(hold_in, 16)
            step(dve.tensor_tensor(agg[:, 0, :], wh[:, NT, :], wh[:, NT, :], ALU.mult))
            tally.done(dve.tensor_reduce(rnv[:, 0:1], agg[:, 0, :], AX.X, ALU.add), norm_in)
            dve.wait_ge(norm_out, 3)
            step(dve.reciprocal(per_dst[:, NT:TILES], rnv[:, 1:2]))
            for half in range(2):
                tally.done(dve.tensor_copy(cin[:, half * D:(half + 1) * D], wh[:, NT, :]), piece_up)
            dve.wait_ge(turned0, 1)
            step(dve.tensor_copy(cT[:, 0:P], bank(7)[:, 0:P]))
            split(cT[:, 0:P], hst_parts[:, 0, :], hst_parts[:, 1, :], low[:, NT, :])
            step(dve.tensor_copy(high_middle[0:D, NT, :], hst_parts[0:D, 0, :]))
            tally.done(dve.tensor_copy(high_middle[D:P, NT, :], hst_parts[D:P, 1, :]), piece_set)
            works0 = Beats(dve, work0, 8)

            def sums0(pair):
                dve.wait_ge(summed0, pair * 2 + 2)
                if late(pair, 1):
                    dve.wait_ge(sums_taken, pair)
                sums, total = psum[:, 0:4, 0:NP // 8], total0.rearrange("d (c n) -> d c n", c=4)
                if late(pair, 1):
                    dve.tensor_tensor(total, sums, total, ALU.add).then_inc(sums_taken, 1)
                else:
                    dve.tensor_scalar(total, sums, 1.0, None, ALU.mult).then_inc(sums_taken, 1)

            def similarity0(j, s):
                works0.group(j)
                works0.wait()
                dve.wait_ge(weighted, j + 1)
                def part(c):
                    dve.wait_ge(signs, j * 4 + c + 1)
                    works0.add(dve.tensor_tensor(parts0[c % 3], signed[:, c % 2, 0, :], signed[:, c % 2, 1, :], ALU.subtract))

                def weigh(c, back):
                    at = c * NP // 4
                    works0.wait(back)
                    works0.add(dve.tensor_tensor(cells[:, s, at:at + NP // 4], cells[:, s, at:at + NP // 4], parts0[c % 3], ALU.mult))
                part(0)
                part(1)
                weigh(0, 1)
                part(2)
                weigh(1, 2)
                works0.wait(2)
                part(3)
                weigh(2, 2)
                weigh(3, 1)

            def edges0(j, s, uses):
                if late(j, 1):
                    dve.wait_ge(weighted, j)
                dve.tensor_scalar(per_pair, per_src, per_dst[:, bass.ds(j, 1)], 1e8, ALU.mult, ALU.min).then_inc(pairs, 1)
                if late(j, 4) and s % 2 == 0:
                    sums0(j // 2 - 2 if isinstance(j, int) else uses * 2 + (s // 2 - 2))
                if late(j, 1):
                    similarity0(j - 1, (s - 1) % 4)
            tiles(dve, edges0)
            similarity0(TILES - 1, (TILES - 1) % 4)
            sums0(TILES // 2 - 2)
            sums0(TILES // 2 - 1)
            dve.wait_ge(sums_taken, TILES // 2)
            dve.wait_ge(turned0, 3)
            sums = bank(0, 4)[:, 0:NT * D].rearrange("p (i c) -> p i c", c=D)
            step(dve.scalar_tensor_tensor(out=agg[:, :, :], in0=wh[:, 0:NT, :], scalar=sc[:, 6:7], in1=sums, op0=ALU.mult, op1=ALU.add))
            step(dve.scalar_tensor_tensor(out=xn[:, :, :], in0=agg[:, :, :], scalar=sc[:, 2:3], in1=xn[:, :, :], op0=ALU.mult, op1=ALU.add))

            for side, name in ((0, "a_src"), (1, "a_dst")):
                prod = area(5300, R, D)[0:D, :, :]
                step(dve.tensor_tensor(prod, wrel_sb[:, :, :], row[name][0:D, :].rearrange("p (r f) -> p r f", f=D), ALU.mult))
                tally.done(dve.tensor_reduce(wa[:, side, :], prod, AX.X, ALU.add), wa_set)
            norm_relu(1)
            beats1 = Beats(dve, node_vec[1], 4)

            def nodes1(b):
                beats1.group(b)
                dve.wait_ge(tab_out, b * 16 + 16 * (1 + 0 * NBATCH))
                at = bass.ds(b * NB, NB)
                for lo, hi, done, used, base in parts(1):
                    dve.wait_ge(done, base + b + 1)
                    if lo == 0:
                        scores = product(5 * 512, NB * 2 * R, 2 * R)
                        beats1.add(dve.tensor_copy(tb1[:, :, :, D], scores[:, :, 0:R]))
                        beats1.done(dve.tensor_scalar(dn1[:, at, 0:R], scores[:, :, R:2 * R], 1.0, None, ALU.mult))
                        loops = dn1[:, at, R:2 * R]
                        beats1.done(dve.tensor_tensor(loops, dn1[:, at, 0:R], scores[:, :, 0:R], ALU.add))
                        beats1.done(dve.scalar_tensor_tensor(out=loops, in0=loops, scalar=SLOPE, in1=loops, op0=ALU.mult, op1=ALU.max))
                    dve.tensor_copy(tb1[:, lo:hi, :, 0:D].rearrange("p j r c -> p (j r) c"), product(lo * R * D, (hi - lo) * R * D, D)).then_inc(used, 1)
            node_phase(1, hn, nodes1)
            dve.wait_ge(taken, 2 * NBATCH)

            dve.wait_ge(ds_in, 16)
            dve.wait_ge(hold_in, 16 * 2)
            for c in range(2 * R):
                step(dve.tensor_tensor_scan(ds[:, :, c], ns[:, :], ds[:, :, c], dinit1[:, c:c + 1], ALU.mult, ALU.add))
            s_src, ev, dsel, tmp = (score[:, k, :] for k in range(4))
            step(dve.scalar_tensor_tensor(out=dsel, in0=etypef[:, :], scalar=0.0, in1=ds[:, :, 0], op0=ALU.is_equal, op1=ALU.mult))
            for r in range(1, R):
                step(dve.scalar_tensor_tensor(out=tmp, in0=etypef[:, :], scalar=float(r), in1=ds[:, :, r], op0=ALU.is_equal, op1=ALU.mult))
                step(dve.tensor_tensor(dsel, dsel, tmp, ALU.add))

            def take1(i, h, first):
                dve.wait_ge(got["1a"][h], i * 16 * K + 16 * K)
                dve.tensor_scalar(s_src[:, bass.ds((i * 2 + h) * K, K)], g1[:, h, :, D], 1.0, None, ALU.mult).then_inc(taken1, 1)
            passes(dve, take1)
            dve.wait_ge(taken1, NG)
            for h in range(2):
                dve.wait_ge(kept["1a"][h], 16 * LOOPS)

            def over_partitions(use, source, width, op):
                flag = {"sum": nhs_row, "max": hneg_row, "back": nhl_row}[op]
                neutral = -BIG if op == "max" else 0.0
                ops = (ALU.add, ALU.max) if op == "max" else (ALU.mult, ALU.add)
                back = op == "back"
                assert back == (use in BACKWARD)
                dve.sem_inc(c_tail, 1)
                step(dve.memset(cT[:, P:P + 1] if back else cT[:, 0:1], neutral))
                dve.wait_ge(c_turn, use + 1)
                rows, flag = bank(0)[0:width, 0:P], flag[0:width, :]
                if back:
                    step(dve.tensor_tensor_scan(cT[0:width, 0:P][:, ::-1], flag[:, ::-1], rows[:, ::-1], neutral, *ops))
                else:
                    step(dve.tensor_tensor_scan(cT[0:width, 1:P + 1], flag, rows, neutral, *ops))
                dve.sem_inc(c_scan, 1)
                dve.wait_ge(c_back, use + 1)
                step(dve.tensor_copy(cin[:, 0:width], bank(1)[:, 0:width]))
                dve.sem_inc(c_in, 1)

            def segment_totals(use, values, totals, n, op):
                marks, neutral = (neg, -BIG) if op == "max" else (ns, 0.0)
                ops = (ALU.add, ALU.max) if op == "max" else (ALU.mult, ALU.add)
                for r in range(n):
                    step(dve.tensor_tensor_scan(totals[:, r, :], marks[:, :], values[:, r, :], neutral, *ops))
                step(dve.tensor_copy(tails[:, 0:n], totals[:, :, T - 1]))
                over_partitions(use, tails, n, op)
                for r in range(n):
                    step(dve.tensor_tensor_scan(totals[:, r, :], marks[:, :], values[:, r, :], cin[:, r:r + 1], *ops))
                for r in range(n):
                    step(dve.tensor_tensor(back_tmp, totals[:, r, :], first_last[:, :], ALU.mult))
                    step(dve.tensor_reduce(heads[:, r:r + 1], back_tmp, AX.X, ALU.add))
                over_partitions(use + 1, heads, n, "back")
                for r in range(n):
                    step(dve.tensor_tensor_scan(totals[:, r, ::-1], (neg_last if op == "max" else nl)[:, ::-1], totals[:, r, ::-1], cin[:, r:r + 1],
                                                ALU.add if op == "max" else ALU.mult, ALU.max))

            back_tmp = tmp
            step(dve.tensor_tensor(ev, s_src, dsel, ALU.add))
            step(dve.scalar_tensor_tensor(out=ev, in0=ev, scalar=SLOPE, in1=ev, op0=ALU.mult, op1=ALU.max))
            for r in range(R):
                step(dve.tensor_scalar(tmp, etypef[:, :], float(r), -BIG, ALU.not_equal, ALU.mult))
                step(dve.tensor_tensor(v1[:, r, :], ev, tmp, ALU.add))
            segment_totals(0, v1, f1, R, "max")
            loop_of_edge = ds[:, :, R:2 * R].rearrange("p t r -> p r t")
            step(dve.tensor_tensor(f1, f1, loop_of_edge, ALU.max))
            step(dve.tensor_tensor(v1, v1, f1, ALU.subtract))
            dve.sem_inc(soft_in, 1)
            step(dve.tensor_tensor(loop_of_edge, loop_of_edge, f1, ALU.subtract))
            dve.sem_inc(soft_in, 1)
            dve.wait_ge(soft_exp, 1)
            segment_totals(2, v1, f1, R, "sum")
            dve.wait_ge(soft_exp, 2)
            step(dve.tensor_tensor(f1, f1, loop_of_edge, ALU.add))
            dve.sem_inc(soft_in, 1)
            step(dve.tensor_reduce(alpha1, v1.rearrange("p r t -> p t r"), AX.X, ALU.add))
            dve.wait_ge(soft_exp, 3)
            for r in range(R):
                step(dve.scalar_tensor_tensor(out=f1[:, r, :], in0=etypef[:, :], scalar=float(r), in1=f1[:, r, :], op0=ALU.is_equal, op1=ALU.mult))
            step(dve.tensor_reduce(tmp, f1.rearrange("p r t -> p t r"), AX.X, ALU.add))
            step(dve.reciprocal(tmp, tmp))
            tally.done(dve.tensor_tensor(alpha1, alpha1, tmp, ALU.mult), weights_set)

            def sum_in(beats, run, values, g, s):
                beats.group(g)
                beats.wait()
                before = zero[:, 0:D] if isinstance(g, int) and g == 0 else run[:, (s - 1) % 4, :, K - 1]
                beats.add(dve.scalar_tensor_tensor(out=values[:, :, 0], in0=before, scalar=mark(ns, g, 0), in1=values[:, :, 0],
                                                   op0=ALU.mult, op1=ALU.add))

            def sum_up(use, beats, run, reset, values, g, s, uses):
                dve.wait_ge(resets, uses[1] + (1 + NG // 2 * use))
                if late(g, 4):
                    dve.wait_ge(state_rows, uses[1] + (NG // 2 * use - 1))
                beats.wait()
                by_component = "p d k -> p (d k)"
                beats.add(dve.tensor_tensor_scan(run[:, s, :, :].rearrange(by_component), reset[:, s, :, :].rearrange(by_component),
                                                 values.rearrange(by_component), 0.0, ALU.mult, ALU.add))
            step(dve.memset(reset1[:, :, :, 0:1], 0.0))
            sums1 = Beats(dve, work1c, 2)

            def sum1(g, s, uses):
                dve.wait_ge(made1, g + 1)
                sum_in(sums1, run1, y1[:, s, :, :], g, s)
                sum_up(0, sums1, run1, reset1, y1[:, s, :, :], g, s, uses)
            quads(dve, sum1)
            dve.wait_ge(work1c, NG * 2)
            over_partitions(4, run1, D, "sum")
            dve.wait_ge(open_moved, 16)
            step(dve.tensor_tensor(open_sum[:, 0:D], open_sum[:, 0:D], cin[:, 0:D], ALU.add))
            dve.sem_inc(ended, 1)
            for r in range(R):
                step(dve.tensor_tensor(row["b_self"], row["b_self"], row["bias_rel"][:, r * D:(r + 1) * D], ALU.add))
            beats1n = Beats(dve, node_vec[2], 8)

            def nodes1b(b):
                beats1n.group(b)
                at = bass.ds(b * NB, NB)
                dve.wait_ge(agg_in, b * 16 * NB + 16 * NB)
                beats1n.done(dve.reciprocal(beta_n[:, at, 0:R], beta_n[:, at, 0:R]))
                beats1n.done(dve.tensor_tensor(beta_n[:, at, 0:R], beta_n[:, at, 0:R], beta_n[:, at, R:2 * R], ALU.mult))
                for lo, hi, done, used, base in parts(2):
                    n = hi - lo
                    dve.wait_ge(done, base + b + 1)
                    if lo == 0:
                        beats1n.done(dve.tensor_tensor(xn[:, at, :], xn[:, at, :], product(5 * 512, NB * D, D), ALU.add))
                        beats1n.done(dve.tensor_tensor(xn[:, at, :], xn[:, at, :], spread(row["b_self"].unsqueeze(1), P, NB, D), ALU.add))
                    beats1n.done(dve.tensor_tensor(prod1[:, lo:hi, :, :], bank(lo, n).rearrange("p (j r c) -> p j r c", r=R, c=D),
                                                   spread(beta_n[:, bass.ds(b * NB + lo, n), 0:R].unsqueeze(3), P, n, R, D), ALU.mult))
                    beats1n.done(dve.tensor_reduce(red1[:, lo:hi, :], prod1[:, lo:hi, :, :].rearrange("p j r c -> p j c r"), AX.X, ALU.add))
                    own = xn[:, bass.ds(b * NB + lo, n), :]
                    dve.tensor_tensor(own, own, red1[:, lo:hi, :], ALU.add).then_inc(used, 1)
            node_phase(2, hn, nodes1b)
            dve.wait_ge(taken, 3 * NBATCH)
            dve.wait_ge(agg_in, 16 * 2 * NT)
            step(dve.tensor_tensor(xn[:, :, :], xn[:, :, :], agg[:, :, :], ALU.add))

            norm_relu(2)
            beats2t = Beats(dve, node_vec[3], 2)

            def nodes2(b):
                beats2t.group(b)
                dve.wait_ge(mixed, 15 + b + 1)
                dve.wait_ge(tab_out, b * 16 + 16 * (1 + 1 * NBATCH))
                halves = product(0, NB * 2 * HID, 2 * HID)
                beats2t.add(dve.tensor_copy(tb2[:, :, 0:HID], halves[:, :, 0:HID]))
                beats2t.add(dve.tensor_scalar(tb2[:, :, HID:W2], hn[:, bass.ds(b * NB, NB), :], 1.0, None, ALU.mult))
                beats2t.wait()
                dve.tensor_tensor(bn_rows[:, bass.ds(b * NB, NB), :], halves[:, :, HID:2 * HID], spread(row["be1"].unsqueeze(1), P, NB, HID),
                                  ALU.add).then_inc(taken, 1)
            node_phase(3, hn, nodes2)
            dve.wait_ge(taken, 4 * NBATCH)

            dve.wait_ge(hold_in, 16 * 3)
            fills2, beats2, scans2 = Beats(dve, filled2, K), Beats(dve, work2, 2), Beats(dve, scan2, 2 * K)

            def relu2(g, h):
                beats2.group(g)
                beats2.wait()
                dve.wait_ge(summed2, g + 1)
                beats2.add(dve.scalar_tensor_tensor(out=pr2, in0=bank(2 * h, 2).rearrange("p (k c) -> p k c", c=HID), scalar=0.0,
                                                    in1=spread(row["we2"].unsqueeze(1), P, K, HID), op0=ALU.max, op1=ALU.mult))

            def reduce2(g, h):
                beats2.wait()
                need(dve, gate2, g - 1 if not isinstance(g, int) else max(g - 1, 0))
                beats2.add(dve.tensor_reduce(e2[:, h, :], pr2, AX.X, ALU.add))

            def sum2(g, s, uses, k):
                h = s % 2
                if k == 0:
                    scans2.group(g)
                    dve.wait_ge(made2, g + 1)
                    if late(g, 2):
                        before = (s - 2) % 4
                        dve.wait_ge(states_out[before], (before_of(g, s, uses, 2)[0] + (1 + states_before(1, before))) * 16)
                start = isinstance(g, int) and g == 0 and k == 0
                prior = st2[:, h, k - 1, :] if k else st2[:, 1 - h, K - 1, :]
                scans2.wait(1 if k else 0)
                scans2.add(dve.scalar_tensor_tensor(out=st2[:, h, k, 0:D], in0=zero[:, 0:D] if start else prior[:, 0:D],
                                                    scalar=mark(ns, g, k), in1=m2[:, h, k, :],
                                                    op0=ALU.mult, op1=ALU.add))
                scans2.wait(1)
                scans2.add(dve.scalar_tensor_tensor(out=st2[:, h, k, D:2 * D], in0=lowest[:, :] if start else prior[:, D:2 * D],
                                                    scalar=mark(neg, g, k), in1=m2[:, h, k, :],
                                                    op0=ALU.add, op1=ALU.max))

            def edges2(g, s, uses):
                dve.wait_ge(rows_in["2"][s], uses[0] * 16 + 16)
                for k in range(K):
                    fill(fills2, z2, hold2, g, s, k)
                    if late(g, 2) and k == 1:
                        relu2(g - 2, s % 2)
                    if late(g, 2) and k == 3:
                        reduce2(g - 2, s % 2)
                    if late(g, 3):
                        sum2(g - 3, (s - 3) % 4, before_of(g, s, uses, 3), k)
            quads(dve, edges2)
            for g in range(NG - 3, NG):
                if g > NG - 3:
                    relu2(g, g % 2)
                    reduce2(g, g % 2)
                for k in range(K):
                    sum2(g, g % 4, (g // 4, g // 2), k)
            dve.wait_ge(scan2, NG * 2 * K)
            dve.sem_inc(c_tail, 1)
            step(dve.memset(cT[0:D, 0:1], 0.0))
            step(dve.memset(cT[D:2 * D, 0:1], -BIG))
            dve.wait_ge(c_turn, 6)
            step(dve.tensor_tensor_scan(cT[0:D, 1:P + 1], nhs_row[0:D, :], bank(0)[0:D, 0:P], 0.0, ALU.mult, ALU.add))
            step(dve.tensor_tensor_scan(cT[D:2 * D, 1:P + 1], hneg_row[D:2 * D, :], bank(0)[D:2 * D, 0:P], -BIG, ALU.add, ALU.max))
            dve.sem_inc(c_scan, 1)
            dve.wait_ge(c_back, 6)
            step(dve.tensor_copy(cin[:, :], bank(1)[:, 0:2 * D]))
            dve.sem_inc(c_in, 1)
            dve.wait_ge(open_moved, 48)
            step(dve.tensor_tensor(open_sum[:, 0:D], open_sum[:, 0:D], cin[:, 0:D], ALU.add))
            step(dve.tensor_tensor(open_sum[:, D:2 * D], open_sum[:, D:2 * D], cin[:, D:2 * D], ALU.max))
            dve.sem_inc(ended, 1)
            step(dve.tensor_tensor(xn[:, :, :], xn[:, :, :], hn[:, :, :], ALU.add))
            beats2n = Beats(dve, node_vec[4], 1)

            def stage2(b):
                need(dve, turned_m, b)
                dve.wait_ge(agg_in, b * 16 * NB + 16 * (2 * NT + NB))
                dve.tensor_scalar(mst2, agg2[:, bass.ds(b * NB, NB), :], 1.0, None, ALU.mult).then_inc(staged_m, 1)
                stage(4, b, hn)

            def nodes2b(b):
                beats2n.group(b)
                dve.wait_ge(mixed, 20 + b + 1)
                red = area(9000, NB, D)
                beats2n.done(dve.tensor_tensor(red, bank(2)[:, 0:NB * D].rearrange("p (j c) -> p j c", c=D),
                                               spread(row["bn2"].unsqueeze(1), P, NB, D), ALU.add))
                dve.tensor_tensor(xn[:, bass.ds(b * NB, NB), :], xn[:, bass.ds(b * NB, NB), :], red, ALU.add).then_inc(taken, 1)
            batches_ahead(dve, stage2, nodes2b, early=True)
            dve.wait_ge(taken, 5 * NBATCH)

            norm_relu(3)
            step(dve.tensor_scalar(rowb[:, 0:HD], row["att"], 1.0 - SLOPE, None, ALU.mult))
            att_relu = rowb[:, 0:HD]
            step(dve.tensor_scalar(row["att"], row["att"], SLOPE, None, ALU.mult))
            lin, xs = area(8000, NB, HD), area(9300, NB, W3)
            beats3t = Beats(dve, node_vec[5], 12)

            def nodes3(b):
                beats3t.group(b)
                dve.wait_ge(tab_out, b * 16 + 16 * (1 + 2 * NBATCH))
                for lo, hi, done, used, base in parts(5):
                    n, own = hi - lo, slice(lo, hi)
                    dve.wait_ge(done, base + b + 1)
                    sides = product(lo * 2 * HD, n * 2 * HD, 2 * HD)
                    beats3t.wait()
                    need(dve, used, base + b)
                    for side, rows, name in ((0, tb3, "b_l"), (1, xs, "b_r")):
                        beats3t.done(dve.tensor_tensor(rows[:, own, 0:HD], sides[:, :, side * HD:(side + 1) * HD],
                                                       spread(row[name].unsqueeze(1), P, n, HD), ALU.add))
                        beats3t.done(dve.tensor_tensor(lin[:, own, :], rows[:, own, 0:HD], spread(row["att"].unsqueeze(1), P, n, HD), ALU.mult))
                        beats3t.done(dve.tensor_reduce(rows[:, own, HD:W3], lin[:, own, :].rearrange("p j (h c) -> p j h c", c=D), AX.X, ALU.add))
                    dve.tensor_scalar(xr_rows[:, bass.ds(b * NB + lo, n), :], xs[:, own, :], 1.0, None, ALU.mult).then_inc(used, 1)
            node_phase(5, hn, nodes3)
            dve.wait_ge(taken, 6 * NBATCH)

            dve.wait_ge(hold_in, 16 * 4)
            fills3, beats3 = Beats(dve, filled3, K), Beats(dve, work3, STEPS3)
            halves3 = [slice(0, K // 2), slice(K // 2, K)]

            def relu3(g, h, part):
                if part == 0:
                    beats3.group(g)
                    dve.wait_ge(summed3, g + 1)
                    need(dve, scored, g)
                columns = halves3[part]
                beats3.add(dve.scalar_tensor_tensor(out=pr3[:, columns, :], in0=bank(4 * h + 2 * part, 2).rearrange("p (k c) -> p k c", c=HD),
                                                    scalar=0.0, in1=spread(att_relu.unsqueeze(1), P, K // 2, HD), op0=ALU.max, op1=ALU.mult))

            def reduce3(part):
                columns = slice(part * K // 4, (part + 1) * K // 4)
                beats3.wait(part)
                beats3.add(dve.tensor_reduce(rs3[:, columns, :], pr3[:, columns, :].rearrange("p k (h c) -> p k h c", c=D), AX.X, ALU.add))

            def linear3(g, s):
                beats3.add(dve.tensor_tensor(zl3, g3[:, s, :, HD:W3], z3[:, s, :, HD:W3], ALU.add))

            def score3(g):
                dve.wait_ge(work3, g * STEPS3 + STEPS3)
                dve.tensor_tensor(score[:, :, bass.ds(g * K, K)].rearrange("p h k -> p k h"), rs3, zl3, ALU.add).then_inc(scored, 1)

            def edges3(g, s, uses):
                dve.wait_ge(rows_in["3a"][s], uses[0] * 16 + 16)
                for k in range(K):
                    fill(fills3, z3, hold3, g, s, k)
                    if late(g, 3) and k == 0:
                        score3(g - 3)
                    if late(g, 2):
                        if k in (1, 3):
                            relu3(g - 2, s % 2, k // 2)
                        if k == 2:
                            linear3(g - 2, (s - 2) % 4)
                        if k >= 4:
                            reduce3(k - 4)
            quads(dve, edges3)
            score3(NG - 3)
            for g in (NG - 2, NG - 1):
                relu3(g, g % 2, 0)
                linear3(g, g % 4)
                relu3(g, g % 2, 1)
                for part in range(4):
                    reduce3(part)
                score3(g)
            dve.wait_ge(scored, NG)
            for s in range(4):
                dve.wait_ge(kept["3a"][s], 16 * ((NG - s + 3) // 4))

            back_tmp = area(3200, T)
            segment_totals(6, score, f3, H, "max")
            step(dve.tensor_tensor(score, score, f3, ALU.subtract))
            dve.sem_inc(soft_in, 1)
            dve.wait_ge(soft_exp, 4)
            segment_totals(8, score, f3, H, "sum")
            step(dve.tensor_scalar(f3, f3, 1e-16, None, ALU.max))
            step(dve.reciprocal(f3, f3))
            step(dve.tensor_tensor(score, score, f3, ALU.mult))
            dve.sem_inc(ended, 1)
            step(dve.memset(reset3[:, :, :, 0:1], 0.0))
            makes3, sums3 = Beats(dve, made3, KD), Beats(dve, work3c, 2)
            dve.sem_inc(weights_set, 1)

            def sums_of(s):
                return bank(s % 2).rearrange("p (c k) -> p c k", k=K)

            def edges3c(g, s, uses):
                behind = late(g, 2)
                makes3.group(g)
                dve.wait_ge(loaded[s], uses[0] * 16 + 16 * (1 + after(3, s)))
                if behind:
                    dve.wait_ge(heads3, g - 1)
                for k in range(KD):
                    makes3.add(dve.tensor_tensor(y3[:, s % 2, k, :].rearrange("p (h c) -> p h c", c=D),
                                                 gc3[:, s, k, 0:HD].rearrange("p (h c) -> p h c", c=D),
                                                 spread(score[:, :, bass.ds(g * K, K)][:, :, k:k + 1], P, H, D), ALU.mult))
                    if behind and k == 0:
                        sum_in(sums3, run3, sums_of(s), g - 2, (s - 2) % 4)
                    if behind and k == 2:
                        sum_up(1, sums3, run3, reset3, sums_of(s), g - 2, (s - 2) % 4, before_of(g, s, uses, 2))
            quads(dve, edges3c)
            for g in (NG - 2, NG - 1):
                dve.wait_ge(heads3, g + 1)
                sum_in(sums3, run3, sums_of(g), g, g % 4)
                sum_up(1, sums3, run3, reset3, sums_of(g), g, g % 4, (g // 4, g // 2))
            dve.wait_ge(work3c, NG * 2)
            over_partitions(10, run3, D, "sum")
            dve.wait_ge(open_moved, 80)
            step(dve.tensor_tensor(open_sum[:, 0:D], open_sum[:, 0:D], cin[:, 0:D], ALU.add))
            dve.sem_inc(ended, 1)
            step(dve.tensor_tensor(hn[:, :, :], hn[:, :, :], spread(row["bias_gat"].unsqueeze(1), P, NT, D), ALU.add))
            step(dve.tensor_tensor(xn[:, :, :], xn[:, :, :], spread(row["beta2"].unsqueeze(1), P, NT, D), ALU.add))
            dve.wait_ge(agg_in, 16 * 4 * NT)
            step(dve.scalar_tensor_tensor(out=agg[:, :, :], in0=agg[:, :, :], scalar=1.0 / H, in1=hn[:, :, :], op0=ALU.mult, op1=ALU.add))

            def batch_norm(n, gamma, beta):
                col = [bnv[:, k, :] for k in range(6)]

                def over_nodes(rows, use):
                    step(dve.tensor_reduce(col[0], rows.rearrange("p i c -> p c i"), AX.X, ALU.add))
                    dve.sem_inc(to_spread, 1)
                    dve.wait_ge(spread_up, 3 + use + 1)
                over_nodes(agg[:, :, :], 2 * n)
                step(dve.tensor_scalar(col[1], bank(0)[:, 0:D], 1.0 / N, None, ALU.mult))
                step(dve.tensor_tensor(agg[:, :, :], agg[:, :, :], spread(col[1].unsqueeze(1), P, NT, D), ALU.subtract))
                step(dve.tensor_tensor(cg, agg[:, :, :], agg[:, :, :], ALU.mult))
                over_nodes(cg, 2 * n + 1)
                step(dve.tensor_scalar(col[2], bank(0)[:, 0:D], 1.0 / N, EPS, ALU.mult, ALU.add))
                dve.sem_inc(root_in, 1)
                dve.wait_ge(root_out, 5 + n)
                step(dve.reciprocal(col[4], col[3]))
                step(dve.tensor_tensor(col[4], col[4], row[gamma], ALU.mult))
                step(dve.tensor_tensor(agg[:, :, :], agg[:, :, :], spread(col[4].unsqueeze(1), P, NT, D), ALU.mult))
                if beta:
                    step(dve.tensor_tensor(agg[:, :, :], agg[:, :, :], spread(row[beta].unsqueeze(1), P, NT, D), ALU.add))
            batch_norm(0, "gamma1", "beta1")
            beats3n = Beats(dve, node_vec[6], 1)

            def nodes3b(b):
                beats3n.group(b)
                dve.wait_ge(mixed, 30 + b + 1)
                beats3n.done(dve.tensor_tensor(red3, bank(4)[:, 0:NB * D].rearrange("p (j c) -> p j c", c=D),
                                               spread(row["b_f2"].unsqueeze(1), P, NB, D), ALU.add))
                dve.tensor_tensor(agg[:, bass.ds(b * NB, NB), :], agg[:, bass.ds(b * NB, NB), :], red3, ALU.add).then_inc(taken, 1)
            node_phase(6, agg, nodes3b)
            dve.wait_ge(taken, 7 * NBATCH)
            batch_norm(1, "gamma2", None)
            tally.done(dve.tensor_tensor(xn[:, :, :], xn[:, :, :], agg[:, :, :], ALU.add), result_set)


_INS = ["x", "src", "dst", "edge_type_8", "edge_weight", "edge_weight_n2", "L0_gnn_W", "L0_gnn_b", "L0_gnn_deg_coeff",
        "L0_gnn_coeff_param", "L0_gnn_scale_param", "L1_gnn_W_self", "L1_gnn_b_self", "L1_gnn_W", "L1_gnn_att_src",
        "L1_gnn_att_dst", "L1_gnn_bias", "L2_gnn_We1", "L2_gnn_be1", "L2_gnn_We2", "L2_gnn_be2", "L2_gnn_Wn1", "L2_gnn_bn1",
        "L2_gnn_Wn2", "L2_gnn_bn2", "L3_gnn_W_l", "L3_gnn_b_l", "L3_gnn_W_r", "L3_gnn_b_r", "L3_gnn_att", "L3_gnn_bias_gat",
        "L3_gnn_gamma1", "L3_gnn_beta1", "L3_gnn_W1", "L3_gnn_b1", "L3_gnn_W2", "L3_gnn_b2", "L3_gnn_gamma2", "L3_gnn_beta2"]


def kernel(**inputs):
    import numpy as np
    import concourse.bacc as bacc
    from concourse.bass_utils import run_bass_kernel_spmd

    nc = bacc.Bacc("TRN2", target_bir_lowering=False, num_devices=1)
    arrays, args = {}, []
    for name in _INS:
        array = np.ascontiguousarray(inputs[name])
        arrays[f"in_{name}_dram"] = array
        args.append(nc.dram_tensor(f"in_{name}_dram", array.shape, mybir.dt.from_np(array.dtype), kind="ExternalInput").ap())
    args.append(nc.dram_tensor("out_0_dram", (N, D), F32, kind="ExternalOutput").ap())
    gnn_program(nc, *args)
    result = run_bass_kernel_spmd(nc, [arrays], core_ids=[0])
    return result.results[0]["out_0_dram"]
```
